# Optimizing a Trainium2 kernel written in Bass

```python
import numpy as np
import jax
import jax.numpy as jnp

def _softmax(x, axis=-1):
    return jax.nn.softmax(x, axis=axis)

def _gelu(x):
    return jax.nn.gelu(x, approximate=True)

def _silu(x):
    return jax.nn.silu(x)

def _sigmoid(x):
    return jax.nn.sigmoid(x)

def _layernorm(x, axis=-1, eps=1e-05):
    m = jnp.mean(x, axis=axis, keepdims=True)
    v = jnp.var(x, axis=axis, keepdims=True)
    return (x - m) / jnp.sqrt(v + eps)

def _scatter_add(tgt, idx, src, axis=0):
    return tgt.at[idx].add(src)

def _segment_sum(src, seg, n):
    return jax.ops.segment_sum(src, seg, n)
kernel_name = 'mk_perceiver_d2_seqx_r8_306f47'

def setup_inputs(seed: int=0):
    np.random.seed(seed)
    _w = jnp.asarray

    def _rec_inputs():
        import jax
        import jax.numpy as jnp
        _rk = jax.random.key(seed)
        x = -0.0002928 + 1 * jax.random.normal(jax.random.fold_in(_rk, 1), (32, 64, 128), jnp.float32)
        _lenS = 64 - jax.random.randint(jax.random.fold_in(_rk, 7), (32,), 0, max(1, 64 // 4) + 1, jnp.int32)
        _lenS2 = 128 - jax.random.randint(jax.random.fold_in(_rk, 8), (32,), 0, max(1, 128 // 4) + 1, jnp.int32)
        _ctx_1024P = jax.random.normal(jax.random.fold_in(_rk, 11), (32, 16, 128), jnp.float32)
        _ctx_1024c = jax.random.dirichlet(jax.random.fold_in(_rk, 511), 0.3 * jnp.ones((16,), jnp.float32), (32, 128))
        _ctx_1024t = jnp.einsum('bsk,bkd->bsd', _ctx_1024c, _ctx_1024P)
        _ctx_1024t = _ctx_1024t * jax.lax.rsqrt(jnp.mean(jnp.square(_ctx_1024t)) + 1e-12) * 0.953939
        ctx_1024 = -1.39393e-06 + 0.999914 * (_ctx_1024t + 0.3 * jax.random.normal(jax.random.fold_in(_rk, 611), (32, 128, 128), jnp.float32))
        _validS = jnp.arange(64)[None, :] < _lenS[:, None]
        _validS2 = jnp.arange(128)[None, :] < _lenS2[:, None]
        _causal = jnp.tril(jnp.ones((64, 64), dtype=bool))
        mask_Bx1x1xS2_ff0 = jnp.where(jnp.ones((32, 1, 1, 128), dtype=bool), 0.0, -1000000000.0).astype(jnp.float32)
        return (x, ctx_1024, mask_Bx1x1xS2_ff0)
    x, ctx_1024, mask_Bx1x1xS2_ff0 = _rec_inputs()

    def _L0_xattn_setup():
        import jax, jax.numpy as jnp
        from jax import lax
        import numpy as np
        B, SQ, SK, H, NH, KS = (2, 256, 256, 128, 16, 3)
        D = H // NH

        def _conv1d_same(x, W, b):
            y = lax.conv_general_dilated(x, W, window_strides=(1,), padding='SAME', dimension_numbers=('NWC', 'WIO', 'NWC'))
            return y + b

        def _split_heads(x):
            b, s, _ = x.shape
            return x.reshape(b, s, NH, D).transpose(0, 2, 1, 3)
        key = jax.random.key(seed)
        ks = jax.random.split(key, 10)
        s = 0.02
        return {'query_input': jax.random.normal(ks[0], (B, SQ, H), jnp.float32), 'source_input': jax.random.normal(ks[1], (B, SK, H), jnp.float32), 'mask': jnp.zeros((B, 1, 1, SK), jnp.float32), 'Wq': jax.random.normal(ks[2], (KS, H, H), jnp.float32) * s, 'bq': jnp.zeros((H,), jnp.float32), 'Wk': jax.random.normal(ks[3], (KS, H, H), jnp.float32) * s, 'bk': jnp.zeros((H,), jnp.float32), 'Wv': jax.random.normal(ks[4], (KS, H, H), jnp.float32) * s, 'bv': jnp.zeros((H,), jnp.float32), 'Wo': jax.random.normal(ks[5], (H, H), jnp.float32) * s, 'bo': jnp.zeros((H,), jnp.float32)}
    _L0_xattn_all = _L0_xattn_setup()
    _L0_xattn_in = {k: v for k, v in _L0_xattn_all.items() if k in ('Wq', 'bq', 'Wk', 'bk', 'Wv', 'bv', 'Wo', 'bo')}
    del _L0_xattn_all

    def _L0_attn_setup():
        import jax, jax.numpy as jnp
        import numpy as np
        DT_MIN, DT_MAX, STAB_EPS, RMS_EPS = (0.0001, 10.0, 1e-08, 1e-06)

        def soft_clamp(x, mn=DT_MIN, mx=DT_MAX):
            center = (mx + mn) / 2.0
            half = (mx - mn) / 2.0
            return center + half * jnp.tanh((x - center) / half)
        key = jax.random.key(seed)
        ks = jax.random.split(key, 8)
        B, L, D, N = (1, 512, 128, 16)
        s = D ** (-0.5)
        x = jax.random.normal(ks[0], (B, L, D), jnp.float32)
        A_log = jnp.broadcast_to(jnp.log(jnp.arange(1, N + 1, dtype=jnp.float32)), (D, N))
        W_delta = jax.random.normal(ks[1], (D, D), jnp.float32) * s
        b_delta = jax.random.normal(ks[2], (D,), jnp.float32) * 0.1
        W_B = jax.random.normal(ks[3], (D, N), jnp.float32) * s
        W_C = jax.random.normal(ks[4], (D, N), jnp.float32) * s
        D_skip = jax.random.normal(ks[5], (D,), jnp.float32) * 0.1 + 1.0
        norm_weight = jnp.ones((D,), jnp.float32)
        return {'x': x, 'A_log': A_log, 'W_delta': W_delta, 'b_delta': b_delta, 'W_B': W_B, 'W_C': W_C, 'D_skip': D_skip, 'norm_weight': norm_weight}
    _L0_attn_all = _L0_attn_setup()
    _L0_attn_in = {k: v for k, v in _L0_attn_all.items() if k in ('A_log', 'W_delta', 'b_delta', 'W_B', 'W_C', 'D_skip', 'norm_weight')}
    del _L0_attn_all

    def _L0_ffn_setup():
        import jax, jax.numpy as jnp
        import numpy as np
        EPS_LN = 1e-05
        EPS_GATE = 1e-08

        def layer_norm(x, gamma, beta):
            mu = jnp.mean(x, axis=-1, keepdims=True)
            var = jnp.mean(jnp.square(x - mu), axis=-1, keepdims=True)
            return (x - mu) * jax.lax.rsqrt(var + EPS_LN) * gamma + beta
        key = jax.random.key(seed)
        ks = jax.random.split(key, 8)
        B, S, D, E, H = (4, 512, 128, 4, 256)
        s_in = 1.0 / np.sqrt(D)
        s_h = 1.0 / np.sqrt(H)
        return {'h': jax.random.normal(ks[0], (B, S, D), dtype=jnp.float32), 'router_w': jax.random.uniform(ks[1], (E, D), jnp.float32, -s_in, s_in), 'rn_g': jnp.ones((D,), jnp.float32), 'rn_b': jnp.zeros((D,), jnp.float32), 'w1': jax.random.uniform(ks[2], (E, D, H), jnp.float32, -s_in, s_in), 'ln_g': jnp.ones((E, H), jnp.float32), 'ln_b': jnp.zeros((E, H), jnp.float32), 'w2': jax.random.uniform(ks[3], (E, H, D), jnp.float32, -s_h, s_h), 'on_g': jnp.ones((D,), jnp.float32), 'on_b': jnp.zeros((D,), jnp.float32)}
    _L0_ffn_all = _L0_ffn_setup()
    _L0_ffn_in = {k: v for k, v in _L0_ffn_all.items() if k in ('router_w', 'rn_g', 'rn_b', 'w1', 'ln_g', 'ln_b', 'w2', 'on_g', 'on_b')}
    del _L0_ffn_all

    def _L1_xattn_setup():
        import jax, jax.numpy as jnp
        import numpy as np
        H = 16
        D = 128
        F = 512
        LN_EPS = 1e-05

        def _glorot(key, shape):
            fan_in, fan_out = (shape[0], shape[1])
            lim = np.sqrt(6.0 / (fan_in + fan_out))
            return jax.random.uniform(key, shape, jnp.float32, -lim, lim)

        def _split_heads(x):
            b, l, _ = x.shape
            return x.reshape(b, l, H, D // H)

        def _mha(x, ctx, mask, qw, qb, kw, kb, vw, vb):
            q = _split_heads(x @ qw + qb)
            k = _split_heads(ctx @ kw + kb)
            v = _split_heads(ctx @ vw + vb)
            scores = jnp.einsum('bqhd,bkhd->bhqk', q, k) / np.sqrt(D // H).astype(np.float32)
            if mask is not None:
                scores = scores + mask
            probs = jax.nn.softmax(scores, axis=-1)
            out = jnp.einsum('bhqk,bkhd->bqhd', probs, v)
            return out.reshape(x.shape[0], x.shape[1], D)

        def _self_output(h, residual, w, b, g, be):
            h = h @ w + b
            h = h + residual
            mu = jnp.mean(h, axis=-1, keepdims=True)
            var = jnp.mean(jnp.square(h - mu), axis=-1, keepdims=True)
            return (h - mu) * jax.lax.rsqrt(var + LN_EPS) * g + be
        key = jax.random.key(seed)
        ks = jax.random.split(key, 16)
        inp = {'input_tensor': jax.random.normal(ks[0], (4, 128, D), jnp.float32), 'ctx_tensor': jax.random.normal(ks[1], (4, 256, D), jnp.float32), 'ctx_attn_mask': jnp.zeros((4, 1, 1, 256), jnp.float32), 'cq_w': _glorot(ks[2], (D, D)), 'cq_b': jnp.zeros((D,)), 'ck_w': _glorot(ks[3], (D, D)), 'ck_b': jnp.zeros((D,)), 'cv_w': _glorot(ks[4], (D, D)), 'cv_b': jnp.zeros((D,)), 'co_w': _glorot(ks[5], (D, D)), 'co_b': jnp.zeros((D,)), 'co_g': jnp.ones((D,)), 'co_be': jnp.zeros((D,)), 'sq_w': _glorot(ks[6], (D, D)), 'sq_b': jnp.zeros((D,)), 'sk_w': _glorot(ks[7], (D, D)), 'sk_b': jnp.zeros((D,)), 'sv_w': _glorot(ks[8], (D, D)), 'sv_b': jnp.zeros((D,)), 'so_w': _glorot(ks[9], (D, D)), 'so_b': jnp.zeros((D,)), 'so_g': jnp.ones((D,)), 'so_be': jnp.zeros((D,)), 'fi_w': _glorot(ks[10], (D, F)), 'fi_b': jnp.zeros((F,)), 'fo_w': _glorot(ks[11], (F, D)), 'fo_b': jnp.zeros((D,)), 'fo_g': jnp.ones((D,)), 'fo_be': jnp.zeros((D,))}
        return inp
    _L1_xattn_all = _L1_xattn_setup()
    _L1_xattn_in = {k: v for k, v in _L1_xattn_all.items() if k in ('cq_w', 'cq_b', 'ck_w', 'ck_b', 'cv_w', 'cv_b', 'co_w', 'co_b', 'co_g', 'co_be', 'sq_w', 'sq_b', 'sk_w', 'sk_b', 'sv_w', 'sv_b', 'so_w', 'so_b', 'so_g', 'so_be', 'fi_w', 'fi_b', 'fo_w', 'fo_b', 'fo_g', 'fo_be')}
    del _L1_xattn_all

    def _L1_attn_setup():
        import jax, jax.numpy as jnp
        import numpy as np
        SLEN, BSZ, D_MODEL = (128, 8, 128)
        N_HEAD, D_HEAD = (16, 64)
        EPS_LN = 1e-05
        SCALE = 1.0 / np.sqrt(D_HEAD)

        def _fast_weight_memory(q, k, v, beta):
            bsz = q.shape[1]
            W0 = jnp.zeros((bsz, N_HEAD, D_HEAD, D_HEAD), q.dtype)

            def step(W, xs):
                qt, kt, vt, bt = xs
                v_old = jnp.einsum('bhij,bhj->bhi', W, kt)
                delta = bt * (vt - v_old)
                W = W + delta[..., :, None] * kt[..., None, :]
                out = jnp.einsum('bhij,bhj->bhi', W, qt)
                return (W, out)
            _, outs = jax.lax.scan(step, W0, (q, k, v, beta))
            return outs
        key = jax.random.key(seed)
        k1, k2, k3 = jax.random.split(key, 3)
        h = jax.random.normal(k1, (SLEN, BSZ, D_MODEL), jnp.float32)
        W_qkvb = jax.random.normal(k2, (D_MODEL, N_HEAD * (3 * D_HEAD + 1)), jnp.float32) * 0.02
        W_o = jax.random.normal(k3, (N_HEAD * D_HEAD, D_MODEL), jnp.float32) * 0.02
        ln_g = jnp.ones((D_MODEL,), jnp.float32)
        ln_b = jnp.zeros((D_MODEL,), jnp.float32)
        return {'h': h, 'W_qkvb': W_qkvb, 'W_o': W_o, 'ln_g': ln_g, 'ln_b': ln_b}
    _L1_attn_all = _L1_attn_setup()
    _L1_attn_in = {k: v for k, v in _L1_attn_all.items() if k in ('W_qkvb', 'W_o', 'ln_g', 'ln_b')}
    del _L1_attn_all

    def _L1_ffn_setup():
        import jax, jax.numpy as jnp
        import numpy as np
        S, B, D = (128, 2, 128)
        E, TOPK = (15, 3)
        F = 128
        FS = 256

        def _uinit(k, shape, out_dim):
            std = out_dim ** (-0.5)
            return jax.random.uniform(k, shape, jnp.float32, -std, std)
        key = jax.random.key(seed)
        ks = jax.random.split(key, 10)
        return {'x': jax.random.normal(ks[0], (S, B, D), jnp.float32), 'gate_w': jax.random.normal(ks[1], (E, D), jnp.float32) * D ** (-0.5), 'fc1_w': _uinit(ks[2], (E, 2 * F, D), 2 * F), 'fc1_b': _uinit(ks[3], (E, 2 * F), 2 * F), 'geglu_mult': jnp.ones((E, F), jnp.float32), 'fc2_w': _uinit(ks[4], (E, D, F), D), 'fc2_b': _uinit(ks[5], (E, D), D), 's_fc1_w': _uinit(ks[6], (2 * FS, D), 2 * FS), 's_fc1_b': _uinit(ks[7], (2 * FS,), 2 * FS), 's_geglu_mult': jnp.ones((FS,), jnp.float32), 's_fc2_w': _uinit(ks[8], (D, FS), D), 's_fc2_b': _uinit(ks[9], (D,), D)}
    _L1_ffn_all = _L1_ffn_setup()
    _L1_ffn_in = {k: v for k, v in _L1_ffn_all.items() if k in ('gate_w', 'fc1_w', 'fc1_b', 'geglu_mult', 'fc2_w', 'fc2_b', 's_fc1_w', 's_fc1_b', 's_geglu_mult', 's_fc2_w', 's_fc2_b')}
    del _L1_ffn_all
    return {'x': x, 'ctx_1024': ctx_1024, 'mask_Bx1x1xS2_ff0': mask_Bx1x1xS2_ff0, 'L0_xattn_Wq': _L0_xattn_in['Wq'], 'L0_xattn_bq': _L0_xattn_in['bq'], 'L0_xattn_Wk': _L0_xattn_in['Wk'], 'L0_xattn_bk': _L0_xattn_in['bk'], 'L0_xattn_Wv': _L0_xattn_in['Wv'], 'L0_xattn_bv': _L0_xattn_in['bv'], 'L0_xattn_Wo': _L0_xattn_in['Wo'], 'L0_xattn_bo': _L0_xattn_in['bo'], 'L0_attn_A_log': _L0_attn_in['A_log'], 'L0_attn_W_delta': _L0_attn_in['W_delta'], 'L0_attn_b_delta': _L0_attn_in['b_delta'], 'L0_attn_W_B': _L0_attn_in['W_B'], 'L0_attn_W_C': _L0_attn_in['W_C'], 'L0_attn_D_skip': _L0_attn_in['D_skip'], 'L0_attn_norm_weight': _L0_attn_in['norm_weight'], 'L0_ffn_router_w': _L0_ffn_in['router_w'], 'L0_ffn_rn_g': _L0_ffn_in['rn_g'], 'L0_ffn_rn_b': _L0_ffn_in['rn_b'], 'L0_ffn_w1': _L0_ffn_in['w1'], 'L0_ffn_ln_g': _L0_ffn_in['ln_g'], 'L0_ffn_ln_b': _L0_ffn_in['ln_b'], 'L0_ffn_w2': _L0_ffn_in['w2'], 'L0_ffn_on_g': _L0_ffn_in['on_g'], 'L0_ffn_on_b': _L0_ffn_in['on_b'], 'L1_xattn_cq_w': _L1_xattn_in['cq_w'], 'L1_xattn_cq_b': _L1_xattn_in['cq_b'], 'L1_xattn_ck_w': _L1_xattn_in['ck_w'], 'L1_xattn_ck_b': _L1_xattn_in['ck_b'], 'L1_xattn_cv_w': _L1_xattn_in['cv_w'], 'L1_xattn_cv_b': _L1_xattn_in['cv_b'], 'L1_xattn_co_w': _L1_xattn_in['co_w'], 'L1_xattn_co_b': _L1_xattn_in['co_b'], 'L1_xattn_co_g': _L1_xattn_in['co_g'], 'L1_xattn_co_be': _L1_xattn_in['co_be'], 'L1_xattn_sq_w': _L1_xattn_in['sq_w'], 'L1_xattn_sq_b': _L1_xattn_in['sq_b'], 'L1_xattn_sk_w': _L1_xattn_in['sk_w'], 'L1_xattn_sk_b': _L1_xattn_in['sk_b'], 'L1_xattn_sv_w': _L1_xattn_in['sv_w'], 'L1_xattn_sv_b': _L1_xattn_in['sv_b'], 'L1_xattn_so_w': _L1_xattn_in['so_w'], 'L1_xattn_so_b': _L1_xattn_in['so_b'], 'L1_xattn_so_g': _L1_xattn_in['so_g'], 'L1_xattn_so_be': _L1_xattn_in['so_be'], 'L1_xattn_fi_w': _L1_xattn_in['fi_w'], 'L1_xattn_fi_b': _L1_xattn_in['fi_b'], 'L1_xattn_fo_w': _L1_xattn_in['fo_w'], 'L1_xattn_fo_b': _L1_xattn_in['fo_b'], 'L1_xattn_fo_g': _L1_xattn_in['fo_g'], 'L1_xattn_fo_be': _L1_xattn_in['fo_be'], 'L1_attn_W_qkvb': _L1_attn_in['W_qkvb'], 'L1_attn_W_o': _L1_attn_in['W_o'], 'L1_attn_ln_g': _L1_attn_in['ln_g'], 'L1_attn_ln_b': _L1_attn_in['ln_b'], 'L1_ffn_gate_w': _L1_ffn_in['gate_w'], 'L1_ffn_fc1_w': _L1_ffn_in['fc1_w'], 'L1_ffn_fc1_b': _L1_ffn_in['fc1_b'], 'L1_ffn_geglu_mult': _L1_ffn_in['geglu_mult'], 'L1_ffn_fc2_w': _L1_ffn_in['fc2_w'], 'L1_ffn_fc2_b': _L1_ffn_in['fc2_b'], 'L1_ffn_s_fc1_w': _L1_ffn_in['s_fc1_w'], 'L1_ffn_s_fc1_b': _L1_ffn_in['s_fc1_b'], 'L1_ffn_s_geglu_mult': _L1_ffn_in['s_geglu_mult'], 'L1_ffn_s_fc2_w': _L1_ffn_in['s_fc2_w'], 'L1_ffn_s_fc2_b': _L1_ffn_in['s_fc2_b']}

def reference(x, ctx_1024, mask_Bx1x1xS2_ff0, L0_xattn_Wq, L0_xattn_bq, L0_xattn_Wk, L0_xattn_bk, L0_xattn_Wv, L0_xattn_bv, L0_xattn_Wo, L0_xattn_bo, L0_attn_A_log, L0_attn_W_delta, L0_attn_b_delta, L0_attn_W_B, L0_attn_W_C, L0_attn_D_skip, L0_attn_norm_weight, L0_ffn_router_w, L0_ffn_rn_g, L0_ffn_rn_b, L0_ffn_w1, L0_ffn_ln_g, L0_ffn_ln_b, L0_ffn_w2, L0_ffn_on_g, L0_ffn_on_b, L1_xattn_cq_w, L1_xattn_cq_b, L1_xattn_ck_w, L1_xattn_ck_b, L1_xattn_cv_w, L1_xattn_cv_b, L1_xattn_co_w, L1_xattn_co_b, L1_xattn_co_g, L1_xattn_co_be, L1_xattn_sq_w, L1_xattn_sq_b, L1_xattn_sk_w, L1_xattn_sk_b, L1_xattn_sv_w, L1_xattn_sv_b, L1_xattn_so_w, L1_xattn_so_b, L1_xattn_so_g, L1_xattn_so_be, L1_xattn_fi_w, L1_xattn_fi_b, L1_xattn_fo_w, L1_xattn_fo_b, L1_xattn_fo_g, L1_xattn_fo_be, L1_attn_W_qkvb, L1_attn_W_o, L1_attn_ln_g, L1_attn_ln_b, L1_ffn_gate_w, L1_ffn_fc1_w, L1_ffn_fc1_b, L1_ffn_geglu_mult, L1_ffn_fc2_w, L1_ffn_fc2_b, L1_ffn_s_fc1_w, L1_ffn_s_fc1_b, L1_ffn_s_geglu_mult, L1_ffn_s_fc2_w, L1_ffn_s_fc2_b):
    import jax
    import jax.numpy as jnp

    def _L0_xattn_ref(query_input, source_input, mask, Wq, bq, Wk, bk, Wv, bv, Wo, bo):
        import jax, jax.numpy as jnp
        from jax import lax
        import numpy as np
        B, SQ, SK, H, NH, KS = (2, 256, 256, 128, 16, 3)
        D = H // NH

        def _conv1d_same(x, W, b):
            y = lax.conv_general_dilated(x, W, window_strides=(1,), padding='SAME', dimension_numbers=('NWC', 'WIO', 'NWC'))
            return y + b

        def _split_heads(x):
            b, s, _ = x.shape
            return x.reshape(b, s, NH, D).transpose(0, 2, 1, 3)
        q = _split_heads(_conv1d_same(query_input, Wq, bq)) * D ** (-0.5)
        k = _split_heads(_conv1d_same(source_input, Wk, bk))
        v = _split_heads(_conv1d_same(source_input, Wv, bv))
        logits = jnp.einsum('bhqd,bhkd->bhqk', q, k) + mask * -1000000000.0
        weights = jax.nn.softmax(logits, axis=-1)
        attn = jnp.einsum('bhqk,bhkd->bhqd', weights, v)
        attn = attn.transpose(0, 2, 1, 3).reshape(q.shape[0], -1, H)
        return attn @ Wo + bo

    def _L0_attn_ref(x, A_log, W_delta, b_delta, W_B, W_C, D_skip, norm_weight):
        import jax, jax.numpy as jnp
        import numpy as np
        DT_MIN, DT_MAX, STAB_EPS, RMS_EPS = (0.0001, 10.0, 1e-08, 1e-06)

        def soft_clamp(x, mn=DT_MIN, mx=DT_MAX):
            center = (mx + mn) / 2.0
            half = (mx - mn) / 2.0
            return center + half * jnp.tanh((x - center) / half)
        rms = jnp.sqrt(jnp.mean(x * x, axis=-1, keepdims=True) + RMS_EPS)
        xn = norm_weight * x / rms
        delta = soft_clamp(jax.nn.softplus(xn @ W_delta + b_delta))
        Bp = xn @ W_B
        C = xn @ W_C
        A = -jnp.exp(A_log)
        half_dA = 0.5 * delta[..., None] * A
        denom_inv = 1.0 / jnp.maximum(1.0 - half_dA, STAB_EPS)
        A_bar = (1.0 + half_dA) * denom_inv
        B_bar = jnp.sqrt(delta)[..., None] * Bp[:, :, None, :] * denom_inv
        Bx = B_bar * xn[..., None]

        def step(h, inp):
            a_t, bx_t, c_t = inp
            h = a_t * h + bx_t
            y_t = jnp.einsum('bdn,bn->bd', h, c_t)
            return (h, y_t)
        h0 = jnp.zeros((x.shape[0], A.shape[0], A.shape[1]), x.dtype)
        seq = (jnp.moveaxis(A_bar, 1, 0), jnp.moveaxis(Bx, 1, 0), jnp.moveaxis(C, 1, 0))
        _, ys = jax.lax.scan(step, h0, seq)
        y = jnp.moveaxis(ys, 0, 1) + D_skip * xn
        return y

    def _L0_ffn_ref(h, router_w, rn_g, rn_b, w1, ln_g, ln_b, w2, on_g, on_b):
        import jax, jax.numpy as jnp
        import numpy as np
        EPS_LN = 1e-05
        EPS_GATE = 1e-08

        def layer_norm(x, gamma, beta):
            mu = jnp.mean(x, axis=-1, keepdims=True)
            var = jnp.mean(jnp.square(x - mu), axis=-1, keepdims=True)
            return (x - mu) * jax.lax.rsqrt(var + EPS_LN) * gamma + beta
        D = h.shape[-1]
        h_norm = layer_norm(h, rn_g, rn_b)
        g = jax.nn.softmax(jnp.einsum('bsd,ed->bse', h_norm, router_w), axis=-1)
        top2_w, top2_idx = jax.lax.top_k(g, 2)
        top2_w = top2_w / (jnp.sum(top2_w, axis=-1, keepdims=True) + EPS_GATE)
        hid = jnp.einsum('bsd,edh->bseh', h, w1)
        hid = jax.nn.relu(layer_norm(hid, ln_g, ln_b))
        expert_out = jnp.einsum('bseh,ehd->bsed', hid, w2)
        idx = jnp.broadcast_to(top2_idx[..., None], top2_idx.shape + (D,))
        top2_out = jnp.take_along_axis(expert_out, idx, axis=-2)
        out = jnp.sum(top2_out * top2_w[..., None], axis=-2)
        return layer_norm(out, on_g, on_b)

    def _L1_xattn_ref(input_tensor, ctx_tensor, ctx_attn_mask, cq_w, cq_b, ck_w, ck_b, cv_w, cv_b, co_w, co_b, co_g, co_be, sq_w, sq_b, sk_w, sk_b, sv_w, sv_b, so_w, so_b, so_g, so_be, fi_w, fi_b, fo_w, fo_b, fo_g, fo_be):
        import jax, jax.numpy as jnp
        import numpy as np
        H = 16
        D = 128
        F = 512
        LN_EPS = 1e-05

        def _glorot(key, shape):
            fan_in, fan_out = (shape[0], shape[1])
            lim = np.sqrt(6.0 / (fan_in + fan_out))
            return jax.random.uniform(key, shape, jnp.float32, -lim, lim)

        def _split_heads(x):
            b, l, _ = x.shape
            return x.reshape(b, l, H, D // H)

        def _mha(x, ctx, mask, qw, qb, kw, kb, vw, vb):
            q = _split_heads(x @ qw + qb)
            k = _split_heads(ctx @ kw + kb)
            v = _split_heads(ctx @ vw + vb)
            scores = jnp.einsum('bqhd,bkhd->bhqk', q, k) / np.sqrt(D // H).astype(np.float32)
            if mask is not None:
                scores = scores + mask
            probs = jax.nn.softmax(scores, axis=-1)
            out = jnp.einsum('bhqk,bkhd->bqhd', probs, v)
            return out.reshape(x.shape[0], x.shape[1], D)

        def _self_output(h, residual, w, b, g, be):
            h = h @ w + b
            h = h + residual
            mu = jnp.mean(h, axis=-1, keepdims=True)
            var = jnp.mean(jnp.square(h - mu), axis=-1, keepdims=True)
            return (h - mu) * jax.lax.rsqrt(var + LN_EPS) * g + be
        ca = _mha(input_tensor, ctx_tensor, ctx_attn_mask, cq_w, cq_b, ck_w, ck_b, cv_w, cv_b)
        x = _self_output(ca, input_tensor, co_w, co_b, co_g, co_be)
        sa = _mha(x, x, None, sq_w, sq_b, sk_w, sk_b, sv_w, sv_b)
        x = _self_output(sa, x, so_w, so_b, so_g, so_be)
        inter = jax.nn.gelu(x @ fi_w + fi_b, approximate=False)
        x = _self_output(inter, x, fo_w, fo_b, fo_g, fo_be)
        return x

    def _L1_attn_ref(h, W_qkvb, W_o, ln_g, ln_b):
        import jax, jax.numpy as jnp
        import numpy as np
        SLEN, BSZ, D_MODEL = (128, 8, 128)
        N_HEAD, D_HEAD = (16, 64)
        EPS_LN = 1e-05
        SCALE = 1.0 / np.sqrt(D_HEAD)

        def _fast_weight_memory(q, k, v, beta):
            bsz = q.shape[1]
            W0 = jnp.zeros((bsz, N_HEAD, D_HEAD, D_HEAD), q.dtype)

            def step(W, xs):
                qt, kt, vt, bt = xs
                v_old = jnp.einsum('bhij,bhj->bhi', W, kt)
                delta = bt * (vt - v_old)
                W = W + delta[..., :, None] * kt[..., None, :]
                out = jnp.einsum('bhij,bhj->bhi', W, qt)
                return (W, out)
            _, outs = jax.lax.scan(step, W0, (q, k, v, beta))
            return outs
        slen, bsz, _ = h.shape
        qkvb = (h @ W_qkvb).reshape(slen, bsz, N_HEAD, 3 * D_HEAD + 1)
        q = qkvb[..., :D_HEAD]
        k = qkvb[..., D_HEAD:2 * D_HEAD]
        v = qkvb[..., 2 * D_HEAD:3 * D_HEAD]
        beta = jax.nn.sigmoid(qkvb[..., 3 * D_HEAD:])
        q = jax.nn.elu(q) + 1.0
        k = jax.nn.elu(k) + 1.0
        q = q / q.sum(-1, keepdims=True)
        k = k / k.sum(-1, keepdims=True)
        outs = _fast_weight_memory(q, k, v, beta)
        layer_out = (SCALE * outs).reshape(slen, bsz, N_HEAD * D_HEAD)
        attn_out = layer_out @ W_o
        x = h + attn_out
        mu = x.mean(-1, keepdims=True)
        var = jnp.mean((x - mu) ** 2, axis=-1, keepdims=True)
        return (x - mu) / jnp.sqrt(var + EPS_LN) * ln_g + ln_b

    def _L1_ffn_ref(x, gate_w, fc1_w, fc1_b, geglu_mult, fc2_w, fc2_b, s_fc1_w, s_fc1_b, s_geglu_mult, s_fc2_w, s_fc2_b):
        import jax, jax.numpy as jnp
        import numpy as np
        S, B, D = (128, 2, 128)
        E, TOPK = (15, 3)
        F = 128
        FS = 256

        def _uinit(k, shape, out_dim):
            std = out_dim ** (-0.5)
            return jax.random.uniform(k, shape, jnp.float32, -std, std)
        s, b, d = x.shape
        xt = x.reshape(-1, d)
        T = xt.shape[0]
        logits = xt @ gate_w.T
        scores = jax.nn.softmax(logits, axis=-1)
        topk_w, topk_idx = jax.lax.top_k(scores, TOPK)
        topk_w = topk_w / (jnp.sum(topk_w, axis=-1, keepdims=True) + 1e-20)
        comb = jnp.zeros((T, E), xt.dtype).at[jnp.arange(T)[:, None], topk_idx].add(topk_w)
        h = jnp.einsum('td,efd->etf', xt, fc1_w) + fc1_b[:, None, :]
        xh, g = (h[..., :F], h[..., F:])
        a = jax.nn.gelu(g, approximate=False) * xh * geglu_mult[:, None, :]
        yexp = jnp.einsum('etf,edf->etd', a, fc2_w) + fc2_b[:, None, :]
        y = jnp.einsum('etd,te->td', yexp, comb)
        hs = xt @ s_fc1_w.T + s_fc1_b
        xs, gs = (hs[..., :FS], hs[..., FS:])
        as_ = jax.nn.gelu(gs, approximate=False) * xs * s_geglu_mult
        ys = as_ @ s_fc2_w.T + s_fc2_b
        return (y + ys).reshape(s, b, d)
    x = x + _L0_xattn_ref(_layernorm(x, axis=-1), ctx_1024, mask_Bx1x1xS2_ff0, L0_xattn_Wq, L0_xattn_bq, L0_xattn_Wk, L0_xattn_bk, L0_xattn_Wv, L0_xattn_bv, L0_xattn_Wo, L0_xattn_bo)
    x = x + _L0_attn_ref(_layernorm(x, axis=-1), L0_attn_A_log, L0_attn_W_delta, L0_attn_b_delta, L0_attn_W_B, L0_attn_W_C, L0_attn_D_skip, L0_attn_norm_weight)
    x = x + _L0_ffn_ref(_layernorm(x, axis=-1), L0_ffn_router_w, L0_ffn_rn_g, L0_ffn_rn_b, L0_ffn_w1, L0_ffn_ln_g, L0_ffn_ln_b, L0_ffn_w2, L0_ffn_on_g, L0_ffn_on_b)
    x = x + _L1_xattn_ref(_layernorm(x, axis=-1), ctx_1024, mask_Bx1x1xS2_ff0, L1_xattn_cq_w, L1_xattn_cq_b, L1_xattn_ck_w, L1_xattn_ck_b, L1_xattn_cv_w, L1_xattn_cv_b, L1_xattn_co_w, L1_xattn_co_b, L1_xattn_co_g, L1_xattn_co_be, L1_xattn_sq_w, L1_xattn_sq_b, L1_xattn_sk_w, L1_xattn_sk_b, L1_xattn_sv_w, L1_xattn_sv_b, L1_xattn_so_w, L1_xattn_so_b, L1_xattn_so_g, L1_xattn_so_be, L1_xattn_fi_w, L1_xattn_fi_b, L1_xattn_fo_w, L1_xattn_fo_b, L1_xattn_fo_g, L1_xattn_fo_be)
    x = x + _L1_attn_ref(_layernorm(x, axis=-1), L1_attn_W_qkvb, L1_attn_W_o, L1_attn_ln_g, L1_attn_ln_b)
    x = x + _L1_ffn_ref(_layernorm(x, axis=-1), L1_ffn_gate_w, L1_ffn_fc1_w, L1_ffn_fc1_b, L1_ffn_geglu_mult, L1_ffn_fc2_w, L1_ffn_fc2_b, L1_ffn_s_fc1_w, L1_ffn_s_fc1_b, L1_ffn_s_geglu_mult, L1_ffn_s_fc2_w, L1_ffn_s_fc2_b)
    return x

_drawn_inputs = setup_inputs


def setup_inputs(seed=0):
    import zlib

    import numpy as np

    out = dict(_drawn_inputs(seed))
    spreads = {'L0_xattn_bq': (0.0, 0.8),
     'L0_xattn_bk': (0.0, 2.0),
     'L0_xattn_bv': (0.0, 0.1),
     'L0_xattn_bo': (0.0, 0.1),
     'L0_attn_norm_weight': (1.0, 0.2),
     'L0_ffn_rn_g': (1.0, 0.2),
     'L0_ffn_rn_b': (0.0, 0.1),
     'L0_ffn_ln_g': (1.0, 0.2),
     'L0_ffn_ln_b': (0.0, 0.1),
     'L0_ffn_on_g': (1.0, 0.2),
     'L0_ffn_on_b': (0.0, 0.1),
     'L1_xattn_cq_b': (0.0, 0.8),
     'L1_xattn_ck_b': (0.0, 2.0),
     'L1_xattn_cv_b': (0.0, 0.1),
     'L1_xattn_co_b': (0.0, 0.268),
     'L1_xattn_co_g': (1.0, 0.2),
     'L1_xattn_co_be': (0.0, 0.1),
     'L1_xattn_sq_b': (0.0, 0.8),
     'L1_xattn_sk_b': (0.0, 2.0),
     'L1_xattn_sv_b': (0.0, 0.293),
     'L1_xattn_so_b': (0.0, 0.279),
     'L1_xattn_so_g': (1.0, 0.2),
     'L1_xattn_so_be': (0.0, 0.267),
     'L1_xattn_fi_b': (0.0, 0.36),
     'L1_xattn_fo_b': (0.0, 0.317),
     'L1_xattn_fo_g': (1.0, 0.2),
     'L1_xattn_fo_be': (0.0, 0.1),
     'L1_attn_ln_g': (1.0, 0.2),
     'L1_attn_ln_b': (0.0, 0.357),
     'L1_ffn_geglu_mult': (1.0, 0.6),
     'L1_ffn_s_geglu_mult': (1.0, 0.6)}
    factors = {'L0_xattn_Wq': 4.566,
     'L0_xattn_Wk': 5.3,
     'L0_attn_b_delta': 3.403,
     'L1_attn_W_qkvb': 8.0,
     'L1_attn_W_o': 8.0,
     'L1_ffn_gate_w': 5.565,
     'L1_ffn_fc1_w': 6.832,
     'L1_ffn_fc1_b': 8.0,
     'L1_ffn_fc2_w': 6.822,
     'L1_ffn_fc2_b': 40.676,
     'L1_ffn_s_fc1_w': 6.214,
     'L1_ffn_s_fc1_b': 8.0,
     'L1_ffn_s_fc2_w': 6.229,
     'L1_ffn_s_fc2_b': 32.388}
    for name, (base, spread) in spreads.items():
        noise = np.random.default_rng([zlib.crc32(name.encode()), seed]).standard_normal(out[name].shape)
        drawn = base * np.exp(spread * noise) if base else spread * noise
        out[name] = jnp.asarray(drawn.astype(out[name].dtype))
    for name, factor in factors.items():
        out[name] = (out[name] * factor).astype(out[name].dtype)
    return out
```

```python
from contextlib import ExitStack

import concourse.bass as bass
import numpy as np
from concourse import mybir

ALU = mybir.AluOpType
ACT = mybir.ActivationFunctionType
AX = mybir.AxisListType
F32 = mybir.dt.float32
BF16 = mybir.dt.bfloat16

P = 128
B, S, SC = 32, 64, 128
NT = B * S // P
NH, DH = 16, 8
NPAIR = NH // 2
KS = 3
NSTATE = 16
E0, H0 = 4, 256
FF = 512
NHM, DM = 16, 64
E1, F1, FS = 15, 128, 256
NE = E1 + FS // F1
EPS = 1e-5
DT_MIN, DT_MAX, RMS_EPS = 0.0001, 10.0, 1e-6

PACKS = {
    "cst": [("ident", P), ("sel64", S), ("headmask", 8), ("bd_strict", P), ("bd_upper", P), ("lvl0", 32), ("lvl1", 32),
            ("lvl2", 32), ("lvl3", 32), ("eye32", 32), ("rowlow", 1), ("rowhigh", 1), ("ind2", 2), ("pick3", 32)],
    "col": [("a_bq", 1), ("a_bk", 1), ("b_delta", 1), ("d_skip", 1), ("norm_w", 1), ("rn_g", 1), ("rn_b", 1),
            ("lng", 8), ("lnb", 8), ("cq_b", 1), ("ck_b", 1), ("sq_b", 1), ("sk_b", 1), ("fi_b", 4)],
    "w_a": [("wq", KS * P), ("wk", KS * P), ("wv", KS * P), ("wo", P)],
    "w_b": [("wdelta", P), ("wbc", 2 * NSTATE), ("alog", NSTATE)],
    "w_c": [("router", E0), ("w1", E0 * H0), ("w2", E0 * H0)],
    "w_d": [("cq", P), ("ck", P), ("cv", P), ("co", P), ("sq", P), ("sk", P), ("sv", P), ("so", P), ("fi", FF), ("fo", FF)],
    "w_e": [("mq", NHM * DM), ("mk", NHM * DM), ("mv", NHM * DM), ("mbeta", NHM), ("mo", NHM * DM)],
    "w_f": [("gate", E1)],
}
ROWS = ["a_bv", "a_bo", "on_g", "on_b", "cv_b", "co_b", "co_g", "co_be", "sv_b", "so_b", "so_g", "so_be",
        "fo_b", "fo_g", "fo_be", "m_g", "m_b"]
EXW = [("fc1", 2 * F1), ("fc2", P), ("b1", 2), ("mult", 1)]


class Shared:
    pass


def width(fields):
    return sum(w for _, w in fields)


def fields_of(ap, fields):
    out, at = {}, 0
    for name, w in fields:
        out[name] = ap[:, at:at + w]
        at += w
    return out


class Order:

    def __init__(self, eng, sem, per, i=0):
        self.eng, self.sem, self.per, self.base, self.n = eng, sem, per, i * per, 0

    def __call__(self, ins):
        ins.then_inc(self.sem, 1)
        self.n += 1
        self.eng.wait_ge(self.sem, self.base + self.n)

    def end(self):
        assert self.n == self.per, (self.n, self.per)


def settle(dve, k):
    dve.memset(k.unused[:, :], 0.0)


def tile(i, w=P):
    return bass.ds(i * w, w)


def pipeline(eng, n, body):
    with eng.Fori(0, n - 1) as i:
        body(i, False)
    body(n - 1, True)


def row_stats(dve, order, k, src):
    for t in range(NT):
        ins = dve.bn_stats(k.st[:, 6 * t:6 * t + 6], src[:, t * P:(t + 1) * P])
    order(ins)
    for t in range(NT):
        ins = dve.bn_aggr(k.mv[:, 2 * t:2 * t + 2], k.st[:, 6 * t:6 * t + 6])
    order(ins)


def aggregate(dve, order, k):
    for t in range(NT):
        ins = dve.bn_aggr(k.mv[:, 2 * t:2 * t + 2], k.st[:, 6 * t:6 * t + 6])
    order(ins)


def variances(k):
    return k.mv[:, :].rearrange("p (t two) -> p t two", two=2)[:, :, 1]


def load_constants(nc, k):
    with nc.Block() as block:
        @block.sync
        def _(sp):
            for name in ("cst", "col", "w_a"):
                sp.dma_start(k.pack[name][:, :], k.dram[name]).then_inc(k.early_loaded, 16)
            sp.dma_start(k.xs[:, :].rearrange("p (t d) -> p t d", d=P),
                         k.dram["x"].rearrange("(t b) s d -> (b s) t d", b=2)).then_inc(k.early_loaded, 16)
            sp.dma_start(k.rows[:, :], k.dram["rows"].partition_broadcast(P)).then_inc(k.early_loaded, 16)
            sp.dma_start(k.mask[:, :], k.dram["mask"]).then_inc(k.early_loaded, 16)
            for name in ("w_b", "w_c", "w_d", "w_e", "w_f"):
                sp.dma_start(k.pack[name][:, :], k.dram[name]).then_inc(k.late_loaded, 16)

        @block.gpsimd
        def _(pool):
            pool.memset(k.ones[:, :], 1.0).then_inc(k.const_made, 1)
            pool.memset(k.ones3[:, :], 1.0).then_inc(k.const_made, 1)
            pool.memset(k.eps[:, :], EPS).then_inc(k.const_made, 1)

        @block.vector
        def _(dve):
            dve.wait_ge(k.early_loaded, 16 * 6)
            order = Order(dve, k.const_ordered, 17)
            for scale, parts in ((-1e9, k.split_a), (1.0, k.split_d)):
                order(dve.tensor_scalar(k.mtmp[:, 0, :], k.mask[:, :], scale, None, ALU.mult))
                order(dve.tensor_copy(parts[:, 0, :], k.mtmp[:, 0, :]))
                order(dve.tensor_tensor(k.mtmp[:, 1, :], k.mtmp[:, 0, :], parts[:, 0, :], ALU.subtract))
                order(dve.tensor_copy(parts[:, 1, :], k.mtmp[:, 1, :]))
                order(dve.tensor_tensor(k.mtmp[:, 0, :], k.mtmp[:, 1, :], parts[:, 1, :], ALU.subtract))
                order(dve.tensor_copy(parts[:, 2, :], k.mtmp[:, 0, :]))
            order(dve.tensor_scalar(k.hm[:, :], k.c["headmask"], float(DH) ** -0.5, None, ALU.mult))
            order(dve.tensor_copy(k.pick3[:, :], k.c["pick3"]))
            row_stats(dve, order, k, k.xs)
            order(dve.tensor_copy(k.identb[:, :], k.c["ident"]))
            order.end()

        @block.scalar
        def _(act):
            act.wait_ge(k.const_ordered, 12)
            for parts, dst in ((k.split_a, k.mask3_a), (k.split_d, k.mask3_d)):
                for j in range(3):
                    act.dma_start(dst[j:j + 1, :].rearrange("o (b n) -> o b n", n=SC), parts[:, j, :]).then_inc(k.mask_moved, 16)
            act.wait_ge(k.mask_moved, 16 * 6)


def attention(nc, k, st, wq, wk, wv, wo, bq, bk, bv_row, bo_row, src, affine, mask3, own_keys):
    taps = len(wq)
    NK = S if own_keys else SC
    PB = SC // NK
    NB = NPAIR // PB
    HB = NB // 2
    first = affine is None and taps == KS
    sem = lambda name: k.sem(f"{st}_{name}")
    with ExitStack() as ctx:
        def sb(name, shape, dt=F32):
            return ctx.enter_context(nc.sbuf_tensor(f"{st}_{name}", shape, dt))

        cx = sb("context", [P, 2, SC + 2])
        xq = sb("query_in", [P, P])
        xs_n = sb("scaled_in", [P, P])
        xT = sb("query_inT", [P, 2, S + 2])
        qT = sb("qT", [P, 2, S])
        qbd = sb("q_heads", [P, 2, 8, S])
        v_in = sb("v_plain", [P, 2, P])
        kT = sb("kT", [P, 2, NK])
        va = sb("v_ones", [P, 2, NB, PB, 17])
        pr = sb("probs", [P, 2, NPAIR, NK])
        prT = sb("probsT", [P, 2, NB, P])
        mx = sb("row_max", [P, 2, NPAIR])
        rd = sb("row_recip", [P, 2, NPAIR])
        on = sb("attended", [P, 2, NPAIR, 2, DH])
        oT = sb("attendedT", [P, P])
        std = sb("std", [P, NT])
        rstd = sb("rstd", [P, NT])
        sc = ctx.enter_context(nc.psum_tensor(f"{st}_scores", [P, 2, 2, 512], F32))
        pt = ctx.enter_context(nc.psum_tensor(f"{st}_turned", [P, 2, 512], F32))
        pa = ctx.enter_context(nc.psum_tensor(f"{st}_turn_bank", [P, 512], F32))
        pb = ctx.enter_context(nc.psum_tensor(f"{st}_out_bank", [P, 512], F32))
        xT_p, oT_p, out_p = pa[:, 0:P], pa[:, 0:P], pb[:, 0:P]
        q_p, k_p, v_p = pt[:, 0, 0:P], pt[:, 0, P:P + 2 * NK], pt[:, 1, 0:2 * P]

        def att_p(b):
            return pb[:, b * 256:b * 256 + NPAIR * 17].rearrange("p (a c) -> p a c", c=17)

        zeroed, stats, std_made, rstd_made = sem("zeroed"), sem("stats"), sem("std_made"), sem("rstd_made")
        ctx_ready, xq_ready, xT_turned, xT_ready = sem("ctx_ready"), sem("xq_ready"), sem("xT_turned"), sem("xT_ready")
        q_done, k_done, v_done = sem("q_done"), sem("k_done"), sem("v_done")
        q_copied, k_ready, v_copied = sem("q_copied"), sem("k_ready"), sem("v_copied")
        q_ready, v_ready = sem("q_ready"), sem("v_ready")
        s_done, max_ready, p_ready, e_ready = sem("s_done"), sem("max_ready"), sem("p_ready"), sem("e_ready")
        t_done, t_ready, o_done, recip_ready, o_ready = sem("t_done"), sem("t_ready"), sem("o_done"), sem("recip_ready"), sem("o_ready")
        oT_done, oT_ready, out_done, sum_ready = sem("oT_done"), sem("oT_ready"), sem("out_done"), sem("sum_ready")
        own, va_cleared, va_filled = sem("tile_steps"), sem("va_cleared"), sem("va_filled")
        block = ctx.enter_context(nc.Block())

        @block.sync
        def _(sp):
            if own_keys:
                return
            sp.wait_ge(zeroed, 3)
            with sp.Fori(0, NT) as i:
                sp.wait_ge(v_done, i)
                sp.dma_start(cx[:, :, 1:SC + 1], k.dram["ctxT"][:, tile(i, 2 * SC)].rearrange("p (b n) -> p b n", b=2))\
                    .then_inc(ctx_ready, 16)

        @block.gpsimd
        def _(pool):
            pool.memset(cx[:, :, :], 0.0).then_inc(zeroed, 1)
            pool.memset(xT[:, :, :], 0.0).then_inc(zeroed, 1)
            pool.memset(on[:, :, :, :, :], 0.0).then_inc(zeroed, 1)
            pool.memset(va[:, :, :, :, :], 0.0).then_inc(va_cleared, 1)
            for n in range(PB):
                pool.wait_ge(va_cleared, n + 1)
                pool.memset(va[n * NK:(n + 1) * NK, :, :, n, 16], 1.0).then_inc(va_cleared, 1)
            pool.wait_ge(va_cleared, PB + 1)
            pool.sem_inc(zeroed, 1)
            with pool.Fori(0, NT) as i:
                pool.wait_ge(q_copied, i + 1)
                pool.wait_ge(s_done, 2 * i)
                pool.tensor_tensor(qbd[:, :, :, :], qT[:, :, :].unsqueeze(2).to_broadcast([P, 2, 8, S]),
                                   k.hm[:, :].unsqueeze(1).unsqueeze(3).to_broadcast([P, 2, 8, S]), ALU.mult).then_inc(q_ready, 1)
                pool.wait_ge(v_copied, i + 1)
                pool.wait_ge(o_done, 2 * i)
                for n in range(PB):
                    r = slice(n * NK, (n + 1) * NK)
                    blocks = lambda ap: ap.rearrange("p (a n c) -> p a n c", n=PB, c=16)[:, :, n, :]
                    for b in range(2):
                        ins = pool.tensor_tensor(va[r, b, :, n, 0:16], blocks(v_in[r, b, :]), blocks(k.row(bv_row)[r, :]), ALU.add)
                    if n < PB - 1:
                        ins.then_inc(va_filled, 1)
                        pool.wait_ge(va_filled, i + 1)
                ins.then_inc(v_ready, 1)
                if PB > 1:
                    pool.wait_ge(v_ready, i + 1)

        @block.scalar
        def _(act):
            act.wait_ge(stats, 1)
            act.activation(std[:, :], variances(k), ACT.Sqrt, bias=k.eps[:, :]).then_inc(std_made, 1)
            act.wait_ge(zeroed, 4)

            def front(i):
                act.wait_ge(xT_turned, i + 1)
                act.wait_ge(v_done, i)
                act.activation(xT[:, :, 1:S + 1], xT_p.rearrange("p (b s) -> p b s", b=2), ACT.Copy).then_inc(xT_ready, 1)

            def keys(i):
                act.wait_ge(k_done, i + 1)
                act.wait_ge(q_ready, i)
                act.activation(qT[:, :, :], q_p.rearrange("p (b s) -> p b s", b=2), ACT.Identity, bias=bq).then_inc(q_copied, 1)
                act.wait_ge(v_done, i + 1)
                act.wait_ge(v_ready, i)
                act.activation(v_in[:, :, :], v_p.rearrange("p (b c) -> p b c", b=2), ACT.Copy).then_inc(v_copied, 1)
                act.wait_ge(s_done, 2 * i)
                act.activation(kT[:, :, :], k_p.rearrange("p (b n) -> p b n", b=2), ACT.Identity, bias=bk).then_inc(k_ready, 1)

            def soft(i, b):
                act.wait_ge(p_ready, 2 * i + b + 1)
                act.activation(pr[:, b, :, :], pr[:, b, :, :], ACT.Exp).then_inc(e_ready, 1)

            def turn(i, b):
                for half in range(2):
                    act.wait_ge(t_done, 4 * i + 2 * b + half + 1)
                    act.wait_ge(o_done, 2 * i)
                    act.activation(prT[:, b, HB * half:HB * half + HB, :], pt[:, half, 0:HB * P].rearrange("p (a c) -> p a c", a=HB),
                                   ACT.Copy).then_inc(t_ready, 1)

            front(0)
            keys(0)

            def body(i, last):
                if not last:
                    front(i + 1)
                soft(i, 0)
                if not last:
                    keys(i + 1)
                soft(i, 1)
                turn(i, 0)
                turn(i, 1)
                act.wait_ge(oT_done, i + 1)
                act.wait_ge(out_done, i)
                act.activation(oT[:, :], oT_p, ACT.Copy).then_inc(oT_ready, 1)

            pipeline(act, NT, body)

        @block.vector
        def _(dve):
            order = Order(dve, stats, 1)
            aggregate(dve, order, k)
            dve.wait_ge(std_made, 1)
            dve.reciprocal(rstd[:, :], std[:, :]).then_inc(rstd_made, 1)
            dve.wait_ge(rstd_made, 1)
            dve.wait_ge(zeroed, 4)

            def norm_in(i):
                dve.wait_ge(xT_turned, i)
                outs = [xq[:, :]] if first else [k.res[:, tile(i)], xq[:, :]]
                plain = [xs_n[:, :]] if affine else outs
                for o in plain:
                    ins = dve.tensor_scalar(o, src[:, tile(i)], k.mv[:, bass.ds(2 * i, 1)], rstd[:, bass.ds(i, 1)],
                                            ALU.subtract, ALU.mult)
                if affine:
                    order = Order(dve, own, 2, i)
                    order(ins)
                    order(dve.tensor_tensor(xs_n[:, :], xs_n[:, :], k.row(affine[0]), ALU.mult))
                    order.end()
                    for o in outs:
                        ins = dve.tensor_tensor(o, xs_n[:, :], k.row(affine[1]), ALU.add)
                ins.then_inc(xq_ready, 1)

            def soft(i, b):
                dve.wait_ge(s_done, 2 * i + b + 1)
                s4 = sc[:, b, :, 0:4 * NK].rearrange("p h (a n) -> p h a n", a=4)
                dve.tensor_reduce(mx[:, b, :].rearrange("p (h a) -> p h a", h=2), s4, AX.X, ALU.max).then_inc(max_ready, 1)
                dve.wait_ge(max_ready, 2 * i + b + 1)
                dve.wait_ge(t_done, 4 * i)
                dve.tensor_tensor(pr[:, b, :, :].rearrange("p (h a) n -> p h a n", h=2), s4,
                                  mx[:, b, :].rearrange("p (h a) -> p h a", h=2).unsqueeze(3).to_broadcast([P, 2, 4, NK]),
                                  ALU.subtract).then_inc(p_ready, 1)

            def divide(i, b):
                dve.wait_ge(o_done, 2 * i + b + 1)
                dve.wait_ge(oT_done, i)
                o = att_p(b)
                dve.reciprocal(rd[:, b, :], o[:, :, 16]).then_inc(recip_ready, 1)
                dve.wait_ge(recip_ready, 2 * i + b + 1)
                for h in range(2):
                    r = slice(h * S, (h + 1) * S)
                    ins = dve.tensor_tensor(on[r, b, :, h, :], o[r, :, h * DH:(h + 1) * DH],
                                            rd[r, b, :].unsqueeze(2).to_broadcast([S, NPAIR, DH]), ALU.mult)
                ins.then_inc(o_ready, 1)

            def add_out(i):
                dve.wait_ge(out_done, i + 1)
                into, old = (k.xs, k.xs) if first else (k.rs, k.res)
                dve.tensor_tensor(into[:, tile(i)], out_p, old[:, tile(i)], ALU.add).then_inc(sum_ready, 1)
                dve.wait_ge(sum_ready, i + 1)
                dve.bn_stats(k.st[:, bass.ds(6 * i, 6)], into[:, tile(i)])

            norm_in(0)

            def body(i, last):
                if not last:
                    norm_in(i + 1)
                soft(i, 0)
                soft(i, 1)
                dve.wait_ge(o_done, 2 * i + 2)
                divide(i, 0)
                divide(i, 1)
                add_out(i)

            pipeline(dve, NT, body)

        @block.tensor
        def _(pe):
            def front(i, not_first=True):
                pe.wait_ge(xq_ready, i + 1)
                if not_first:
                    pe.wait_ge(oT_ready, i - 1)
                pe.transpose(xT_p, xq[:, :], k.c["ident"]).then_inc(xT_turned, 1)
                pe.wait_ge(xT_ready, i + 1)
                if not_first:
                    pe.wait_ge(t_ready, 4 * i - 4)
                kv = xT if own_keys else cx
                if not own_keys:
                    pe.wait_ge(ctx_ready, 16 * (i + 1))
                for t in range(taps):
                    a = 1 + t - taps // 2
                    pe.matmul(q_p.rearrange("p (b s) -> p b s", b=2), wq[t], xT[:, :, a:a + S], start=t == 0, stop=t == taps - 1)
                for t in range(taps):
                    a = 1 + t - taps // 2
                    mm = pe.matmul(k_p.rearrange("p (b n) -> p b n", b=2), wk[t], kv[:, :, a:a + NK],
                                   start=t == 0, stop=t == taps - 1)
                mm.then_inc(k_done, 1)
                for b in range(2):
                    for n in range(PB):
                        for t in range(taps):
                            a = 1 + t - taps // 2
                            mm = pe.matmul(v_p[n * NK:(n + 1) * NK, b * P:(b + 1) * P], kv[:, b, a:a + NK], wv[t],
                                           start=t == 0, stop=t == taps - 1)
                mm.then_inc(v_done, 1)

            def scores(i):
                pe.wait_ge(q_ready, i + 1)
                pe.wait_ge(k_ready, i + 1)
                for b in range(2):
                    pe.wait_ge(p_ready, 2 * i)
                    for h in range(2):
                        out = sc[:, b, h, 0:4 * NK].rearrange("p (a n) -> p a n", a=4)
                        if mask3 is not None:
                            m = mask3[:, bass.ds((2 * i + b) * SC, NK)].unsqueeze(1).to_broadcast([3, 4, NK])
                            pe.matmul(out, k.ones3[0:3, :], m, start=True, stop=False)
                        for a in range(4):
                            mm = pe.matmul(out[:, a, :], qbd[64 * h:64 * h + 64, b, 2 * a:2 * a + 2, :].rearrange("p a s -> p (a s)"),
                                           kT[64 * h:64 * h + 64, b, :], start=mask3 is None, stop=mask3 is None or a == 3)
                    mm.then_inc(s_done, 1)

            def turn(i, b, last):
                if b == 0 and not last:
                    pe.wait_ge(k_ready, i + 2)
                    pe.wait_ge(v_copied, i + 2)
                pe.wait_ge(e_ready, 2 * i + b + 1)
                for half in range(2):
                    if b:
                        pe.wait_ge(t_ready, 4 * i + half + 1)
                    for j in range(HB):
                        a = (HB * half + j) * PB
                        mm = pe.transpose(pt[:, half, j * P:(j + 1) * P], pr[:, b, a:a + PB, :].rearrange("p a n -> p (a n)"),
                                          k.c["ident"])
                    mm.then_inc(t_done, 1)

            def attend(i, b):
                pe.wait_ge(t_ready, 4 * i + 2 * b + 2)
                pe.wait_ge(v_ready, i + 1)
                pe.wait_ge(sum_ready, i)
                o = att_p(b)
                for n in range(NB):
                    mm = pe.matmul(o[:, n * PB:(n + 1) * PB, :].rearrange("p a c -> p (a c)"), prT[:, b, n, :],
                                   va[:, b, n, :, :].rearrange("p a c -> p (a c)"), start=True, stop=True)
                mm.then_inc(o_done, 1)

            def project(i):
                pe.wait_ge(o_ready, 2 * i + 2)
                for b in range(2):
                    mm = pe.matmul(oT_p[:, b * S:(b + 1) * S], on[:, b, :, :, :].rearrange("p a h d -> p (a h d)"), k.c["sel64"],
                                   start=True, stop=True)
                mm.then_inc(oT_done, 1)
                pe.wait_ge(oT_ready, i + 1)
                pe.matmul(out_p, k.ones[0:1, :], k.row(bo_row)[0:1, :], start=True, stop=False)
                pe.matmul(out_p, oT[:, :], wo, start=False, stop=True).then_inc(out_done, 1)

            front(0, False)

            def body(i, last):
                scores(i)
                if not last:
                    front(i + 1)
                turn(i, 0, last)
                turn(i, 1, last)
                attend(i, 0)
                attend(i, 1)
                project(i)

            pipeline(pe, NT, body)


def scan_stage(nc, k):
    CH = 512
    NC = B * S // CH
    G = 4
    centre, half = (DT_MAX + DT_MIN) / 2.0, (DT_MAX - DT_MIN) / 2.0
    sem = lambda name: k.sem(f"b_{name}")
    with ExitStack() as ctx:
        def sb(name, shape, dt=F32):
            return ctx.enter_context(nc.sbuf_tensor(f"b_{name}", shape, dt))

        xnT = sb("xnT", [P, B * S])
        delta = sb("delta", [P, B * S])
        u = sb("sqrt_delta_x", [P, B * S])
        yT = sb("yT", [P, B * S])
        bc3 = sb("bc_terms", [96, B * S], BF16)
        sa = sb("half_a", [P, NSTATE])
        small = sb("row_factors", [P, 6, NT])
        neg1 = sb("minus_one", [P, 1])
        tbias = sb("tanh_bias", [P, 1])
        rbias = sb("rms_eps", [P, 1])
        with ExitStack() as inner:
            t1 = inner.enter_context(nc.sbuf_tensor("b_t1", [P, B * S], F32))
            t2 = inner.enter_context(nc.sbuf_tensor("b_t2", [P, B * S], F32))
            rest = inner.enter_context(nc.sbuf_tensor("b_rest", [32, 2, CH], F32))
            low = inner.enter_context(nc.sbuf_tensor("b_low", [32, 2, B * S], BF16))
            turned = inner.enter_context(nc.psum_tensor("b_turned", [P, 2, 512], F32))
            dp = inner.enter_context(nc.psum_tensor("b_delta_p", [P, 2, 512], F32))
            bp = inner.enter_context(nc.psum_tensor("b_bc_p", [32, 2, 512], F32))
            made, varied, std1, std2 = sem("constants"), sem("varied"), sem("std1"), sem("std2")
            xn_ready, xn_turned, xnT_ready = sem("xn_ready"), sem("xn_turned"), sem("xnT_ready")
            d_done, d_left, bc_done, bc_left = sem("d_done"), sem("d_left"), sem("bc_done"), sem("bc_left")
            act_steps, dve_steps, low_ready = sem("act_steps"), sem("dve_steps"), sem("low_ready")
            soft_ready, sum_ready, exp_ready, delta_ready, root_ready = (
                sem("soft_ready"), sem("sum_ready"), sem("exp_ready"), sem("delta_ready"), sem("root_ready"))
            a_ready, moved = sem("a_ready"), sem("moved")
            with nc.Block() as block:
                @block.gpsimd
                def _(pool):
                    pool.memset(neg1[:, :], -1.0).then_inc(made, 1)
                    pool.memset(tbias[:, :], -2.0 * centre / half).then_inc(made, 1)
                    pool.memset(rbias[:, :], RMS_EPS).then_inc(made, 1)
                    pool.wait_ge(low_ready, NC)
                    for j in range(2):
                        pool.tensor_copy(bc3[32 * (j + 1):32 * (j + 2), :], low[:, j, :]).then_inc(moved, 1)
                        pool.wait_ge(moved, j + 1)
                    pool.wait_ge(xnT_ready, NC)
                    pool.tensor_scalar(yT[:, :], xnT[:, :], k.c["d_skip"], None, ALU.mult)

                @block.vector
                def _(dve):
                    order = Order(dve, dve_steps, 8 + 5 * NC)
                    aggregate(dve, order, k)
                    dve.sem_inc(varied, 1)
                    dve.wait_ge(std1, 1)
                    rstd, msq, r2, rs = small[:, 1, :], small[:, 2, :], small[:, 4, :], small[:, 5, :]
                    order(dve.reciprocal(rstd, small[:, 0, :]))
                    order(dve.tensor_tensor(msq, variances(k), rstd, ALU.mult))
                    order(dve.tensor_tensor(msq, msq, rstd, ALU.mult))
                    dve.sem_inc(varied, 1)
                    dve.wait_ge(std2, 1)
                    order(dve.reciprocal(r2, small[:, 3, :]))
                    order(dve.tensor_tensor(rs, rstd, r2, ALU.mult))
                    for t in range(NT):
                        ins = dve.tensor_scalar(k.res[:, t * P:(t + 1) * P], k.xs[:, t * P:(t + 1) * P], k.mv[:, 2 * t:2 * t + 1],
                                                rs[:, t:t + 1], ALU.subtract, ALU.mult)
                        if t % 4 == 3:
                            ins.then_inc(xn_ready, 1)
                    for c in range(NC):
                        r = slice(c * CH, (c + 1) * CH)
                        dve.wait_ge(bc_done, c + 1)
                        b = bp[:, c % 2, :]
                        order(dve.tensor_copy(bc3[0:32, r], b))
                        order(dve.tensor_tensor(rest[:, 0, :], b, bc3[0:32, r], ALU.subtract))
                        dve.sem_inc(bc_left, 1)
                        order(dve.tensor_copy(low[:, 0, r], rest[:, 0, :]))
                        order(dve.tensor_tensor(rest[:, 1, :], rest[:, 0, :], low[:, 0, r], ALU.subtract))
                        order(dve.tensor_copy(low[:, 1, r], rest[:, 1, :]))
                        dve.sem_inc(low_ready, 1)
                    dve.wait_ge(soft_ready, 1)
                    dve.tensor_tensor(t1[:, :], t1[:, :], t2[:, :], ALU.add).then_inc(sum_ready, 1)
                    dve.wait_ge(exp_ready, 1)
                    order(dve.tensor_scalar(t1[:, :], t1[:, :], 1.0, None, ALU.add))
                    order(dve.reciprocal(t1[:, :], t1[:, :]))
                    dve.tensor_scalar(delta[:, :], t1[:, :], -2.0 * half, centre + half, ALU.mult, ALU.add).then_inc(delta_ready, 1)
                    dve.wait_ge(root_ready, 1)
                    dve.tensor_tensor(u[:, :], t2[:, :], xnT[:, :], ALU.mult)
                    dve.wait_ge(a_ready, 1)
                    dve.tensor_scalar(sa[:, :], sa[:, :], 0.5, None, ALU.mult)
                    order.end()

                @block.scalar
                def _(act):
                    act.wait_ge(k.late_loaded, 16 * 5)
                    act.wait_ge(varied, 1)
                    act.activation(small[:, 0, :], variances(k), ACT.Sqrt, bias=k.eps[:, :]).then_inc(std1, 1)
                    act.wait_ge(varied, 2)
                    act.wait_ge(made, 3)
                    act.activation(small[:, 3, :], small[:, 2, :], ACT.Sqrt, bias=rbias[:, :]).then_inc(std2, 1)
                    for c in range(NC):
                        act.wait_ge(xn_turned, c + 1)
                        act.activation(xnT[:, c * CH:(c + 1) * CH], turned[:, c % 2, :], ACT.Copy, scale=k.c["norm_w"]).then_inc(xnT_ready, 1)
                    for c in range(NC):
                        r = slice(c * CH, (c + 1) * CH)
                        act.wait_ge(d_done, c + 1)
                        act.activation(t1[:, r], dp[:, c % 2, :], ACT.Abs, bias=k.c["b_delta"])
                        act.activation(t2[:, r], dp[:, c % 2, :], ACT.Relu, bias=k.c["b_delta"]).then_inc(d_left, 1)
                    act.wait_ge(d_left, NC)
                    order = Order(act, act_steps, 1)
                    order(act.activation(t1[:, :], t1[:, :], ACT.Exp, scale=-1.0))
                    act.activation(t1[:, :], t1[:, :], ACT.Ln, bias=k.ones[:, 0:1]).then_inc(soft_ready, 1)
                    act.wait_ge(sum_ready, 1)
                    act.activation(t1[:, :], t1[:, :], ACT.Exp, bias=tbias[:, :], scale=2.0 / half).then_inc(exp_ready, 1)
                    act.activation(sa[:, :], k.c["alog"], ACT.Exp).then_inc(a_ready, 1)
                    act.wait_ge(delta_ready, 1)
                    act.activation(t2[:, :], delta[:, :], ACT.Sqrt).then_inc(root_ready, 1)

                @block.tensor
                def _(pe):
                    pe.wait_ge(k.late_loaded, 16 * 5)
                    for c in range(NC):
                        pe.wait_ge(xn_ready, c + 1)
                        if c >= 2:
                            pe.wait_ge(xnT_ready, c - 1)
                        for j in range(4):
                            t = 4 * c + j
                            mm = pe.transpose(turned[:, c % 2, j * P:(j + 1) * P], k.res[:, t * P:(t + 1) * P], k.c["ident"])
                        mm.then_inc(xn_turned, 1)
                    for c in range(NC):
                        r = slice(c * CH, (c + 1) * CH)
                        pe.wait_ge(xnT_ready, c + 1)
                        if c >= 2:
                            pe.wait_ge(d_left, c - 1)
                            pe.wait_ge(bc_left, c - 1)
                        pe.matmul(dp[:, c % 2, :], k.c["wdelta"], xnT[:, r], start=True, stop=True).then_inc(d_done, 1)
                        pe.matmul(bp[:, c % 2, :], k.c["wbc"], xnT[:, r], start=True, stop=True).then_inc(bc_done, 1)

        with ExitStack() as inner:
            def buf(name, shape=None):
                return inner.enter_context(nc.sbuf_tensor(f"b_{name}", shape or [P, G, CH], F32))

            den, inv, ab, w, bx, h, hc = (buf(n) for n in ("denom", "inverse", "a_bar", "inverse_u", "b_x", "states", "states_c"))
            bb = inner.enter_context(nc.psum_tensor("b_b_bank", [P, G, 512], F32))
            cb = inner.enter_context(nc.psum_tensor("b_c_bank", [P, G, 512], F32))
            cleared, den_ready, inv_ready, ab_ready, w_ready = (sem(n) for n in ("cleared", "den_ready", "inv_ready", "ab_ready", "w_ready"))
            bb_done, bx_ready, h_ready, hc_ready, y_ready = (sem(n) for n in ("bb_done", "bx_ready", "h_ready", "hc_ready", "y_ready"))

            def groups(eng, body):
                for c in range(NC):
                    with eng.Fori(0, NSTATE // G) as g:
                        body(c, G * g, NSTATE * c + G * g)

            with nc.Block() as block:
                @block.scalar
                def _(act):
                    act.wait_ge(cleared, 1)

                    def body(c, n, s):
                        act.wait_ge(inv_ready, s)
                        for j in range(G):
                            act.activation(den[:, j, :], delta[:, c * CH:(c + 1) * CH], ACT.Identity, bias=k.ones[:, 0:1],
                                           scale=sa[:, bass.ds(n + j, 1)]).then_inc(den_ready, 1)
                        act.wait_ge(h_ready, s)
                        for j in range(G):
                            act.wait_ge(inv_ready, s + j + 1)
                            act.activation(ab[:, j, :].rearrange("p (b s) -> p b s", s=S)[:, :, 1:S],
                                           inv[:, j, :].rearrange("p (b s) -> p b s", s=S)[:, :, 1:S],
                                           ACT.Identity, bias=neg1[:, :], scale=2.0).then_inc(ab_ready, 1)

                    groups(act, body)

                @block.gpsimd
                def _(pool):
                    pool.memset(ab[:, :, :], 0.0).then_inc(cleared, 1)

                    def body(c, n, s):
                        pool.wait_ge(bx_ready, s)
                        for j in range(G):
                            pool.wait_ge(inv_ready, s + j + 1)
                            pool.tensor_tensor(w[:, j, :], inv[:, j, :], u[:, c * CH:(c + 1) * CH], ALU.mult).then_inc(w_ready, 1)
                        for j in range(G):
                            pool.wait_ge(hc_ready, s + j + 1)
                            pool.wait_ge(y_ready, s + j)
                            pool.tensor_tensor(yT[:, c * CH:(c + 1) * CH], yT[:, c * CH:(c + 1) * CH], hc[:, j, :], ALU.add).then_inc(y_ready, 1)

                    groups(pool, body)

                @block.vector
                def _(dve):
                    dve.wait_ge(cleared, 1)

                    def body(c, n, s):
                        dve.wait_ge(ab_ready, s)
                        dve.wait_ge(w_ready, s)
                        for j in range(G):
                            dve.wait_ge(den_ready, s + j + 1)
                            dve.reciprocal(inv[:, j, :], den[:, j, :]).then_inc(inv_ready, 1)
                        for j in range(G):
                            dve.wait_ge(w_ready, s + j + 1)
                            dve.wait_ge(bb_done, s + j + 1)
                            dve.tensor_tensor(bx[:, j, :], w[:, j, :], bb[:, j, :], ALU.mult).then_inc(bx_ready, 1)
                            dve.wait_ge(bx_ready, s + j + 1)
                            dve.wait_ge(ab_ready, s + j + 1)
                            dve.tensor_tensor_scan(h[:, j, :], ab[:, j, :], bx[:, j, :], 0.0, ALU.mult, ALU.add).then_inc(h_ready, 1)
                            dve.wait_ge(h_ready, s + j + 1)
                            dve.wait_ge(y_ready, s)
                            dve.tensor_tensor(hc[:, j, :], h[:, j, :], cb[:, j, :], ALU.mult).then_inc(hc_ready, 1)

                    groups(dve, body)

                @block.tensor
                def _(pe):
                    def body(c, n, s):
                        pe.wait_ge(hc_ready, s)
                        for j in range(G):
                            pe.matmul(bb[:, j, :], k.pick3[0:96, bass.ds(n + j, 1)].to_broadcast([96, P]), bc3[:, c * CH:(c + 1) * CH],
                                      start=True, stop=True)
                            pe.matmul(cb[:, j, :], k.pick3[0:96, bass.ds(n + j + NSTATE, 1)].to_broadcast([96, P]), bc3[:, c * CH:(c + 1) * CH],
                                      start=True, stop=True).then_inc(bb_done, 1)

                    groups(pe, body)

        turned, added, rows_turned = ctx.enter_context(nc.psum_tensor("b_rows", [P, NC, 512], F32)), sem("added"), sem("rows_turned")
        with nc.Block() as block:
            @block.tensor
            def _(pe):
                for t in range(NT):
                    mm = pe.transpose(turned[:, t // 4, t % 4 * P:(t % 4 + 1) * P], yT[:, t * P:(t + 1) * P], k.c["ident"])
                    if t % 4 == 3:
                        mm.then_inc(rows_turned, 1)

            @block.vector
            def _(dve):
                for c in range(NC):
                    r = slice(c * CH, (c + 1) * CH)
                    dve.wait_ge(rows_turned, c + 1)
                    dve.tensor_tensor(k.xs[:, r], k.xs[:, r], turned[:, c, :], ALU.add).then_inc(added, 1)
                    dve.wait_ge(added, c + 1)
                    for t in range(4 * c, 4 * c + 4):
                        dve.bn_stats(k.st[:, 6 * t:6 * t + 6], k.xs[:, t * P:(t + 1) * P])


def top_experts(dve, order, pool_filled, score, picked, values, kept, n, top, pad):
    for t in range(NT):
        ins = dve.max(values[:, t, :], score[:, t, :])
    order(ins)
    order(dve.memset(values[:, :, top:8], -1.0))
    for t in range(NT):
        ins = dve.match_replace(picked[:, t, :], values[:, t, :], score[:, t, :], -2.0)
    order(ins)
    order(dve.tensor_scalar(picked[:, :, 0:n], picked[:, :, 0:n], -2.0, None, ALU.is_equal))
    order(dve.tensor_tensor(kept, picked[:, :, 0:n], score[:, :, 0:n], ALU.mult))


def experts_stage(nc, k):
    N8 = E0 * H0 // P
    sem = lambda name: k.sem(f"c_{name}")
    with ExitStack() as ctx:
        def sb(name, shape, dt=F32):
            return ctx.enter_context(nc.sbuf_tensor(f"c_{name}", shape, dt))

        def psum(name, shape):
            return ctx.enter_context(nc.psum_tensor(f"c_{name}", shape, F32))

        comb = sb("weights", [P, NT, E0])
        rstd = sb("rstd", [P, NT])
        with ExitStack() as inner:
            hT = inner.enter_context(nc.sbuf_tensor("c_hT_all", [P, B * S], F32))
            small = inner.enter_context(nc.sbuf_tensor("c_row_factors", [P, 4, NT], F32))
            gR = inner.enter_context(nc.sbuf_tensor("c_scaled_router", [P, E0], F32))
            bR = inner.enter_context(nc.sbuf_tensor("c_router_bias", [P, E0], F32))
            lg = inner.enter_context(nc.sbuf_tensor("c_logits", [P, NT, E0], F32))
            score = inner.enter_context(nc.sbuf_tensor("c_scores", [P, NT, E0 + 6], F32))
            picked = inner.enter_context(nc.sbuf_tensor("c_picked", [P, NT, E0 + 6], F32))
            values = inner.enter_context(nc.sbuf_tensor("c_values", [P, NT, 8], F32))
            red = inner.enter_context(nc.sbuf_tensor("c_reduced", [P, 4, NT], F32))
            turned = inner.enter_context(nc.psum_tensor("c_turned_p", [P, 2, 512], F32))
            lp = inner.enter_context(nc.psum_tensor("c_logit_p", [P, 512], F32))
            bp = inner.enter_context(nc.psum_tensor("c_bias_p", [P, 512], F32))
            varied, std1, std2, filled, steps = sem("varied"), sem("std1"), sem("std2"), sem("filled"), sem("router_steps")
            h_ready, h_turned, hT_ready, gR_ready = sem("h_ready"), sem("h_turned"), sem("hT_ready"), sem("gR_ready")
            logit_done, shifted, exp_ready = sem("logit_done"), sem("shifted"), sem("exp_ready")
            with nc.Block() as block:
                @block.gpsimd
                def _(pool):
                    pool.memset(score[:, :, :], -1.0).then_inc(filled, 1)

                @block.scalar
                def _(act):
                    act.wait_ge(varied, 1)
                    act.activation(small[:, 0, :], variances(k), ACT.Sqrt, bias=k.eps[:, :]).then_inc(std1, 1)
                    act.wait_ge(varied, 2)
                    act.activation(small[:, 2, :], small[:, 1, :], ACT.Sqrt, bias=k.eps[:, :]).then_inc(std2, 1)
                    for c in range(4):
                        act.wait_ge(h_turned, c + 1)
                        act.activation(hT[:, c * 512:(c + 1) * 512], turned[:, c % 2, :], ACT.Copy).then_inc(hT_ready, 1)
                    act.wait_ge(shifted, 1)
                    act.activation(lg[:, :, :], lg[:, :, :], ACT.Exp).then_inc(exp_ready, 1)

                @block.tensor
                def _(pe):
                    for c in range(4):
                        pe.wait_ge(h_ready, c + 1)
                        if c >= 2:
                            pe.wait_ge(hT_ready, c - 1)
                        for j in range(4):
                            t = 4 * c + j
                            mm = pe.transpose(turned[:, c % 2, j * P:(j + 1) * P], k.res[:, t * P:(t + 1) * P], k.c["ident"])
                        mm.then_inc(h_turned, 1)
                    pe.wait_ge(gR_ready, 1)
                    pe.matmul(bp[:, 0:E0], k.c["rn_b"].to_broadcast([P, P]), k.c["router"], start=True, stop=True)
                    for t in range(NT):
                        if t % 4 == 0:
                            pe.wait_ge(hT_ready, t // 4 + 1)
                        mm = pe.matmul(lp[:, t * E0:(t + 1) * E0], hT[:, t * P:(t + 1) * P], gR[:, :], start=True, stop=True)
                    mm.then_inc(logit_done, 1)

                @block.vector
                def _(dve):
                    order = Order(dve, steps, 21)
                    aggregate(dve, order, k)
                    dve.sem_inc(varied, 1)
                    dve.wait_ge(std1, 1)
                    order(dve.reciprocal(rstd[:, :], small[:, 0, :]))
                    order(dve.tensor_tensor(small[:, 1, :], variances(k), rstd[:, :], ALU.mult))
                    order(dve.tensor_tensor(small[:, 1, :], small[:, 1, :], rstd[:, :], ALU.mult))
                    dve.sem_inc(varied, 1)
                    dve.tensor_scalar(gR[:, :], k.c["router"], k.c["rn_g"], None, ALU.mult).then_inc(gR_ready, 1)
                    for t in range(NT):
                        ins = dve.tensor_scalar(k.res[:, t * P:(t + 1) * P], k.xs[:, t * P:(t + 1) * P], k.mv[:, 2 * t:2 * t + 1],
                                                rstd[:, t:t + 1], ALU.subtract, ALU.mult)
                        if t % 4 == 3:
                            ins.then_inc(h_ready, 1)
                    dve.wait_ge(std2, 1)
                    order(dve.reciprocal(small[:, 3, :], small[:, 2, :]))
                    dve.wait_ge(logit_done, 1)
                    order(dve.tensor_copy(bR[:, :], bp[:, 0:E0]))
                    order(dve.tensor_tensor(lg[:, :, :], lp[:, 0:NT * E0].rearrange("p (t e) -> p t e", e=E0),
                                            small[:, 3, :].unsqueeze(2).to_broadcast([P, NT, E0]), ALU.mult))
                    order(dve.tensor_tensor(lg[:, :, :], lg[:, :, :], bR[:, :].unsqueeze(1).to_broadcast([P, NT, E0]), ALU.add))
                    order(dve.tensor_reduce(red[:, 0, :], lg[:, :, :], AX.X, ALU.max))
                    dve.tensor_tensor(lg[:, :, :], lg[:, :, :], red[:, 0, :].unsqueeze(2).to_broadcast([P, NT, E0]),
                                      ALU.subtract).then_inc(shifted, 1)
                    dve.wait_ge(exp_ready, 1)
                    order(dve.tensor_reduce(red[:, 1, :], lg[:, :, :], AX.X, ALU.add))
                    order(dve.reciprocal(red[:, 1, :], red[:, 1, :]))
                    dve.wait_ge(filled, 1)
                    order(dve.tensor_tensor(score[:, :, 0:E0], lg[:, :, :], red[:, 1, :].unsqueeze(2).to_broadcast([P, NT, E0]), ALU.mult))
                    top_experts(dve, order, filled, score, picked, values, comb[:, :, :], E0, 2, 6)
                    order(dve.tensor_reduce(red[:, 2, :], comb[:, :, :], AX.X, ALU.add))
                    order(dve.tensor_scalar(red[:, 2, :], red[:, 2, :], 1e-8, None, ALU.add))
                    order(dve.reciprocal(red[:, 2, :], red[:, 2, :]))
                    order(dve.tensor_tensor(comb[:, :, :], comb[:, :, :], red[:, 2, :].unsqueeze(2).to_broadcast([P, NT, E0]), ALU.mult))
                    order.end()

        xq, hT, z, aT = sb("h", [P, P]), sb("hT", [P, P]), sb("hidden_n", [P, E0, H0]), sb("hidden_T", [P, N8, P])
        st4, mv4, std4, r4 = sb("st4", [P, E0, 6]), sb("mv4", [P, E0, 2]), sb("std4", [P, E0]), sb("rstd4", [P, E0])
        acc, y, so, mo, stdo, ro = (sb("mixed", [P, P]), sb("mixed_n", [P, P]), sb("sto", [P, 6]), sb("mvo", [P, 2]),
                                    sb("stdo", [P, 1]), sb("rstdo", [P, 1]))
        tp, hp, zp, op = psum("turn_bank", [P, 512]), psum("hidden_p", [P, 2, 512]), psum("z_turned", [P, 2, 512]), psum("out_p", [P, 512])
        x_ready, x_turned, xT_ready, hid_done, var_ready, std_ready = (
            sem(n) for n in ("x_ready", "x_turned", "xT_ready", "hid_done", "var_ready", "std_ready"))
        z_ready, z_turned, a_ready, out_done, steps = (sem(n) for n in ("z_ready", "z_turned", "a_ready", "out_done", "tile_steps"))
        mixed, ovar_ready, ostd_ready, msteps, x_added = (sem(n) for n in ("mixed", "ovar_ready", "ostd_ready", "mix_steps", "x_added"))
        with nc.Block() as block:
            @block.vector
            def _(dve):
                def norm_in(i):
                    dve.wait_ge(x_turned, i)
                    dve.tensor_scalar(xq[:, :], k.xs[:, tile(i)], k.mv[:, bass.ds(2 * i, 1)], rstd[:, bass.ds(i, 1)],
                                      ALU.subtract, ALU.mult).then_inc(x_ready, 1)

                def norm_hidden(i):
                    order = Order(dve, steps, 3, i)
                    dve.wait_ge(hid_done, i + 1)
                    for e in range(E0):
                        ins = dve.bn_stats(st4[:, e, :], hp[:, e // 2, e % 2 * H0:(e % 2 + 1) * H0])
                    order(ins)
                    settle(dve, k)
                    for e in range(E0):
                        ins = dve.bn_aggr(mv4[:, e, :], st4[:, e, :])
                    order(ins)
                    dve.sem_inc(var_ready, 1)
                    dve.wait_ge(std_ready, i + 1)
                    order(dve.reciprocal(r4[:, :], std4[:, :]))
                    order.end()
                    dve.wait_ge(z_turned, i)
                    for e in range(E0):
                        ins = dve.tensor_scalar(z[:, e, :], hp[:, e // 2, e % 2 * H0:(e % 2 + 1) * H0], mv4[:, e, 0:1],
                                                r4[:, e:e + 1], ALU.subtract, ALU.mult)
                    ins.then_inc(z_ready, 1)

                def mix(i):
                    order = Order(dve, msteps, 9, i)
                    dve.wait_ge(out_done, i + 1)
                    order(dve.tensor_scalar(acc[:, :], op[:, 0:P], comb_of(i, 0), None, ALU.mult))
                    for e in range(1, E0):
                        order(dve.scalar_tensor_tensor(acc[:, :], op[:, e * P:(e + 1) * P], comb_of(i, e), acc[:, :], ALU.mult, ALU.add))
                    dve.sem_inc(mixed, 1)
                    order(dve.bn_stats(so[:, :], acc[:, :]))
                    settle(dve, k)
                    order(dve.bn_aggr(mo[:, :], so[:, :]))
                    dve.sem_inc(ovar_ready, 1)
                    dve.wait_ge(ostd_ready, i + 1)
                    order(dve.reciprocal(ro[:, :], stdo[:, :]))
                    order(dve.tensor_scalar(y[:, :], acc[:, :], mo[:, 0:1], ro[:, :], ALU.subtract, ALU.mult))
                    order(dve.tensor_tensor(y[:, :], y[:, :], k.row("on_g"), ALU.mult))
                    order.end()
                    dve.tensor_tensor(y[:, :], y[:, :], k.row("on_b"), ALU.add).then_inc(x_added, 1)
                    dve.wait_ge(x_added, 2 * i + 1)
                    dve.tensor_tensor(k.xs[:, tile(i)], k.xs[:, tile(i)], y[:, :], ALU.add).then_inc(x_added, 1)
                    dve.wait_ge(x_added, 2 * i + 2)
                    dve.bn_stats(k.st[:, bass.ds(6 * i, 6)], k.xs[:, tile(i)])

                def comb_of(i, e):
                    return comb[:, :, :].rearrange("p t e -> p (t e)")[:, bass.ds(E0 * i + e, 1)]

                norm_in(0)
                norm_in(1)
                norm_hidden(0)
                with dve.Fori(1, NT - 1) as i:
                    norm_in(i + 1)
                    norm_hidden(i)
                    mix(i - 1)
                norm_hidden(NT - 1)
                mix(NT - 2)
                mix(NT - 1)

            @block.scalar
            def _(act):
                def front(i):
                    act.wait_ge(x_turned, i + 1)
                    act.wait_ge(hid_done, i)
                    act.activation(hT[:, :], tp[:, 0:P], ACT.Copy).then_inc(xT_ready, 1)

                def std(i):
                    act.wait_ge(var_ready, i + 1)
                    act.activation(std4[:, :], mv4[:, :, 1], ACT.Sqrt, bias=k.eps[:, :]).then_inc(std_ready, 1)

                def gains(i):
                    act.wait_ge(out_done, i)
                    for n in range(N8):
                        if n % 4 == 0:
                            act.wait_ge(z_turned, i + 1)
                        ins = act.activation(aT[:, n, :], zp[:, n // 4, n % 4 * P:(n % 4 + 1) * P], ACT.Relu,
                                             bias=k.c["lnb"][:, n:n + 1], scale=k.c["lng"][:, n:n + 1])
                    ins.then_inc(a_ready, 1)

                def ostd(i):
                    act.wait_ge(ovar_ready, i + 1)
                    act.activation(stdo[:, :], mo[:, 1:2], ACT.Sqrt, bias=k.eps[:, :]).then_inc(ostd_ready, 1)

                front(0)
                front(1)
                std(0)
                with act.Fori(1, NT - 1) as i:
                    gains(i - 1)
                    front(i + 1)
                    std(i)
                    ostd(i - 1)
                gains(NT - 2)
                std(NT - 1)
                gains(NT - 1)
                ostd(NT - 2)
                ostd(NT - 1)

            @block.tensor
            def _(pe):
                def front(i):
                    pe.wait_ge(x_ready, i + 1)
                    pe.wait_ge(xT_ready, i)
                    pe.transpose(tp[:, 0:P], xq[:, :], k.c["ident"]).then_inc(x_turned, 1)

                def hidden(i):
                    pe.wait_ge(xT_ready, i + 1)
                    pe.wait_ge(z_ready, i)
                    for h in range(2):
                        mm = pe.matmul(hp[:, h, :], hT[:, :], k.c["w1"][:, h * 512:(h + 1) * 512], start=True, stop=True)
                    mm.then_inc(hid_done, 1)

                def turn(i):
                    pe.wait_ge(z_ready, i + 1)
                    pe.wait_ge(a_ready, i)
                    zf = z[:, :, :].rearrange("p e h -> p (e h)")
                    for n in range(N8):
                        mm = pe.transpose(zp[:, n // 4, n % 4 * P:(n % 4 + 1) * P], zf[:, n * P:(n + 1) * P], k.c["ident"])
                    mm.then_inc(z_turned, 1)

                def down(i):
                    pe.wait_ge(a_ready, i + 1)
                    pe.wait_ge(mixed, i)
                    for e in range(E0):
                        for j in range(2):
                            n = 2 * e + j
                            mm = pe.matmul(op[:, e * P:(e + 1) * P], aT[:, n, :], k.c["w2"][:, n * P:(n + 1) * P],
                                           start=j == 0, stop=j == 1)
                    mm.then_inc(out_done, 1)

                front(0)
                hidden(0)
                front(1)
                turn(0)
                with pe.Fori(1, NT - 1) as i:
                    hidden(i)
                    front(i + 1)
                    down(i - 1)
                    turn(i)
                hidden(NT - 1)
                down(NT - 2)
                turn(NT - 1)
                down(NT - 1)


def feed_forward(nc, k):
    NB = FF // P
    sem = lambda name: k.sem(f"f_{name}")
    with ExitStack() as ctx:
        def sb(name, shape, dt=F32):
            return ctx.enter_context(nc.sbuf_tensor(f"f_{name}", shape, dt))

        def psum(name, shape):
            return ctx.enter_context(nc.psum_tensor(f"f_{name}", shape, F32))

        std, rstd = sb("std", [P, NT]), sb("rstd", [P, NT])
        xn, xq, xT, gT = sb("normal", [P, P]), sb("y", [P, P]), sb("yT", [P, P]), sb("innerT", [P, NB, P])
        tp, ip, op = psum("turn_bank", [P, 512]), psum("inner_p", [P, 2, 512]), psum("out_p", [P, 2, 512])
        stats, std_made, made, own = sem("stats"), sem("std_made"), sem("rstd_made"), sem("tile_steps")
        x_ready, x_turned, xT_ready, in_done, g_ready, out_done, summed = (
            sem(n) for n in ("x_ready", "x_turned", "xT_ready", "in_done", "g_ready", "out_done", "summed"))
        end_steps, var_ready, end_std = sem("end_steps"), sem("var_ready"), sem("end_std")
        stored, loaded, x_final = sem("stored"), sem("loaded"), sem("x_final")
        with nc.Block() as block:
            @block.vector
            def _(dve):
                aggregate(dve, Order(dve, stats, 1), k)
                dve.wait_ge(std_made, 1)
                dve.reciprocal(rstd[:, :], std[:, :]).then_inc(made, 1)
                dve.wait_ge(made, 1)

                def norm_in(i):
                    dve.wait_ge(x_turned, i)
                    order = Order(dve, own, 2, i)
                    order(dve.tensor_scalar(xn[:, :], k.rs[:, tile(i)], k.mv[:, bass.ds(2 * i, 1)], rstd[:, bass.ds(i, 1)],
                                            ALU.subtract, ALU.mult))
                    order(dve.tensor_tensor(xn[:, :], xn[:, :], k.row("so_g"), ALU.mult))
                    order.end()
                    dve.tensor_tensor(k.res[:, tile(i)], xn[:, :], k.row("so_be"), ALU.add)
                    dve.tensor_tensor(xq[:, :], xn[:, :], k.row("so_be"), ALU.add).then_inc(x_ready, 1)

                def add_out(i, j):
                    dve.wait_ge(out_done, i + 1)
                    dve.tensor_tensor(k.rs[:, tile(i)], op[:, j, 0:P], k.res[:, tile(i)], ALU.add).then_inc(summed, 1)
                    dve.wait_ge(summed, i + 1)
                    dve.bn_stats(k.st[:, bass.ds(6 * i, 6)], k.rs[:, tile(i)])

                norm_in(0)
                norm_in(1)
                with dve.Fori(0, NT // 2 - 1) as m:
                    for j in range(2):
                        add_out(2 * m + j, j)
                        norm_in(2 * m + j + 2)
                for j in range(2):
                    add_out(NT - 2 + j, j)

            @block.scalar
            def _(act):
                act.wait_ge(stats, 1)
                act.activation(std[:, :], variances(k), ACT.Sqrt, bias=k.eps[:, :]).then_inc(std_made, 1)

                def turned(i):
                    act.wait_ge(x_turned, i + 1)
                    act.wait_ge(in_done, i)
                    act.activation(xT[:, :], tp[:, 0:P], ACT.Copy).then_inc(xT_ready, 1)

                def inner(i, j):
                    act.wait_ge(out_done, i)
                    for n in range(NB):
                        if n == 0:
                            act.wait_ge(in_done, i + 1)
                        ins = act.activation(gT[:, n, :], ip[:, j, n * P:(n + 1) * P], ACT.Gelu, bias=k.c["fi_b"][:, n:n + 1])
                    ins.then_inc(g_ready, 1)

                turned(0)
                with act.Fori(0, NT // 2 - 1) as m:
                    for j in range(2):
                        turned(2 * m + j + 1)
                        inner(2 * m + j, j)
                turned(NT - 1)
                inner(NT - 2, 0)
                inner(NT - 1, 1)

            @block.tensor
            def _(pe):
                def front(i, j):
                    pe.wait_ge(x_ready, i + 1)
                    pe.wait_ge(xT_ready, i)
                    pe.transpose(tp[:, 0:P], xq[:, :], k.c["ident"]).then_inc(x_turned, 1)
                    pe.wait_ge(xT_ready, i + 1)
                    for n in range(NB):
                        mm = pe.matmul(ip[:, j, n * P:(n + 1) * P], k.c["fi"][:, n * P:(n + 1) * P], xT[:, :], start=True, stop=True)
                    mm.then_inc(in_done, 1)

                def down(i, j):
                    pe.wait_ge(g_ready, i + 1)
                    pe.matmul(op[:, j, 0:P], k.ones[0:1, :], k.row("fo_b")[0:1, :], start=True, stop=False)
                    for n in range(NB):
                        mm = pe.matmul(op[:, j, 0:P], gT[:, n, :], k.c["fo"][:, n * P:(n + 1) * P], start=False, stop=n == NB - 1)
                    mm.then_inc(out_done, 1)

                front(0, 0)
                front(1, 1)
                with pe.Fori(0, NT // 2 - 1) as m:
                    for j in range(2):
                        i = 2 * m + j
                        pe.wait_ge(summed, i)
                        down(i, j)
                        front(i + 2, j)
                pe.wait_ge(summed, NT - 2)
                down(NT - 2, 0)
                down(NT - 1, 1)

        with nc.Block() as block:
            all3 = lambda ap: ap[:, :].rearrange("p (t d) -> p t d", d=P)
            rows3 = lambda name: k.row(name).unsqueeze(1).to_broadcast([P, NT, P])

            @block.vector
            def _(dve):
                order = Order(dve, end_steps, 4)
                aggregate(dve, order, k)
                dve.sem_inc(var_ready, 1)
                dve.wait_ge(end_std, 1)
                order(dve.reciprocal(rstd[:, :], std[:, :]))
                for t in range(NT):
                    ins = dve.tensor_scalar(k.rs[:, t * P:(t + 1) * P], k.rs[:, t * P:(t + 1) * P], k.mv[:, 2 * t:2 * t + 1],
                                            rstd[:, t:t + 1], ALU.subtract, ALU.mult)
                order(ins)
                order(dve.tensor_tensor(all3(k.rs), all3(k.rs), rows3("fo_g"), ALU.mult))
                order.end()
                dve.tensor_tensor(all3(k.rs), all3(k.rs), rows3("fo_be"), ALU.add).then_inc(x_final, 1)
                dve.wait_ge(x_final, 1)
                dve.tensor_tensor(k.xs[:, :], k.xs[:, :], k.rs[:, :], ALU.add).then_inc(x_final, 1)

            @block.scalar
            def _(act):
                act.wait_ge(var_ready, 1)
                act.activation(std[:, :], variances(k), ACT.Sqrt, bias=k.eps[:, :]).then_inc(end_std, 1)

            @block.sync
            def _(sp):
                sp.wait_ge(x_final, 2)
                sp.dma_start(k.turn_dram.rearrange("(t b) s d -> (b s) t d", b=2), all3(k.xs)).then_inc(stored, 16)
                sp.wait_ge(stored, 16)
                load_turned(sp, k, k.turn_dram, loaded)
                sp.wait_ge(loaded, 64)


def load_turned(sp, k, src, loaded):
    for q in range(4):
        sp.dma_start(k.xe[32 * q:32 * q + 32, :].rearrange("p (g d) -> p g d", d=P),
                     src.rearrange("t (g q) d -> q t g d", q=4)[q]).then_inc(loaded, 16)


def memory_stage(nc, k):
    HD = NHM * DM
    NP2 = NHM // 2
    SCALE = 1.0 / np.sqrt(DM)
    sem = lambda name: k.sem(f"m_{name}")
    with ExitStack() as ctx:
        def sb(name, shape, dt=F32):
            return ctx.enter_context(nc.sbuf_tensor(f"m_{name}", shape, dt))

        std, rstd = sb("std", [P, NT]), sb("rstd", [P, NT])
        xq, hT = sb("h", [P, P]), sb("hT", [P, P])
        ex = sb("exp", [P, 2, 512])
        kq = sb("features", [P, NP2, 2, P])
        bs = sb("beta_sums", [P, 3 * NHM])
        eb, cc, sh = sb("exp_beta", [P, NHM]), sb("sigma_sums", [P, NHM]), sb("sums_kept", [P, 1])
        c = sb("c", [P, 2, NHM])
        clow = sb("c_low", [P, 2, NHM])
        rq = sb("q_scale", [P, 2, NHM])
        R = sb("rhs", [P, 2, NHM, DM])
        gm = sb("products", [P, 2, NHM, 2, P])
        X, Ym, cX, T = (sb(n, [P, NHM, 32]) for n in ("inverse", "masked", "c_inverse", "inverse_T"))
        Tb = sb("inverse_T_blocks", [P, NHM, P])
        U0, V, U, on = (sb(n, [P, NHM, DM]) for n in ("u0", "v", "u", "out_rows"))
        oT = sb("outT", [P, NP2, P])
        F = ctx.enter_context(nc.psum_tensor("m_front", [P, 3, 512], F32))
        C = ctx.enter_context(nc.psum_tensor("m_chain", [P, 5, 512], F32))
        h32 = lambda ap: ap.rearrange("p (h n) -> p h n", n=32)
        h64 = lambda a: C[:, a:a + 2, :].rearrange("p b (h n) -> p (b h) n", n=DM)
        bc = lambda v, n: v.unsqueeze(2).to_broadcast([P, NHM, n])
        lvl = lambda j: k.c[f"lvl{j}"].unsqueeze(1).to_broadcast([P, NHM, 32])
        eye = k.c["eye32"].unsqueeze(1).to_broadcast([P, NHM, 32])
        masks = k.pack["cst"][:, 200:200 + 2 * P].rearrange("p (g t) -> p g t", g=2)
        assert [n for n, _ in PACKS["cst"]][3:5] == ["bd_strict", "bd_upper"] and width(PACKS["cst"][:3]) == 200

        stats, std_made, made, cleared = sem("stats"), sem("std_made"), sem("rstd_made"), sem("cleared")
        x_ready, x_turned, hT_ready = sem("x_ready"), sem("x_turned"), sem("hT_ready")
        qk_done, ex_ready, clipped, kq_ready = sem("qk_done"), sem("ex_ready"), sem("clipped"), sem("kq_ready")
        v_done, sum_done, bs_ready, eb_ready, small, rhs_ready = (
            sem(n) for n in ("v_done", "sum_done", "bs_ready", "eb_ready", "small_steps", "rhs_ready"))
        ga_done, gm_ready, c_ready = sem("ga_done"), sem("gm_ready"), sem("c_ready")
        cx_ready, y_done, ysteps, ym_ready, z_done, X_ready, T_ready, Tb_ready = (
            sem(n) for n in ("cx_ready", "y_done", "y_steps", "ym_ready", "z_done", "X_ready", "T_ready", "Tb_ready"))
        u0_done, u0_ready, v1_ready, gy_done, v2_ready, xy_done, u_ready, cu_ready = (
            sem(n) for n in ("u0_done", "u0_ready", "v1_ready", "gy_done", "v2_ready", "xy_done", "u_ready", "cu_ready"))
        o_done, on_ready, oT_done, oT_ready, p_done, summed = (
            sem(n) for n in ("o_done", "on_ready", "oT_done", "oT_ready", "p_done", "summed"))

        CHAIN = ["y0", "y1", "z1", "y2", "z2", "y3", "z3", "u0", "gy", "xy", "o", "oT", "proj"]
        FRONT = ["x", "qk0", "qk1", "qk2", "qk3", "v", "sum", "ga0", "ga1", "ga2", "ga3"]
        BOTH = [s for pair in zip(CHAIN, ["x", "qk0", "qk1", "qk2", "qk3", "v", "sum", "ga0", "ga1", "ga2", "ga3", "", ""])
                for s in pair if s]

        def schedule(eng, steps):
            def run(names, i, j):
                for name in names:
                    if name in steps:
                        if name in CHAIN:
                            steps[name](i, j)
                        else:
                            steps[name](i + 1, 1 - j)

            run(FRONT, -1, 1)
            with eng.Fori(0, NT // 2 - 1) as m:
                run(BOTH, 2 * m, 0)
                run(BOTH, 2 * m + 1, 1)
            run(BOTH, NT - 2, 0)
            run(CHAIN, NT - 1, 1)

        block = ctx.enter_context(nc.Block())

        @block.tensor
        def _(pe):
            def x(i, j):
                pe.wait_ge(x_ready, i + 1)
                pe.wait_ge(bs_ready, i)
                pe.transpose(F[:, 2, 0:P], xq[:, :], k.c["ident"]).then_inc(x_turned, 1)

            def qk(g):
                def step(i, j):
                    if g == 0:
                        pe.wait_ge(hT_ready, i + 1)
                        pe.wait_ge(gm_ready, 8 * i)
                    if g >= 2:
                        pe.wait_ge(kq_ready, 4 * i + g - 1)
                    w = k.c["mk"] if g % 2 == 0 else k.c["mq"]
                    for a in range(4):
                        n = 4 * (g // 2) + a
                        mm = pe.matmul(F[:, g % 2, a * P:(a + 1) * P], w[:, n * P:(n + 1) * P], hT[:, :], start=True, stop=True)
                    mm.then_inc(qk_done, 1)
                return step

            def v(i, j):
                pe.wait_ge(kq_ready, 4 * i + 4)
                for h in range(2):
                    pe.matmul(F[:, h, :], hT[:, :], k.c["mv"][:, h * 512:(h + 1) * 512], start=True, stop=True)
                pe.matmul(F[:, 2, P:P + NHM], hT[:, :], k.c["mbeta"], start=True, stop=True).then_inc(v_done, 1)

            def sums(i, j):
                for w in range(2):
                    for a in range(NP2):
                        at = P + NHM * (w + 1) + 2 * a
                        mm = pe.matmul(F[:, 2, at:at + 2], kq[:, a, w, :], k.c["ind2"], start=True, stop=True)
                mm.then_inc(sum_done, 1)

            def ga(r):
                def step(i, j):
                    if r == 0:
                        pe.wait_ge(rhs_ready, i + 1)
                    else:
                        pe.wait_ge(gm_ready, 8 * i + 2 * r)
                    for h in range(2):
                        for a in range(2):
                            rows = slice(DM * h, DM * (h + 1))
                            mm = pe.matmul(F[:, h, a * 2 * P:(a + 1) * 2 * P], kq[rows, 2 * r + a, 0, :],
                                           kq[rows, 2 * r + a, :, :].rearrange("p w t -> p (w t)"), start=True, stop=True)
                        mm.then_inc(ga_done, 1)
                return step

            def y(l):
                def step(i, j):
                    pe.wait_ge(cx_ready, 4 * i + l + 1)
                    if l == 0:
                        pe.wait_ge(gm_ready, 8 * i + 8)
                        pe.wait_ge(on_ready, i)
                    for h in range(NHM):
                        mm = pe.matmul(C[:, 0, 32 * h:32 * h + 32], gm[:, j, h, 0, :], cX[:, h, :], start=True, stop=True)
                    mm.then_inc(y_done, 1)
                return step

            def z(l):
                def step(i, j):
                    pe.wait_ge(ym_ready, 3 * i + l)
                    pe.wait_ge(Tb_ready, 4 * i + l)
                    for h in range(NHM):
                        mm = pe.matmul(C[:, 1, 32 * h:32 * h + 32], Tb[:, h, :], Ym[:, h, :], start=True, stop=True)
                    mm.then_inc(z_done, 1)
                return step

            def apply(at, left, right, done):
                for h in range(NHM):
                    mm = pe.matmul(C[:, at + h // 8, h % 8 * DM:(h % 8 + 1) * DM], left(h), right[:, h, :], start=True, stop=True)
                mm.then_inc(done, 1)

            def u0(i, j):
                pe.wait_ge(Tb_ready, 4 * i + 4)
                pe.wait_ge(oT_ready, i)
                apply(2, lambda h: Tb[:, h, :], R[:, j, :, :], u0_done)

            def gy(i, j):
                pe.wait_ge(v1_ready, i + 1)
                pe.wait_ge(X_ready, 4 * i + 4)
                apply(0, lambda h: gm[:, j, h, 0, :], V, gy_done)

            def xy(i, j):
                pe.wait_ge(v2_ready, i + 1)
                pe.wait_ge(u0_ready, i + 1)
                apply(2, lambda h: Tb[:, h, :], V, xy_done)

            def o(i, j):
                pe.wait_ge(cu_ready, i + 1)
                apply(0, lambda h: gm[:, j, h, 1, :], V, o_done)

            def oT_(i, j):
                pe.wait_ge(on_ready, i + 1)
                pe.wait_ge(u_ready, i + 1)
                of = on[:, :, :].rearrange("p h n -> p (h n)")
                for a in range(NP2):
                    mm = pe.transpose(C[:, 2 + a // 4, a % 4 * P:(a % 4 + 1) * P], of[:, a * P:(a + 1) * P], k.c["ident"])
                mm.then_inc(oT_done, 1)

            def proj(i, j):
                pe.wait_ge(oT_ready, i + 1)
                pe.wait_ge(summed, i)
                for a in range(NP2):
                    mm = pe.matmul(C[:, 4, 0:P], oT[:, a, :], k.c["mo"][:, a * P:(a + 1) * P], start=a == 0, stop=a == NP2 - 1)
                mm.then_inc(p_done, 1)

            schedule(pe, {"x": x, "v": v, "sum": sums, "u0": u0, "gy": gy, "xy": xy, "o": o, "oT": oT_, "proj": proj,
                          **{f"qk{g}": qk(g) for g in range(4)}, **{f"ga{r}": ga(r) for r in range(4)},
                          **{f"y{l}": y(l) for l in range(4)}, **{f"z{l}": z(l) for l in range(1, 4)}})

        @block.scalar
        def _(act):
            act.wait_ge(stats, 1)
            act.activation(std[:, :], variances(k), ACT.Sqrt, bias=k.eps[:, :]).then_inc(std_made, 1)
            act.wait_ge(cleared, 1)

            def x(i, j):
                act.wait_ge(x_turned, i + 1)
                act.wait_ge(v_done, i)
                act.activation(hT[:, :], F[:, 2, 0:P], ACT.Copy).then_inc(hT_ready, 1)

            def qk(g):
                def step(i, j):
                    act.wait_ge(qk_done, 4 * i + g + 1)
                    if g >= 2:
                        act.wait_ge(kq_ready, 4 * i + g - 1)
                    else:
                        act.wait_ge(kq_ready, 4 * i)
                    act.activation(ex[:, g % 2, :], F[:, g % 2, :], ACT.Exp).then_inc(ex_ready, 1)
                return step

            def sums(i, j):
                act.wait_ge(bs_ready, i + 1)
                act.wait_ge(c_ready, i)
                act.activation(eb[:, :], bs[:, 0:NHM], ACT.Exp, scale=-1.0).then_inc(eb_ready, 1)

            def spread(n):
                def step(i, j):
                    act.wait_ge(T_ready, 4 * i + n)
                    if n == 1:
                        act.wait_ge(xy_done, i)
                    else:
                        act.wait_ge(z_done, 3 * i + n - 1)
                    for q in range(4):
                        r = slice(32 * q, 32 * q + 32)
                        ins = act.activation(Tb[r, :, r], T[r, :, :], ACT.Copy)
                    ins.then_inc(Tb_ready, 1)
                return step

            def u0(i, j):
                pass

            def gy(i, j):
                act.wait_ge(gy_done, i + 1)
                act.activation(V[:, :, :], h64(0), ACT.Copy, scale=k.c["rowhigh"]).then_inc(v2_ready, 1)

            def oT_(i, j):
                act.wait_ge(oT_done, i + 1)
                act.wait_ge(p_done, i)
                act.activation(oT[:, :, :], C[:, 2:4, :].rearrange("p b (a t) -> p (b a) t", t=P), ACT.Copy).then_inc(oT_ready, 1)

            schedule(act, {"x": x, "sum": sums, "gy": gy, "oT": oT_, "y0": spread(1), "z1": spread(2), "z2": spread(3),
                           "z3": spread(4), **{f"qk{g}": qk(g) for g in range(4)}})

        @block.gpsimd
        def _(pool):
            pool.memset(Tb[:, :, :], 0.0).then_inc(cleared, 1)

            def cx(l):
                def step(i, j):
                    if l == 0:
                        pool.wait_ge(c_ready, i + 1)
                    else:
                        pool.wait_ge(X_ready, 4 * i + l)
                    if l == 0:
                        pool.wait_ge(y_done, 4 * i)
                    else:
                        pool.wait_ge(y_done, 4 * i + l)
                    pool.tensor_tensor(cX[:, :, :], eye if l == 0 else X[:, :, :], bc(c[:, j, :], 32), ALU.mult).then_inc(cx_ready, 1)
                return step

            def u0(i, j):
                pool.wait_ge(u0_ready, i + 1)
                pool.wait_ge(o_done, i)
                pool.tensor_tensor(V[:, :, :], U0[:, :, :], bc(clow[:, j, :], DM), ALU.mult).then_inc(v1_ready, 1)

            def xy(i, j):
                pool.wait_ge(u_ready, i + 1)
                pool.tensor_tensor(V[:, :, :], U[:, :, :], bc(c[:, j, :], DM), ALU.mult).then_inc(cu_ready, 1)

            schedule(pool, {"u0": u0, "xy": xy, **{f"y{l}": cx(l) for l in range(4)}})

        @block.vector
        def _(dve):
            row_stats(dve, Order(dve, stats0 := sem("stats0"), 2), k, k.xe)
            dve.sem_inc(stats, 1)
            dve.wait_ge(std_made, 1)
            dve.reciprocal(rstd[:, :], std[:, :]).then_inc(made, 1)
            dve.wait_ge(made, 1)

            def x(i, j):
                dve.wait_ge(x_turned, i)
                for out in (k.rs[:, tile(i)], xq[:, :]):
                    ins = dve.tensor_scalar(out, k.xe[:, tile(i)], k.mv[:, bass.ds(2 * i, 1)], rstd[:, bass.ds(i, 1)],
                                            ALU.subtract, ALU.mult)
                ins.then_inc(x_ready, 1)

            def qk(g):
                def step(i, j):
                    dve.wait_ge(ex_ready, 4 * i + g + 1)
                    dve.tensor_scalar(ex[:, g % 2, :], ex[:, g % 2, :], 1.0, None, ALU.min).then_inc(clipped, 1)
                    dve.wait_ge(clipped, 4 * i + g + 1)
                    dve.wait_ge(ga_done, 8 * i)
                    n = 4 * (g // 2)
                    dve.scalar_tensor_tensor(kq[:, n:n + 4, g % 2, :], F[:, g % 2, :].rearrange("p (a t) -> p a t", t=P), 0.0,
                                             ex[:, g % 2, :].rearrange("p (a t) -> p a t", t=P), ALU.max, ALU.add).then_inc(kq_ready, 1)
                return step

            def sums(i, j):
                dve.wait_ge(sum_done, i + 1)
                dve.wait_ge(eb_ready, i)
                dve.tensor_copy(bs[:, :], F[:, 2, P:P + 3 * NHM]).then_inc(bs_ready, 1)
                dve.wait_ge(bs_ready, i + 1)
                sk, sq = bs[:, NHM:2 * NHM], bs[:, 2 * NHM:]
                dve.tensor_tensor(R[:, j, :, :], F[:, 0:2, :].rearrange("p b (h n) -> p (b h) n", n=DM), bc(sk, DM),
                                  ALU.mult).then_inc(rhs_ready, 1)
                order = Order(dve, small, 6, i)
                order(dve.reciprocal(rq[:, j, :], sq))
                order(dve.tensor_scalar(rq[:, j, :], rq[:, j, :], float(SCALE), None, ALU.mult))
                dve.wait_ge(eb_ready, i + 1)
                order(dve.tensor_scalar(cc[:, :], eb[:, :], 1.0, None, ALU.add))
                order(dve.tensor_tensor(cc[:, :], cc[:, :], sk, ALU.mult))
                order(dve.tensor_tensor(cc[:, :], cc[:, :], sk, ALU.mult))
                order(dve.reciprocal(c[:, j, :], cc[:, :]))
                order.end()
                dve.tensor_scalar(clow[:, j, :], c[:, j, :], k.c["rowlow"], None, ALU.mult).then_inc(c_ready, 1)

            def ga(r):
                def step(i, j):
                    for h in range(2):
                        dve.wait_ge(ga_done, 8 * i + 2 * r + h + 1)
                        out = gm[:, j, 4 * r + h:4 * r + 4:2, :, :]
                        dve.tensor_tensor(out, F[:, h, :].rearrange("p (a g t) -> p a g t", a=2, g=2),
                                          masks.unsqueeze(1).to_broadcast([P, 2, 2, P]), ALU.mult).then_inc(gm_ready, 1)
                return step

            def y(l):
                def step(i, j):
                    dve.wait_ge(y_done, 4 * i + l + 1)
                    if l:
                        dve.wait_ge(z_done, 3 * i + l - 1)
                        dve.tensor_tensor(Ym[:, :, :], h32(C[:, 0, :]), lvl(l), ALU.mult).then_inc(ym_ready, 1)
                    else:
                        dve.tensor_tensor(Ym[:, :, :], h32(C[:, 0, :]), lvl(0), ALU.mult).then_inc(ysteps, 1)
                        dve.wait_ge(ysteps, i + 1)
                        dve.tensor_tensor(X[:, :, :], eye, Ym[:, :, :], ALU.subtract).then_inc(X_ready, 1)
                        turn(1, i)
                return step

            def turn(n, i):
                dve.wait_ge(X_ready, 4 * i + n)
                dve.wait_ge(Tb_ready, 4 * i + n - 1)
                dve.transpose(T[:, :, :], X[:, :, :]).then_inc(T_ready, 1)

            def z(l):
                def step(i, j):
                    dve.wait_ge(z_done, 3 * i + l)
                    dve.wait_ge(cx_ready, 4 * i + l + 1)
                    dve.tensor_tensor(X[:, :, :], X[:, :, :], h32(C[:, 1, :]), ALU.subtract).then_inc(X_ready, 1)
                    turn(l + 1, i)
                return step

            def u0(i, j):
                dve.wait_ge(u0_done, i + 1)
                dve.tensor_copy(U0[:, :, :], h64(2)).then_inc(u0_ready, 1)

            def xy(i, j):
                dve.wait_ge(xy_done, i + 1)
                dve.tensor_tensor(U[:, :, :], U0[:, :, :], h64(2), ALU.subtract).then_inc(u_ready, 1)

            def o(i, j):
                dve.wait_ge(o_done, i + 1)
                dve.tensor_tensor(on[:, :, :], h64(0), bc(rq[:, j, :], DM), ALU.mult).then_inc(on_ready, 1)

            def proj(i, j):
                dve.wait_ge(p_done, i + 1)
                dve.tensor_tensor(k.rs[:, tile(i)], C[:, 4, 0:P], k.rs[:, tile(i)], ALU.add).then_inc(summed, 1)
                dve.wait_ge(summed, i + 1)
                dve.bn_stats(k.st[:, bass.ds(6 * i, 6)], k.rs[:, tile(i)])

            schedule(dve, {"x": x, "sum": sums, "u0": u0, "xy": xy, "o": o, "proj": proj,
                           **{f"qk{g}": qk(g) for g in range(4)}, **{f"ga{r}": ga(r) for r in range(4)},
                           **{f"y{l}": y(l) for l in range(4)}, **{f"z{l}": z(l) for l in range(1, 4)}})

    memory_end(nc, k)


def memory_end(nc, k):
    sem = lambda name: k.sem(f"n_{name}")
    with nc.sbuf_tensor("n_std", [P, NT], F32) as std, nc.sbuf_tensor("n_rstd", [P, NT], F32) as rstd:
        steps, var_ready, std_made = sem("steps"), sem("var_ready"), sem("std_made")
        all3 = lambda ap: ap[:, :].rearrange("p (t d) -> p t d", d=P)
        rows3 = lambda name: k.row(name).unsqueeze(1).to_broadcast([P, NT, P])
        with nc.Block() as block:
            @block.vector
            def _(dve):
                order = Order(dve, steps, 5)
                aggregate(dve, order, k)
                dve.sem_inc(var_ready, 1)
                dve.wait_ge(std_made, 1)
                order(dve.reciprocal(rstd[:, :], std[:, :]))
                for t in range(NT):
                    ins = dve.tensor_scalar(k.rs[:, t * P:(t + 1) * P], k.rs[:, t * P:(t + 1) * P], k.mv[:, 2 * t:2 * t + 1],
                                            rstd[:, t:t + 1], ALU.subtract, ALU.mult)
                order(ins)
                order(dve.tensor_tensor(all3(k.rs), all3(k.rs), rows3("m_g"), ALU.mult))
                order(dve.tensor_tensor(all3(k.rs), all3(k.rs), rows3("m_b"), ALU.add))
                order.end()
                dve.tensor_tensor(k.xe[:, :], k.xe[:, :], k.rs[:, :], ALU.add)

            @block.scalar
            def _(act):
                act.wait_ge(var_ready, 1)
                act.activation(std[:, :], variances(k), ACT.Sqrt, bias=k.eps[:, :]).then_inc(std_made, 1)


def shared_experts_stage(nc, k):
    NA = E1 + 1
    sem = lambda name: k.sem(f"s_{name}")
    with ExitStack() as ctx:
        def sb(name, shape, dt=F32):
            return ctx.enter_context(nc.sbuf_tensor(f"s_{name}", shape, dt))

        xT = sb("xT", [P, B * S])
        comb = sb("weights", [P, NT, NE])
        acc = k.xs
        with ExitStack() as inner:
            def isb(name, shape):
                return inner.enter_context(nc.sbuf_tensor(f"s_{name}", shape, F32))

            lg, score, picked = isb("logits", [P, NT, E1]), isb("scores", [P, NT, E1 + 5]), isb("picked", [P, NT, E1 + 5])
            values, red, b2, combT = isb("values", [P, NT, 8]), isb("reduced", [P, 3, NT]), isb("b2", [NA, P]), isb("weightsT", [NA, NT, P])
            std, rstd = isb("std", [P, NT]), isb("rstd", [P, NT])
            varied, std_made, norm_steps, xn_ready = (sem(n) for n in ("varied", "std_made", "norm_steps", "xn_ready"))
            turned = inner.enter_context(nc.psum_tensor("s_turned_p", [P, 4, 512], F32))
            lp = inner.enter_context(nc.psum_tensor("s_logit_p", [P, 512], F32))
            filled, steps, turned_s, xT_ready, logit_done, shifted, exp_ready, b2_loaded = (
                sem(n) for n in ("filled", "router_steps", "rows_turned", "xT_ready", "logit_done", "shifted", "exp_ready", "b2_loaded"))
            comb_ready, combT_done, combT_ready, bias_done, acc_ready = (
                sem(n) for n in ("comb_ready", "combT_done", "combT_ready", "bias_done", "acc_ready"))
            with nc.Block() as block:
                @block.sync
                def _(sp):
                    sp.dma_start(b2[:, :], k.dram["b2"]).then_inc(b2_loaded, 16)

                @block.gpsimd
                def _(pool):
                    pool.memset(score[:, :, :], -1.0).then_inc(filled, 1)
                    pool.memset(comb[:, :, :], 1.0).then_inc(filled, 1)

                @block.scalar
                def _(act):
                    act.wait_ge(varied, 2)
                    act.activation(std[:, :], variances(k), ACT.Sqrt, bias=k.eps[:, :]).then_inc(std_made, 1)
                    for c in range(4):
                        act.wait_ge(turned_s, c + 1)
                        act.activation(xT[:, c * 512:(c + 1) * 512], turned[:, c, :], ACT.Copy).then_inc(xT_ready, 1)
                    act.wait_ge(shifted, 1)
                    act.activation(lg[:, :, :], lg[:, :, :], ACT.Exp).then_inc(exp_ready, 1)
                    for c in range(4):
                        act.wait_ge(combT_done, c + 1)
                        act.activation(combT[:, 4 * c:4 * c + 4, :], turned[0:NA, c, :].rearrange("p (t n) -> p t n", n=P),
                                       ACT.Copy).then_inc(combT_ready, 1)

                @block.tensor
                def _(pe):
                    for t in range(NT):
                        if t % 4 == 0:
                            pe.wait_ge(xn_ready, t // 4 + 1)
                        mm = pe.transpose(turned[:, t // 4, t % 4 * P:(t % 4 + 1) * P], k.rs[:, t * P:(t + 1) * P], k.c["ident"])
                        if t % 4 == 3:
                            mm.then_inc(turned_s, 1)
                    for t in range(NT):
                        if t % 4 == 0:
                            pe.wait_ge(xT_ready, t // 4 + 1)
                        mm = pe.matmul(lp[:, t * E1:(t + 1) * E1], xT[:, t * P:(t + 1) * P], k.c["gate"], start=True, stop=True)
                    mm.then_inc(logit_done, 1)
                    pe.wait_ge(comb_ready, 1)
                    for t in range(NT):
                        mm = pe.matmul(turned[0:NA, t // 4, t % 4 * P:(t % 4 + 1) * P], comb[:, t, 0:NA], k.c["ident"], start=True, stop=True)
                        if t % 4 == 3:
                            mm.then_inc(combT_done, 1)
                    pe.wait_ge(b2_loaded, 16)
                    for t in range(NT):
                        if t % 4 == 0:
                            pe.wait_ge(combT_ready, t // 4 + 1)
                        mm = pe.matmul(turned[:, t // 4, t % 4 * P:(t % 4 + 1) * P], combT[:, t, :], b2[:, :], start=True, stop=True)
                        if t % 4 == 3:
                            mm.then_inc(bias_done, 1)

                @block.vector
                def _(dve):
                    row_stats(dve, Order(dve, varied, 2), k, k.xe)
                    norm = Order(dve, norm_steps, 1)
                    dve.wait_ge(std_made, 1)
                    norm(dve.reciprocal(rstd[:, :], std[:, :]))
                    for t in range(NT):
                        ins = dve.tensor_scalar(k.rs[:, t * P:(t + 1) * P], k.xe[:, t * P:(t + 1) * P], k.mv[:, 2 * t:2 * t + 1],
                                                rstd[:, t:t + 1], ALU.subtract, ALU.mult)
                        if t % 4 == 3:
                            ins.then_inc(xn_ready, 1)
                    order = Order(dve, steps, 13)
                    dve.wait_ge(logit_done, 1)
                    l3 = lp[:, 0:NT * E1].rearrange("p (t e) -> p t e", e=E1)
                    over = lambda n: red[:, n, :].unsqueeze(2).to_broadcast([P, NT, E1])
                    order(dve.tensor_reduce(red[:, 0, :], l3, AX.X, ALU.max))
                    dve.tensor_tensor(lg[:, :, :], l3, over(0), ALU.subtract).then_inc(shifted, 1)
                    dve.wait_ge(exp_ready, 1)
                    order(dve.tensor_reduce(red[:, 1, :], lg[:, :, :], AX.X, ALU.add))
                    order(dve.reciprocal(red[:, 1, :], red[:, 1, :]))
                    dve.wait_ge(filled, 2)
                    order(dve.tensor_tensor(score[:, :, 0:E1], lg[:, :, :], over(1), ALU.mult))
                    top_experts(dve, order, filled, score, picked, values, lg[:, :, :], E1, 3, 5)
                    order(dve.tensor_reduce(red[:, 2, :], lg[:, :, :], AX.X, ALU.add))
                    order(dve.tensor_scalar(red[:, 2, :], red[:, 2, :], 1e-20, None, ALU.add))
                    order(dve.reciprocal(red[:, 2, :], red[:, 2, :]))
                    dve.tensor_tensor(comb[:, :, 0:E1], lg[:, :, :], over(2), ALU.mult).then_inc(comb_ready, 1)
                    order(dve.memset(k.unused[:, :], 0.0))
                    order.end()
                    for c in range(4):
                        dve.wait_ge(bias_done, c + 1)
                        r = slice(c * 512, (c + 1) * 512)
                        dve.tensor_tensor(acc[:, r], turned[:, c, :], k.xe[:, r], ALU.add).then_inc(acc_ready, 1)

        WX = width(EXW)
        ew, w2 = sb("expert_weights", [P, 2, WX]), sb("down_weights", [P, 2, P])
        gl, a = sb("gates", [P, 2, 512]), sb("gated", [P, 2, 512])
        up = ctx.enter_context(nc.psum_tensor("s_up", [P, 2, 2, 512], F32))
        dn = ctx.enter_context(nc.psum_tensor("s_down", [P, 2, 512], F32))
        e_loaded = [sem(f"expert_loaded{j}") for j in range(2)]
        w2_ready, up_done, g_ready, a_ready, dn_done, mixed, out_stored = (
            sem(n) for n in ("w2_ready", "up_done", "g_ready", "a_ready", "dn_done", "mixed", "out_stored"))
        w = [fields_of(ew[:, j, :], EXW) for j in range(2)]
        flat = comb[:, :, :].rearrange("p t e -> p (t e)")

        def experts(eng, step):
            with eng.Fori(0, NE // 2) as m:
                for j in range(2):
                    step(m, j, False)
            step(NE // 2, 0, True)

        with nc.Block() as block:
            @block.sync
            def _(sp):
                for e in range(2):
                    sp.dma_start(ew[:, e, :], k.dram["experts"][e]).then_inc(e_loaded[e], 16)

                def load(e, j):
                    sp.wait_ge(dn_done, 4 * e + 4)
                    sp.wait_ge(a_ready, 4 * e + 4)
                    sp.dma_start(ew[:, j, :], k.dram["experts"][bass.ds(e + 2, 1), :, :].rearrange("e p w -> p (e w)")).then_inc(e_loaded[j], 16)

                with sp.Fori(0, NE // 2 - 1) as m:
                    for j in range(2):
                        load(2 * m + j, j)
                load(NE - 3, 0)
                sp.wait_ge(mixed, 4 * NE)
                for q in range(4):
                    sp.dma_start(k.out.rearrange("t (g q) d -> q t g d", q=4)[q],
                                 acc[32 * q:32 * q + 32, :].rearrange("p (g d) -> p g d", d=P)).then_inc(out_stored, 16)
                sp.wait_ge(out_stored, 64)

            @block.gpsimd
            def _(pool):
                def step(m, j, used):
                    e = 2 * m + j
                    if used:
                        pool.wait_ge(dn_done, 4 * e - 4)
                    pool.wait_ge(e_loaded[j], 16 * (m + 1))
                    pool.tensor_tensor(w2[:, j, :], w[j]["fc2"], w[j]["mult"].to_broadcast([P, P]), ALU.mult).then_inc(w2_ready, 1)

                for j in range(2):
                    step(0, j, False)
                with pool.Fori(1, NE // 2) as m:
                    for j in range(2):
                        step(m, j, True)
                step(NE // 2, 0, True)

            @block.scalar
            def _(act):
                def step(m, j, last):
                    e = 2 * m + j
                    for c in range(4):
                        act.wait_ge(up_done, 4 * e + c + 1)
                        act.activation(gl[:, c % 2, :], up[:, c % 2, 1, :], ACT.Gelu, bias=w[j]["b1"][:, 1:2]).then_inc(g_ready, 1)

                experts(act, step)

            @block.tensor
            def _(pe):
                def project_up(m, j, c):
                    if c == 0:
                        pe.wait_ge(e_loaded[j], 16 * (m + 1))
                    for h in range(2):
                        mm = pe.matmul(up[:, c % 2, h, :], w[j]["fc1"][:, h * F1:(h + 1) * F1], xT[:, c * 512:(c + 1) * 512],
                                       start=True, stop=True)
                    mm.then_inc(up_done, 1)

                def step(m, j, last):
                    e = 2 * m + j
                    for c in range(4):
                        if not (last and c == 3):
                            pe.wait_ge(a_ready, 4 * e + c)
                            if c < 3:
                                project_up(m, j, c + 1)
                            else:
                                project_up(m + j, 1 - j, 0)
                        pe.wait_ge(a_ready, 4 * e + c + 1)
                        pe.wait_ge(w2_ready, e + 1)
                        pe.wait_ge(mixed, 4 * e + c)
                        for q in range(4):
                            mm = pe.matmul(dn[:, c % 2, q * P:(q + 1) * P], a[:, c % 2, q * P:(q + 1) * P], w2[:, j, :],
                                           start=True, stop=True)
                        mm.then_inc(dn_done, 1)

                project_up(0, 0, 0)
                experts(pe, step)

            @block.vector
            def _(dve):
                def step(m, j, last):
                    e = 2 * m + j
                    for c in range(4):
                        s = 4 * e + c
                        dve.wait_ge(g_ready, s + 1)
                        dve.scalar_tensor_tensor(a[:, c % 2, :], up[:, c % 2, 0, :], w[j]["b1"][:, 0:1], gl[:, c % 2, :],
                                                 ALU.add, ALU.mult).then_inc(a_ready, 1)
                        dve.wait_ge(dn_done, s + 1)
                        for q in range(4):
                            t = 4 * c + q
                            r = slice(t * P, (t + 1) * P)
                            ins = dve.scalar_tensor_tensor(acc[:, r], dn[:, c % 2, q * P:(q + 1) * P], flat[:, bass.ds(t * NE + e, 1)],
                                                           acc[:, r], ALU.mult, ALU.add)
                        ins.then_inc(mixed, 1)

                experts(dve, step)


def build(nc, dram, out):
    with ExitStack() as ctx:
        def sb(name, shape, dt=F32):
            return ctx.enter_context(nc.sbuf_tensor(f"all_{name}", shape, dt))

        k = Shared()
        k.dram, k.out = dram, out
        taken = []

        def sem(name):
            taken.append(nc.alloc_semaphore(name=name))
            return taken[-1]

        def stage(part, *args):
            part(nc, k, *args)
            nc.clear_and_free_semaphores(taken)
            nc.all_engine_barrier()
            taken.clear()

        k.sem = sem
        k.pack = {name: sb(f"pack_{name}", [P, width(f)]) for name, f in PACKS.items()}
        k.c = {}
        for name, f in PACKS.items():
            k.c.update(fields_of(k.pack[name], f))
        k.rows = sb("rows", [P, len(ROWS) * P])
        k.row = lambda name: k.rows[:, ROWS.index(name) * P:(ROWS.index(name) + 1) * P]
        k.xs = sb("x_tiles", [P, NT * P])
        k.res = sb("residual_tiles", [P, NT * P])
        k.rs = sb("sum_tiles", [P, NT * P])
        k.st = sb("six_tuples", [P, 6 * NT])
        k.mv = sb("mean_var", [P, 2 * NT])
        k.ones = sb("ones", [P, P])
        k.eps = sb("eps", [P, 1])
        k.unused = sb("unused", [P, 1])
        k.ones3 = sb("ones3", [P, P], BF16)
        k.identb = sb("identb", [P, P], BF16)
        k.pick3 = sb("pick3", [P, 32], BF16)
        k.hm = sb("head_scale", [P, 8])
        k.mask3_a = sb("mask3_a", [3, B * SC], BF16)
        k.mask3_d = sb("mask3_d", [3, B * SC], BF16)
        k.mask = sb("mask", [B, SC])
        k.mtmp = sb("mask_rest", [B, 2, SC])
        k.split_a = sb("mask_split_a", [B, 3, SC], BF16)
        k.split_d = sb("mask_split_d", [B, 3, SC], BF16)
        k.xe = k.res
        k.turn_dram = nc.dram_tensor("turned_rows", (B, S, P), F32).ap()
        k.early_loaded, k.late_loaded, k.const_made, k.const_ordered, k.mask_moved = (
            ctx.enter_context(nc.semaphore(n)) for n in ("early_loaded", "late_loaded", "const_made", "const_ordered", "mask_moved"))
        c = k.c
        taps = lambda w: [w[:, t * P:(t + 1) * P] for t in range(KS)]
        load_constants(nc, k)
        stage(attention, "a", taps(c["wq"]), taps(c["wk"]), taps(c["wv"]), c["wo"], c["a_bq"], c["a_bk"], "a_bv", "a_bo",
                  k.xs, None, k.mask3_a, False)
        stage(scan_stage)
        experts_stage(nc, k)
        stage(attention, "dc", [c["cq"]], [c["ck"]], [c["cv"]], c["co"], c["cq_b"], c["ck_b"], "cv_b", "co_b",
                  k.xs, None, k.mask3_d, False)
        stage(attention, "ds", [c["sq"]], [c["sk"]], [c["sv"]], c["so"], c["sq_b"], c["sk_b"], "sv_b", "so_b",
                  k.rs, ("co_g", "co_be"), None, True)
        stage(feed_forward)
        stage(memory_stage)
        stage(shared_experts_stage)


def constants():
    r, c = np.arange(P)[:, None], np.arange(P)[None, :]
    c32 = np.arange(32)[None, :]
    same = r // 32 == c // 32
    cst = {
        "ident": r == c,
        "sel64": r % S == np.arange(S)[None, :],
        "headmask": (r // DH) % 8 == np.arange(8)[None, :],
        "bd_strict": same & (r < c),
        "bd_upper": same & (r <= c),
        "eye32": r % 32 == c32,
        "rowlow": r % 32 < 16,
        "rowhigh": r % 32 >= 16,
        "ind2": r // 64 == np.arange(2)[None, :],
        "pick3": (r % 32 == c32) & (r < 96),
    }
    for j in range(4):
        w = 2 ** j
        cst[f"lvl{j}"] = ((r % 32) // (2 * w) == c32 // (2 * w)) & ((r % 32) // w % 2 == 1) & (c32 // w % 2 == 0)
    return {n: v.astype(np.float32) for n, v in cst.items()}


def lay_out(a):
    cat = lambda *xs: np.concatenate(xs, axis=1)
    taps = lambda w: cat(*w)
    col = lambda v: v.reshape(-1, P).T
    down = lambda w: cat(*w.reshape(-1, P, w.shape[-1]))
    parts = constants()
    parts.update(
        a_bq=col(a["L0_xattn_bq"]), a_bk=col(a["L0_xattn_bk"]), b_delta=col(a["L0_attn_b_delta"]), d_skip=col(a["L0_attn_D_skip"]),
        norm_w=col(a["L0_attn_norm_weight"]), rn_g=col(a["L0_ffn_rn_g"]), rn_b=col(a["L0_ffn_rn_b"]), lng=col(a["L0_ffn_ln_g"]),
        lnb=col(a["L0_ffn_ln_b"]), cq_b=col(a["L1_xattn_cq_b"]), ck_b=col(a["L1_xattn_ck_b"]), sq_b=col(a["L1_xattn_sq_b"]),
        sk_b=col(a["L1_xattn_sk_b"]), fi_b=col(a["L1_xattn_fi_b"]),
        wq=taps(a["L0_xattn_Wq"]), wk=taps(a["L0_xattn_Wk"]), wv=taps(a["L0_xattn_Wv"]), wo=a["L0_xattn_Wo"],
        wdelta=a["L0_attn_W_delta"], wbc=cat(a["L0_attn_W_B"], a["L0_attn_W_C"]), alog=a["L0_attn_A_log"],
        router=a["L0_ffn_router_w"].T, w1=cat(*a["L0_ffn_w1"]), w2=down(a["L0_ffn_w2"].reshape(-1, P)),
        fi=a["L1_xattn_fi_w"], fo=down(a["L1_xattn_fo_w"]), gate=a["L1_ffn_gate_w"].T)
    for n in ("cq", "ck", "cv", "co", "sq", "sk", "sv", "so"):
        parts[n] = a[f"L1_xattn_{n}_w"]
    w = a["L1_attn_W_qkvb"].reshape(P, NHM, 3 * DM + 1)
    parts.update(mq=w[:, :, 0:DM].reshape(P, -1), mk=w[:, :, DM:2 * DM].reshape(P, -1), mv=w[:, :, 2 * DM:3 * DM].reshape(P, -1),
                 mbeta=w[:, :, 3 * DM], mo=down(a["L1_attn_W_o"]))
    arrays = {name: cat(*(parts[n] for n, _ in f)) for name, f in PACKS.items()}
    rows = dict(a_bv="L0_xattn_bv", a_bo="L0_xattn_bo", on_g="L0_ffn_on_g", on_b="L0_ffn_on_b", m_g="L1_attn_ln_g", m_b="L1_attn_ln_b")
    arrays["rows"] = np.concatenate([a[rows.get(n, f"L1_xattn_{n}")] for n in ROWS])
    f1, f2, sf1, sf2 = a["L1_ffn_fc1_w"], a["L1_ffn_fc2_w"], a["L1_ffn_s_fc1_w"], a["L1_ffn_s_fc2_w"]
    up, down2, bias, mult = list(f1), list(f2), list(a["L1_ffn_fc1_b"]), list(a["L1_ffn_geglu_mult"])
    for h in range(FS // F1):
        r = slice(h * F1, (h + 1) * F1)
        g = slice(FS + h * F1, FS + (h + 1) * F1)
        up.append(np.concatenate([sf1[r], sf1[g]]))
        down2.append(sf2[:, r])
        bias.append(np.concatenate([a["L1_ffn_s_fc1_b"][r], a["L1_ffn_s_fc1_b"][g]]))
        mult.append(a["L1_ffn_s_geglu_mult"][r])
    arrays["experts"] = np.stack([cat(u.T, d.T, col(v), col(m)) for u, d, v, m in zip(up, down2, bias, mult)])
    arrays["b2"] = cat(*[v[None] for v in (np.concatenate([a["L1_ffn_fc2_b"], a["L1_ffn_s_fc2_b"][None]]))]).reshape(E1 + 1, P)
    arrays["x"] = a["x"]
    arrays["ctxT"] = a["ctx_1024"].transpose(2, 0, 1).reshape(P, B * SC)
    arrays["mask"] = a["mask_Bx1x1xS2_ff0"].reshape(B, SC)
    return {n: np.ascontiguousarray(v) for n, v in arrays.items()}


def kernel(**inputs):
    import concourse.bacc as _bacc
    from concourse import mybir as _mybir
    from concourse.bass_utils import run_bass_kernel_spmd as _run

    nc = _bacc.Bacc("TRN2", target_bir_lowering=False, num_devices=1)
    laid = lay_out({n: np.asarray(v) for n, v in inputs.items()})
    arrays, dram = {}, {}
    for name, a in laid.items():
        arrays[f"in_{name}_dram"] = a
        dram[name] = nc.dram_tensor(f"in_{name}_dram", a.shape, _mybir.dt.from_np(a.dtype), kind="ExternalInput").ap()
    out = nc.dram_tensor("out_0_dram", (B, S, P), F32, kind="ExternalOutput").ap()
    build(nc, dram, out)
    r = _run(nc, [arrays], core_ids=[0])
    return r.results[0]["out_0_dram"]
```

```python
from contextlib import ExitStack

import concourse.bass as bass
import numpy as np
from concourse import mybir

ALU = mybir.AluOpType
ACT = mybir.ActivationFunctionType
AX = mybir.AxisListType
F32 = mybir.dt.float32
BF16 = mybir.dt.bfloat16

P = 128
B, S, SC = 32, 64, 128
NT = B * S // P
NH, DH = 16, 8
NPAIR = NH // 2
KS = 3
NSTATE = 16
E0, H0 = 4, 256
FF = 512
NHM, DM = 16, 64
E1, F1, FS = 15, 128, 256
NE = E1 + FS // F1
EPS = 1e-5
DT_MIN, DT_MAX, RMS_EPS = 0.0001, 10.0, 1e-6

PACKS = {
    "cst": [("ident", P), ("sel64", S), ("headmask", 16), ("bd_strict", P), ("bd_upper", P), ("ind2", 2), ("lvl0", 32), ("lvl1", 32),
            ("lvl2", 32), ("lvl3", 32), ("eye32", 32), ("rowlow", 1), ("rowhigh", 1), ("pick3", 32)],
    "col": [("a_bq", 1), ("a_bk", 1), ("b_delta", 1), ("d_skip", 1), ("norm_w", 1), ("rn_g", 1), ("rn_b", 1),
            ("lng", 8), ("lnb", 8), ("cq_b", 1), ("ck_b", 1), ("sq_b", 1), ("sk_b", 1), ("fi_b", 4)],
    "w_a": [("wq", KS * P), ("wk", KS * P), ("wv", KS * P), ("wo", P)],
    "w_b": [("wdelta", P), ("wbc", 2 * NSTATE), ("alog", NSTATE)],
    "w_c": [("router", E0), ("w1", E0 * H0), ("w2", E0 * H0)],
    "w_d": [("cq", P), ("ck", P), ("cv", P), ("co", P), ("sq", P), ("sk", P), ("sv", P), ("so", P), ("fi", FF), ("fo", FF)],
    "w_e": [("mq", NHM * DM), ("mk", NHM * DM), ("mv", NHM * DM), ("mbeta", NHM), ("mo", NHM * DM)],
    "w_f": [("gate", E1)],
}
ROWS = ["a_bv", "a_bo", "on_g", "on_b", "cv_b", "co_b", "co_g", "co_be", "sv_b", "so_b", "so_g", "so_be",
        "fo_b", "fo_g", "fo_be", "m_g", "m_b"]
EXW = [("fc1", 2 * F1), ("fc2", P), ("b1", 2), ("mult", 1)]


class Shared:
    pass


def width(fields):
    return sum(w for _, w in fields)


def fields_of(ap, fields):
    out, at = {}, 0
    for name, w in fields:
        out[name] = ap[:, at:at + w]
        at += w
    return out


class Order:

    def __init__(self, eng, sem, per, i=0):
        self.eng, self.sem, self.per, self.base, self.n = eng, sem, per, i * per, 0

    def __call__(self, ins):
        ins.then_inc(self.sem, 1)
        self.n += 1
        self.eng.wait_ge(self.sem, self.base + self.n)

    def end(self):
        assert self.n == self.per, (self.n, self.per)


def settle(dve, k):
    dve.memset(k.unused[:, :], 0.0)


def tile(i, w=P):
    return bass.ds(i * w, w)


def pipeline(eng, n, body):
    with eng.Fori(0, n - 1) as i:
        body(i, False)
    body(n - 1, True)


def reused(eng, sem, count):
    if not (isinstance(count, int) and count <= 0):
        eng.wait_ge(sem, count)


def three_deep(eng, steps, period, apply, middle):
    def run(i, j, with_apply=True, with_middle=True, with_front=True):
        for name in period:
            ahead = 0 if name in apply else 1 if name in middle else 2
            if name in steps and (with_apply, with_middle, with_front)[ahead]:
                steps[name](i + ahead, (j + ahead) % 2)

    run(-2, 0, with_apply=False, with_middle=False)
    run(-1, 1, with_apply=False)
    run(0, 0)
    run(1, 1)
    with eng.Fori(1, NT // 2 - 1) as m:
        run(2 * m, 0)
        run(2 * m + 1, 1)
    run(NT - 2, 0, with_front=False)
    run(NT - 1, 1, with_middle=False, with_front=False)


def row_stats(dve, order, k, src):
    for t in range(NT):
        ins = dve.bn_stats(k.st[:, 6 * t:6 * t + 6], src[:, t * P:(t + 1) * P])
    order(ins)
    for t in range(NT):
        ins = dve.bn_aggr(k.mv[:, 2 * t:2 * t + 2], k.st[:, 6 * t:6 * t + 6])
    order(ins)


def aggregate(dve, order, k):
    for t in range(NT):
        ins = dve.bn_aggr(k.mv[:, 2 * t:2 * t + 2], k.st[:, 6 * t:6 * t + 6])
    order(ins)


def variances(k):
    return k.mv[:, :].rearrange("p (t two) -> p t two", two=2)[:, :, 1]


def load_constants(nc, k):
    with nc.Block() as block:
        @block.sync
        def _(sp):
            for name in ("cst", "col", "w_a"):
                sp.dma_start(k.pack[name][:, :], k.dram[name]).then_inc(k.early_loaded, 16)
            sp.dma_start(k.xs[:, :].rearrange("p (t d) -> p t d", d=P),
                         k.dram["x"].rearrange("(t b) s d -> (b s) t d", b=2)).then_inc(k.early_loaded, 16)
            sp.dma_start(k.rows[:, :], k.dram["rows"].partition_broadcast(P)).then_inc(k.early_loaded, 16)
            sp.dma_start(k.mask[:, :], k.dram["mask"]).then_inc(k.early_loaded, 16)
            for name in ("w_b", "w_c", "w_d", "w_e", "w_f"):
                sp.dma_start(k.pack[name][:, :], k.dram[name]).then_inc(k.late_loaded, 16)

        @block.gpsimd
        def _(pool):
            pool.memset(k.ones[:, :], 1.0).then_inc(k.const_made, 1)
            pool.memset(k.ones3[:, :], 1.0).then_inc(k.const_made, 1)
            pool.memset(k.eps[:, :], EPS).then_inc(k.const_made, 1)

        @block.vector
        def _(dve):
            dve.wait_ge(k.early_loaded, 16 * 6)
            order = Order(dve, k.const_ordered, 17)
            for scale, parts in ((-1e9, k.split_a), (1.0, k.split_d)):
                order(dve.tensor_scalar(k.mtmp[:, 0, :], k.mask[:, :], scale, None, ALU.mult))
                order(dve.tensor_copy(parts[:, 0, :], k.mtmp[:, 0, :]))
                order(dve.tensor_tensor(k.mtmp[:, 1, :], k.mtmp[:, 0, :], parts[:, 0, :], ALU.subtract))
                order(dve.tensor_copy(parts[:, 1, :], k.mtmp[:, 1, :]))
                order(dve.tensor_tensor(k.mtmp[:, 0, :], k.mtmp[:, 1, :], parts[:, 1, :], ALU.subtract))
                order(dve.tensor_copy(parts[:, 2, :], k.mtmp[:, 0, :]))
            order(dve.tensor_scalar(k.hm[:, :], k.c["headmask"], float(DH) ** -0.5, None, ALU.mult))
            order(dve.tensor_copy(k.pick3[:, :], k.c["pick3"]))
            row_stats(dve, order, k, k.xs)
            order(dve.tensor_copy(k.identb[:, :], k.c["ident"]))
            order.end()

        @block.scalar
        def _(act):
            act.wait_ge(k.const_ordered, 12)
            for parts, dst in ((k.split_a, k.mask3_a), (k.split_d, k.mask3_d)):
                for j in range(3):
                    act.dma_start(dst[j:j + 1, :].rearrange("o (b n) -> o b n", n=SC), parts[:, j, :]).then_inc(k.mask_moved, 16)
            act.wait_ge(k.mask_moved, 16 * 6)


def attention(nc, k, st, wq, wk, wv, wo, bq, bk, bv_row, bo_row, src, affine, mask3, own_keys):
    taps = len(wq)
    NK = S if own_keys else SC
    PB = SC // NK
    NB = NPAIR // PB
    HB = NB // 2
    first = affine is None and taps == KS
    sem = lambda name: k.sem(f"{st}_{name}")
    with ExitStack() as ctx:
        def sb(name, shape, dt=F32):
            return ctx.enter_context(nc.sbuf_tensor(f"{st}_{name}", shape, dt))

        cx = sb("context", [P, 2, 2, SC + 2])
        xq = sb("query_in", [P, P])
        xs_n = sb("scaled_in", [P, P])
        xT = sb("query_inT", [P, 2, S + 2])
        qT = sb("qT", [P, 2, S])
        qbd = sb("q_heads", [P, 2, NH, S])
        v_in = sb("v_plain", [P, 2, P])
        kT = sb("kT", [P, 2, NK])
        va = sb("v_ones", [P, 2, 2, NB, PB, 17])
        pr = sb("probs", [P, 2, 2, NPAIR, NK])
        prT = sb("probsT", [P, 2, NB, P])
        mx = sb("row_max", [P, 2, NPAIR])
        rd = sb("row_recip", [P, 2, NPAIR])
        on = sb("attended", [P, 2, NPAIR, 2, DH])
        oT = sb("attendedT", [P, P])
        std = sb("std", [P, NT])
        rstd = sb("rstd", [P, NT])
        sc = ctx.enter_context(nc.psum_tensor(f"{st}_scores", [P, 2, 2, 512], F32))
        pt = ctx.enter_context(nc.psum_tensor(f"{st}_turned", [P, 2, 512], F32))
        pa = ctx.enter_context(nc.psum_tensor(f"{st}_even_bank", [P, 512], F32))
        pb = ctx.enter_context(nc.psum_tensor(f"{st}_odd_bank", [P, 512], F32))
        oT_p, out_p = pa[:, 384:512], pb[:, 384:512]
        q_p, k_p, v_p, xT_p = pt[:, 0, 0:P], pt[:, 0, P:P + 2 * NK], pt[:, 1, 0:2 * P], pt[:, 0, 384:512]

        def att_p(b):
            return (pa, pb)[b][:, 0:NPAIR * 17].rearrange("p (a c) -> p a c", c=17)

        FRONT = ["n", "x", "qkv"]
        SCORE = ["S0", "E0", "S1", "E1"]
        APPLY = ["T0", "T1", "O0", "D0", "O1", "D1", "P1", "P2"]
        PERIOD = ["n", "S0", "T0", "S1", "E0", "T1", "x", "O0", "D0", "E1", "O1", "D1", "qkv", "P1", "P2"]
        assert sorted(PERIOD) == sorted(FRONT + SCORE + APPLY)

        zeroed, stats, std_made, rstd_made = sem("zeroed"), sem("stats"), sem("std_made"), sem("rstd_made")
        ctx_ready, xq_ready, xT_turned, xT_ready = [sem("ctx_ready0"), sem("ctx_ready1")], sem("xq_ready"), sem("xT_turned"), sem("xT_ready")
        q_done, k_done, v_done = sem("q_done"), sem("k_done"), sem("v_done")
        q_copied, k_ready, v_copied = sem("q_copied"), sem("k_ready"), sem("v_copied")
        q_ready, v_ready = sem("q_ready"), sem("v_ready")
        s_done, max_ready, p_ready, e_ready = sem("s_done"), sem("max_ready"), sem("p_ready"), sem("e_ready")
        t_done, t_ready, o_done, recip_ready, o_ready = sem("t_done"), sem("t_ready"), sem("o_done"), sem("recip_ready"), sem("o_ready")
        oT_done, oT_ready, out_done, sum_ready = sem("oT_done"), sem("oT_ready"), sem("out_done"), sem("sum_ready")
        own, va_cleared, va_filled = sem("tile_steps"), sem("va_cleared"), sem("va_filled")
        block = ctx.enter_context(nc.Block())

        @block.sync
        def _(sp):
            if own_keys:
                return
            sp.wait_ge(zeroed, 3)

            def load(i, j):
                reused(sp, v_done, i - 1)
                sp.dma_start(cx[:, j, :, 1:SC + 1], k.dram["ctxT"][:, tile(i, 2 * SC)].rearrange("p (b n) -> p b n", b=2))\
                    .then_inc(ctx_ready[j], 16)

            load(0, 0)
            load(1, 1)
            with sp.Fori(1, NT // 2) as m:
                load(2 * m, 0)
                load(2 * m + 1, 1)

        @block.gpsimd
        def _(pool):
            pool.memset(cx[:, :, :, :], 0.0).then_inc(zeroed, 1)
            pool.memset(xT[:, :, :], 0.0).then_inc(zeroed, 1)
            pool.memset(on[:, :, :, :, :], 0.0).then_inc(zeroed, 1)
            pool.memset(va[:, :, :, :, :, :], 0.0).then_inc(va_cleared, 1)
            for n in range(PB):
                pool.wait_ge(va_cleared, n + 1)
                pool.memset(va[n * NK:(n + 1) * NK, :, :, :, n, 16], 1.0).then_inc(va_cleared, 1)
            pool.wait_ge(va_cleared, PB + 1)
            pool.sem_inc(zeroed, 1)

            def qkv(i, j):
                pool.wait_ge(q_copied, i + 1)
                reused(pool, s_done, 2 * i)
                pool.tensor_tensor(qbd[:, :, :, :], qT[:, :, :].unsqueeze(2).to_broadcast([P, 2, NH, S]),
                                   k.hm[:, :].unsqueeze(1).unsqueeze(3).to_broadcast([P, 2, NH, S]), ALU.mult).then_inc(q_ready, 1)
                pool.wait_ge(v_copied, i + 1)
                reused(pool, o_done, 2 * i - 2)
                for n in range(PB):
                    r = slice(n * NK, (n + 1) * NK)
                    blocks = lambda ap: ap.rearrange("p (a n c) -> p a n c", n=PB, c=16)[:, :, n, :]
                    for b in range(2):
                        ins = pool.tensor_tensor(va[r, j, b, :, n, 0:16], blocks(v_in[r, b, :]), blocks(k.row(bv_row)[r, :]), ALU.add)
                    if n < PB - 1:
                        ins.then_inc(va_filled, 1)
                        pool.wait_ge(va_filled, i + 1)
                ins.then_inc(v_ready, 1)
                if PB > 1:
                    pool.wait_ge(v_ready, i + 1)

            three_deep(pool, {"qkv": qkv}, PERIOD, APPLY, SCORE)

        @block.scalar
        def _(act):
            act.wait_ge(stats, 1)
            act.activation(std[:, :], variances(k), ACT.Sqrt, bias=k.eps[:, :]).then_inc(std_made, 1)
            act.wait_ge(zeroed, 4)

            def x(i, j):
                act.wait_ge(xT_turned, i + 1)
                reused(act, v_done, i)
                act.activation(xT[:, :, 1:S + 1], xT_p.rearrange("p (b s) -> p b s", b=2), ACT.Copy).then_inc(xT_ready, 1)

            def qkv(i, j):
                act.wait_ge(k_done, i + 1)
                reused(act, q_ready, i)
                act.activation(qT[:, :, :], q_p.rearrange("p (b s) -> p b s", b=2), ACT.Identity, bias=bq).then_inc(q_copied, 1)
                reused(act, s_done, 2 * i)
                act.activation(kT[:, :, :], k_p.rearrange("p (b n) -> p b n", b=2), ACT.Identity, bias=bk).then_inc(k_ready, 1)
                act.wait_ge(v_done, i + 1)
                reused(act, v_ready, i)
                act.activation(v_in[:, :, :], v_p.rearrange("p (b c) -> p b c", b=2), ACT.Copy).then_inc(v_copied, 1)

            def exp(b):
                def step(i, j):
                    act.wait_ge(p_ready, 2 * i + b + 1)
                    act.activation(pr[:, j, b, :, :], pr[:, j, b, :, :], ACT.Exp).then_inc(e_ready, 1)
                return step

            def turn(b):
                def step(i, j):
                    for half in range(2):
                        act.wait_ge(t_done, 4 * i + 2 * b + half + 1)
                        reused(act, o_done, 2 * i + b - 1)
                        act.activation(prT[:, b, HB * half:HB * half + HB, :],
                                       pt[:, half, 0:HB * P].rearrange("p (a c) -> p a c", a=HB), ACT.Copy).then_inc(t_ready, 1)
                return step

            def out_turn(i, j):
                act.wait_ge(oT_done, i + 1)
                reused(act, out_done, i)
                act.activation(oT[:, :], oT_p, ACT.Copy).then_inc(oT_ready, 1)

            act.preload_act_table_set("exp_and_others")
            three_deep(act, {"x": x, "qkv": qkv, "E0": exp(0), "E1": exp(1), "T0": turn(0), "T1": turn(1), "P1": out_turn},
                       PERIOD, APPLY, SCORE)

        @block.vector
        def _(dve):
            order = Order(dve, stats, 1)
            aggregate(dve, order, k)
            dve.wait_ge(std_made, 1)
            dve.reciprocal(rstd[:, :], std[:, :]).then_inc(rstd_made, 1)
            dve.wait_ge(rstd_made, 1)
            dve.wait_ge(zeroed, 4)

            def norm_in(i, j):
                reused(dve, xT_turned, i)
                outs = [xq[:, :]] if first else [k.res[:, tile(i)], xq[:, :]]
                plain = [xs_n[:, :]] if affine else outs
                for o in plain:
                    ins = dve.tensor_scalar(o, src[:, tile(i)], k.mv[:, bass.ds(2 * i, 1)], rstd[:, bass.ds(i, 1)],
                                            ALU.subtract, ALU.mult)
                if affine:
                    order = Order(dve, own, 2, i)
                    order(ins)
                    order(dve.tensor_tensor(xs_n[:, :], xs_n[:, :], k.row(affine[0]), ALU.mult))
                    order.end()
                    for o in outs:
                        ins = dve.tensor_tensor(o, xs_n[:, :], k.row(affine[1]), ALU.add)
                ins.then_inc(xq_ready, 1)

            def soft(b):
                def step(i, j):
                    dve.wait_ge(s_done, 2 * i + b + 1)
                    s4 = sc[:, b, :, 0:4 * NK].rearrange("p h (a n) -> p h a n", a=4)
                    dve.tensor_reduce(mx[:, b, :].rearrange("p (h a) -> p h a", h=2), s4, AX.X, ALU.max).then_inc(max_ready, 1)
                    dve.wait_ge(max_ready, 2 * i + b + 1)
                    reused(dve, t_done, 4 * i + 2 * b - 6)
                    dve.tensor_tensor(pr[:, j, b, :, :].rearrange("p (h a) n -> p h a n", h=2), s4,
                                      mx[:, b, :].rearrange("p (h a) -> p h a", h=2).unsqueeze(3).to_broadcast([P, 2, 4, NK]),
                                      ALU.subtract).then_inc(p_ready, 1)
                return step

            def divide(b):
                def step(i, j):
                    dve.wait_ge(o_done, 2 * i + b + 1)
                    o = att_p(b)
                    dve.reciprocal(rd[:, b, :], o[:, :, 16]).then_inc(recip_ready, 1)
                    dve.wait_ge(recip_ready, 2 * i + b + 1)
                    reused(dve, oT_done, i)
                    for h in range(2):
                        r = slice(h * S, (h + 1) * S)
                        ins = dve.tensor_tensor(on[r, b, :, h, :], o[r, :, h * DH:(h + 1) * DH],
                                                rd[r, b, :].unsqueeze(2).to_broadcast([S, NPAIR, DH]), ALU.mult)
                    ins.then_inc(o_ready, 1)
                return step

            def add_out(i, j):
                dve.wait_ge(out_done, i + 1)
                into, old = (k.xs, k.xs) if first else (k.rs, k.res)
                dve.tensor_tensor(into[:, tile(i)], out_p, old[:, tile(i)], ALU.add).then_inc(sum_ready, 1)
                dve.wait_ge(sum_ready, i + 1)
                dve.bn_stats(k.st[:, bass.ds(6 * i, 6)], into[:, tile(i)])

            three_deep(dve, {"n": norm_in, "S0": soft(0), "S1": soft(1), "D0": divide(0), "D1": divide(1), "P2": add_out},
                       PERIOD, APPLY, SCORE)

        @block.tensor
        def _(pe):
            def x(i, j):
                pe.wait_ge(xq_ready, i + 1)
                reused(pe, t_ready, 4 * i - 4)
                pe.transpose(xT_p, xq[:, :], k.c["ident"]).then_inc(xT_turned, 1)

            def qkv(i, j):
                pe.wait_ge(xT_ready, i + 1)
                kv = xT if own_keys else cx[:, j, :, :]
                if not own_keys:
                    pe.wait_ge(ctx_ready[j], 8 * i - 8 * j + 16)
                for t in range(taps):
                    a = 1 + t - taps // 2
                    pe.matmul(q_p.rearrange("p (b s) -> p b s", b=2), wq[t], xT[:, :, a:a + S], start=t == 0, stop=t == taps - 1)
                for t in range(taps):
                    a = 1 + t - taps // 2
                    mm = pe.matmul(k_p.rearrange("p (b n) -> p b n", b=2), wk[t], kv[:, :, a:a + NK],
                                   start=t == 0, stop=t == taps - 1)
                mm.then_inc(k_done, 1)
                for b in range(2):
                    for n in range(PB):
                        for t in range(taps):
                            a = 1 + t - taps // 2
                            mm = pe.matmul(v_p[n * NK:(n + 1) * NK, b * P:(b + 1) * P], kv[:, b, a:a + NK], wv[t],
                                           start=t == 0, stop=t == taps - 1)
                mm.then_inc(v_done, 1)

            def scores(b):
                def step(i, j):
                    if b == 0:
                        pe.wait_ge(q_ready, i + 1)
                        pe.wait_ge(k_ready, i + 1)
                    reused(pe, p_ready, 2 * i + b - 1)
                    for h in range(2):
                        out = sc[:, b, h, 0:4 * NK].rearrange("p (a n) -> p a n", a=4)
                        if mask3 is not None:
                            m = mask3[:, bass.ds((2 * i + b) * SC, NK)].unsqueeze(1).to_broadcast([3, 4, NK])
                            pe.matmul(out, k.ones3[0:3, :], m, start=True, stop=False)
                        for a in range(4):
                            n = 8 * h + 2 * a
                            mm = pe.matmul(out[:, a, :], qbd[:, b, n:n + 2, :].rearrange("p a s -> p (a s)"), kT[:, b, :], start=mask3 is None, stop=mask3 is None or a == 3)
                    mm.then_inc(s_done, 1)
                return step

            def turn(b):
                def step(i, j):
                    if b == 0 and not (isinstance(i, int) and i == NT - 1):
                        pe.wait_ge(k_ready, i + 2)
                        pe.wait_ge(v_copied, i + 2)
                    pe.wait_ge(e_ready, 2 * i + b + 1)
                    for half in range(2):
                        if b:
                            pe.wait_ge(t_ready, 4 * i + half + 1)
                        for n in range(HB):
                            a = (HB * half + n) * PB
                            mm = pe.transpose(pt[:, half, n * P:(n + 1) * P],
                                              pr[:, j, b, a:a + PB, :].rearrange("p a n -> p (a n)"), k.c["ident"])
                        mm.then_inc(t_done, 1)
                return step

            def attend(b):
                def step(i, j):
                    pe.wait_ge(t_ready, 4 * i + 2 * b + 2)
                    pe.wait_ge(v_ready, i + 1)
                    reused(pe, (oT_ready, sum_ready)[b], i)
                    for n in range(NB):
                        last = min(n + 6 // PB, NB)
                        mm = pe.matmul((pa, pb)[b][:, n * 17 * PB:last * 17 * PB], prT[:, b, n, :],
                                       va[:, j, b, n:last, :, :].rearrange("p n a c -> p (n a c)"), start=True, stop=True)
                    mm.then_inc(o_done, 1)
                return step

            def out_turn(i, j):
                pe.wait_ge(o_ready, 2 * i + 2)
                for b in range(2):
                    mm = pe.matmul(oT_p[:, b * S:(b + 1) * S], on[:, b, :, :, :].rearrange("p a h d -> p (a h d)"), k.c["sel64"],
                                   start=True, stop=True)
                mm.then_inc(oT_done, 1)

            def project(i, j):
                pe.wait_ge(oT_ready, i + 1)
                pe.matmul(out_p, k.ones[0:1, :], k.row(bo_row)[0:1, :], start=True, stop=False)
                pe.matmul(out_p, oT[:, :], wo, start=False, stop=True).then_inc(out_done, 1)

            three_deep(pe, {"x": x, "qkv": qkv, "S0": scores(0), "S1": scores(1), "T0": turn(0), "T1": turn(1), "O0": attend(0),
                            "O1": attend(1), "P1": out_turn, "P2": project}, PERIOD, APPLY, SCORE)


def scan_stage(nc, k):
    CH = 512
    NC = B * S // CH
    G = 4
    centre, half = (DT_MAX + DT_MIN) / 2.0, (DT_MAX - DT_MIN) / 2.0
    sem = lambda name: k.sem(f"b_{name}")
    with ExitStack() as ctx:
        def sb(name, shape, dt=F32):
            return ctx.enter_context(nc.sbuf_tensor(f"b_{name}", shape, dt))

        xnT = sb("xnT", [P, B * S])
        delta = sb("delta", [P, B * S])
        u = sb("sqrt_delta_x", [P, B * S])
        bc3 = sb("bc_terms", [96, B * S], BF16)
        sa = sb("half_a", [P, NSTATE])
        zeros = sb("zeros", [1, CH], BF16)
        dskip = sb("skip_diagonal", [P, P])
        small = sb("row_factors", [P, 6, NT])
        neg1 = sb("minus_one", [P, 1])
        tbias = sb("tanh_bias", [P, 1])
        rbias = sb("rms_eps", [P, 1])
        with ExitStack() as inner:
            t1 = inner.enter_context(nc.sbuf_tensor("b_t1", [P, B * S], F32))
            t2 = inner.enter_context(nc.sbuf_tensor("b_t2", [P, B * S], F32))
            rest = inner.enter_context(nc.sbuf_tensor("b_rest", [32, 2, CH], F32))
            low = inner.enter_context(nc.sbuf_tensor("b_low", [32, 2, B * S], BF16))
            turned = inner.enter_context(nc.psum_tensor("b_turned", [P, 2, 512], F32))
            dp = inner.enter_context(nc.psum_tensor("b_delta_p", [P, 2, 512], F32))
            bp = inner.enter_context(nc.psum_tensor("b_bc_p", [32, 2, 512], F32))
            made, varied, std1, std2 = sem("constants"), sem("varied"), sem("std1"), sem("std2")
            xn_ready, xn_turned, xnT_ready = sem("xn_ready"), sem("xn_turned"), sem("xnT_ready")
            d_done, d_left, bc_done, bc_left = sem("d_done"), sem("d_left"), sem("bc_done"), sem("bc_left")
            act_steps, dve_steps, low_ready = sem("act_steps"), sem("dve_steps"), sem("low_ready")
            soft_ready, sum_ready, exp_ready, delta_ready, root_ready = (
                sem("soft_ready"), sem("sum_ready"), sem("exp_ready"), sem("delta_ready"), sem("root_ready"))
            a_ready, moved = sem("a_ready"), sem("moved")
            with nc.Block() as block:
                @block.gpsimd
                def _(pool):
                    pool.memset(zeros[:, :], 0.0)
                    pool.memset(neg1[:, :], -1.0).then_inc(made, 1)
                    pool.memset(tbias[:, :], -2.0 * centre / half).then_inc(made, 1)
                    pool.memset(rbias[:, :], RMS_EPS).then_inc(made, 1)
                    pool.wait_ge(low_ready, NC)
                    for j in range(2):
                        pool.tensor_copy(bc3[32 * (j + 1):32 * (j + 2), :], low[:, j, :]).then_inc(moved, 1)
                        pool.wait_ge(moved, j + 1)
                    pool.tensor_scalar(dskip[:, :], k.c["ident"], k.c["d_skip"], None, ALU.mult)

                @block.vector
                def _(dve):
                    order = Order(dve, dve_steps, 8 + 5 * NC)
                    aggregate(dve, order, k)
                    dve.sem_inc(varied, 1)
                    dve.wait_ge(std1, 1)
                    rstd, msq, r2, rs = small[:, 1, :], small[:, 2, :], small[:, 4, :], small[:, 5, :]
                    order(dve.reciprocal(rstd, small[:, 0, :]))
                    order(dve.tensor_tensor(msq, variances(k), rstd, ALU.mult))
                    order(dve.tensor_tensor(msq, msq, rstd, ALU.mult))
                    dve.sem_inc(varied, 1)
                    dve.wait_ge(std2, 1)
                    order(dve.reciprocal(r2, small[:, 3, :]))
                    order(dve.tensor_tensor(rs, rstd, r2, ALU.mult))
                    for t in range(NT):
                        ins = dve.tensor_scalar(k.res[:, t * P:(t + 1) * P], k.xs[:, t * P:(t + 1) * P], k.mv[:, 2 * t:2 * t + 1],
                                                rs[:, t:t + 1], ALU.subtract, ALU.mult)
                        if t % 4 == 3:
                            ins.then_inc(xn_ready, 1)
                    for c in range(NC):
                        r = slice(c * CH, (c + 1) * CH)
                        dve.wait_ge(bc_done, c + 1)
                        b = bp[:, c % 2, :]
                        order(dve.tensor_copy(bc3[0:32, r], b))
                        order(dve.tensor_tensor(rest[:, 0, :], b, bc3[0:32, r], ALU.subtract))
                        dve.sem_inc(bc_left, 1)
                        order(dve.tensor_copy(low[:, 0, r], rest[:, 0, :]))
                        order(dve.tensor_tensor(rest[:, 1, :], rest[:, 0, :], low[:, 0, r], ALU.subtract))
                        order(dve.tensor_copy(low[:, 1, r], rest[:, 1, :]))
                        dve.sem_inc(low_ready, 1)
                    dve.wait_ge(soft_ready, 1)
                    dve.tensor_tensor(t1[:, :], t1[:, :], t2[:, :], ALU.add).then_inc(sum_ready, 1)
                    dve.wait_ge(exp_ready, 1)
                    order(dve.tensor_scalar(t1[:, :], t1[:, :], 1.0, None, ALU.add))
                    order(dve.reciprocal(t1[:, :], t1[:, :]))
                    dve.tensor_scalar(delta[:, :], t1[:, :], -2.0 * half, centre + half, ALU.mult, ALU.add).then_inc(delta_ready, 1)
                    dve.wait_ge(root_ready, 1)
                    dve.tensor_tensor(u[:, :], t2[:, :], xnT[:, :], ALU.mult)
                    dve.wait_ge(a_ready, 1)
                    dve.tensor_scalar(sa[:, :], sa[:, :], 0.5, None, ALU.mult)
                    order.end()

                @block.scalar
                def _(act):
                    act.wait_ge(k.late_loaded, 16 * 5)
                    act.wait_ge(varied, 1)
                    act.activation(small[:, 0, :], variances(k), ACT.Sqrt, bias=k.eps[:, :]).then_inc(std1, 1)
                    act.wait_ge(varied, 2)
                    act.wait_ge(made, 3)
                    act.activation(small[:, 3, :], small[:, 2, :], ACT.Sqrt, bias=rbias[:, :]).then_inc(std2, 1)
                    for c in range(NC):
                        act.wait_ge(xn_turned, c + 1)
                        act.activation(xnT[:, c * CH:(c + 1) * CH], turned[:, c % 2, :], ACT.Copy, scale=k.c["norm_w"]).then_inc(xnT_ready, 1)
                    for c in range(NC):
                        r = slice(c * CH, (c + 1) * CH)
                        act.wait_ge(d_done, c + 1)
                        act.activation(t1[:, r], dp[:, c % 2, :], ACT.Abs, bias=k.c["b_delta"])
                        act.activation(t2[:, r], dp[:, c % 2, :], ACT.Relu, bias=k.c["b_delta"]).then_inc(d_left, 1)
                    act.wait_ge(d_left, NC)
                    order = Order(act, act_steps, 1)
                    order(act.activation(t1[:, :], t1[:, :], ACT.Exp, scale=-1.0))
                    act.activation(t1[:, :], t1[:, :], ACT.Ln, bias=k.ones[:, 0:1]).then_inc(soft_ready, 1)
                    act.wait_ge(sum_ready, 1)
                    act.activation(t1[:, :], t1[:, :], ACT.Exp, bias=tbias[:, :], scale=2.0 / half).then_inc(exp_ready, 1)
                    act.activation(sa[:, :], k.c["alog"], ACT.Exp).then_inc(a_ready, 1)
                    act.wait_ge(delta_ready, 1)
                    act.activation(t2[:, :], delta[:, :], ACT.Sqrt).then_inc(root_ready, 1)

                @block.tensor
                def _(pe):
                    pe.wait_ge(k.late_loaded, 16 * 5)
                    for c in range(NC):
                        pe.wait_ge(xn_ready, c + 1)
                        if c >= 2:
                            pe.wait_ge(xnT_ready, c - 1)
                        for j in range(4):
                            t = 4 * c + j
                            mm = pe.transpose(turned[:, c % 2, j * P:(j + 1) * P], k.res[:, t * P:(t + 1) * P], k.c["ident"])
                        mm.then_inc(xn_turned, 1)
                    for c in range(NC):
                        r = slice(c * CH, (c + 1) * CH)
                        pe.wait_ge(xnT_ready, c + 1)
                        if c >= 2:
                            pe.wait_ge(d_left, c - 1)
                            pe.wait_ge(bc_left, c - 1)
                        pe.matmul(dp[:, c % 2, :], k.c["wdelta"], xnT[:, r], start=True, stop=True).then_inc(d_done, 1)
                        pe.matmul(bp[:, c % 2, :], k.c["wbc"], xnT[:, r], start=True, stop=True).then_inc(bc_done, 1)

        with ExitStack() as inner:
            def buf(name, n):
                return inner.enter_context(nc.sbuf_tensor(f"b_{name}", [P, n, CH], F32))

            inv, ab, w, bx, h, hc = buf("inverse", G), buf("a_bar", G), buf("inverse_u", G), buf("b_x", 2), buf("states", 2), buf("states_c", 2)
            bb = inner.enter_context(nc.psum_tensor("b_b_bank", [P, 2, 512], F32))
            cb = inner.enter_context(nc.psum_tensor("b_c_bank", [P, 2, 512], F32))
            yp = inner.enter_context(nc.psum_tensor("b_y_bank", [P, 2, 512], F32))
            cleared, ln_ready, inv_ready, ab_ready, w_ready = (sem(n) for n in ("cleared", "ln_ready", "inv_ready", "ab_ready", "w_ready"))
            bb_done, bx_ready, h_ready, hc_ready, y_done, added = (
                sem(n) for n in ("bb_done", "bx_ready", "h_ready", "hc_ready", "y_done", "added"))

            def groups(eng, body, chunk_end=None):
                for c in range(NC):
                    body(c, 0, NSTATE * c, c == 0)
                    with eng.Fori(1, NSTATE // G) as g:
                        body(c, G * g, NSTATE * c + G * g, False)
                    if chunk_end:
                        chunk_end(c)

            with nc.Block() as block:
                @block.scalar
                def _(act):
                    act.wait_ge(cleared, 1)
                    act.preload_act_table_set("natural_log_exp_and_others")

                    def body(c, n, s, first):
                        for p in (0, 2):
                            if not first:
                                act.wait_ge(w_ready, s + p - 2)
                            for j in (p, p + 1):
                                ins = act.activation(inv[:, j, :], delta[:, c * CH:(c + 1) * CH], ACT.Ln, bias=k.ones[:, 0:1],
                                                     scale=sa[:, bass.ds(n + j, 1)])
                            ins.then_inc(ln_ready, 2)
                            act.wait_ge(ln_ready, s + p + 2)
                            act.activation(inv[:, p:p + 2, :], inv[:, p:p + 2, :], ACT.Exp, scale=-1.0).then_inc(inv_ready, 2)
                            act.wait_ge(inv_ready, s + p + 2)
                            if not first:
                                act.wait_ge(h_ready, s + p - 2)
                            act.activation(ab[:, p:p + 2, :].rearrange("p j (b s) -> p (j b) s", s=S)[:, :, 1:S],
                                           inv[:, p:p + 2, :].rearrange("p j (b s) -> p (j b) s", s=S)[:, :, 1:S],
                                           ACT.Identity, bias=neg1[:, :], scale=2.0).then_inc(ab_ready, 2)

                    groups(act, body)

                @block.gpsimd
                def _(pool):
                    pool.memset(ab[:, :, :], 0.0).then_inc(cleared, 1)

                    def body(c, n, s, first):
                        for j in range(G):
                            pool.wait_ge(inv_ready, s + j - j % 2 + 2)
                            if not first:
                                pool.wait_ge(bx_ready, s + j - 3)
                            pool.tensor_tensor(w[:, j, :], inv[:, j, :], u[:, c * CH:(c + 1) * CH], ALU.mult).then_inc(w_ready, 1)

                    groups(pool, body)

                @block.vector
                def _(dve):
                    dve.wait_ge(cleared, 1)

                    def body(c, n, s, first):
                        for j in range(G):
                            dve.wait_ge(w_ready, s + j + 1)
                            dve.wait_ge(bb_done, s + j + 1)
                            dve.tensor_tensor(bx[:, j % 2, :], w[:, j, :], bb[:, j % 2, :], ALU.mult).then_inc(bx_ready, 1)
                            dve.wait_ge(bx_ready, s + j + 1)
                            dve.wait_ge(ab_ready, s + j - j % 2 + 2)
                            dve.tensor_tensor_scan(h[:, j % 2, :], ab[:, j, :], bx[:, j % 2, :], 0.0, ALU.mult, ALU.add).then_inc(h_ready, 1)
                            dve.wait_ge(h_ready, s + j + 1)
                            if not (first and j < 2):
                                dve.wait_ge(y_done, s + j - 1)
                            dve.tensor_tensor(hc[:, j % 2, :], h[:, j % 2, :], cb[:, j % 2, :], ALU.mult).then_inc(hc_ready, 1)

                    def chunk_end(c):
                        r = slice(c * CH, (c + 1) * CH)
                        dve.wait_ge(y_done, NSTATE * (c + 1))
                        dve.tensor_tensor(k.xs[:, r], k.xs[:, r], yp[:, c % 2, :], ALU.add).then_inc(added, 1)
                        dve.wait_ge(added, c + 1)
                        for t in range(4 * c, 4 * c + 4):
                            dve.bn_stats(k.st[:, 6 * t:6 * t + 6], k.xs[:, t * P:(t + 1) * P])

                    groups(dve, body, chunk_end)

                @block.tensor
                def _(pe):
                    def add(c, j, last=False):
                        for q in range(4):
                            mm = pe.matmul(yp[:, c % 2, q * P:(q + 1) * P], hc[:, j % 2, q * P:(q + 1) * P], k.c["ident"],
                                           start=False, stop=last and q == 3)
                        mm.then_inc(y_done, 1)

                    def body(c, n, s, first):
                        for j in range(G):
                            if not (first and j < 2):
                                pe.wait_ge(hc_ready, s + j - 1)
                            pe.matmul(bb[:, j % 2, :], k.pick3[0:96, bass.ds(n + j, 1)].to_broadcast([96, P]),
                                      bc3[:, c * CH:(c + 1) * CH], start=True, stop=True)
                            pe.matmul(cb[:, j % 2, :], k.pick3[0:96, bass.ds(n + j + NSTATE, 1)].to_broadcast([96, P]),
                                      bc3[:, c * CH:(c + 1) * CH], start=True, stop=True).then_inc(bb_done, 1)
                            if isinstance(n, int) and j == 0:
                                if c >= 2:
                                    pe.wait_ge(added, c - 1)
                                pe.matmul(yp[:, c % 2, :], k.ones3[0:1, :], zeros[:, :], start=True, stop=False)
                                for q in range(4):
                                    pe.matmul(yp[:, c % 2, q * P:(q + 1) * P], xnT[:, c * CH + q * P:c * CH + (q + 1) * P],
                                              dskip[:, :], start=False, stop=False)
                            else:
                                pe.wait_ge(hc_ready, s + j)
                                add(c, j - 1)

                    def chunk_end(c):
                        pe.wait_ge(hc_ready, NSTATE * (c + 1))
                        add(c, G - 1, True)

                    groups(pe, body, chunk_end)


def top_experts(dve, order, pool_filled, score, picked, values, kept, n, top, pad):
    for t in range(NT):
        ins = dve.max(values[:, t, :], score[:, t, :])
    order(ins)
    order(dve.memset(values[:, :, top:8], -1.0))
    for t in range(NT):
        ins = dve.match_replace(picked[:, t, :], values[:, t, :], score[:, t, :], -2.0)
    order(ins)
    order(dve.tensor_scalar(picked[:, :, 0:n], picked[:, :, 0:n], -2.0, None, ALU.is_equal))
    order(dve.tensor_tensor(kept, picked[:, :, 0:n], score[:, :, 0:n], ALU.mult))


def experts_stage(nc, k):
    N8 = E0 * H0 // P
    sem = lambda name: k.sem(f"c_{name}")
    with ExitStack() as ctx:
        def sb(name, shape, dt=F32):
            return ctx.enter_context(nc.sbuf_tensor(f"c_{name}", shape, dt))

        def psum(name, shape):
            return ctx.enter_context(nc.psum_tensor(f"c_{name}", shape, F32))

        comb = sb("weights", [P, NT, E0])
        rstd = sb("rstd", [P, NT])
        with ExitStack() as inner:
            hT = inner.enter_context(nc.sbuf_tensor("c_hT_all", [P, B * S], F32))
            small = inner.enter_context(nc.sbuf_tensor("c_row_factors", [P, 4, NT], F32))
            gR = inner.enter_context(nc.sbuf_tensor("c_scaled_router", [P, E0], F32))
            bR = inner.enter_context(nc.sbuf_tensor("c_router_bias", [P, E0], F32))
            lg = inner.enter_context(nc.sbuf_tensor("c_logits", [P, NT, E0], F32))
            score = inner.enter_context(nc.sbuf_tensor("c_scores", [P, NT, E0 + 6], F32))
            picked = inner.enter_context(nc.sbuf_tensor("c_picked", [P, NT, E0 + 6], F32))
            values = inner.enter_context(nc.sbuf_tensor("c_values", [P, NT, 8], F32))
            red = inner.enter_context(nc.sbuf_tensor("c_reduced", [P, 4, NT], F32))
            turned = inner.enter_context(nc.psum_tensor("c_turned_p", [P, 2, 512], F32))
            lp = inner.enter_context(nc.psum_tensor("c_logit_p", [P, 512], F32))
            bp = inner.enter_context(nc.psum_tensor("c_bias_p", [P, 512], F32))
            varied, std1, std2, filled, steps = sem("varied"), sem("std1"), sem("std2"), sem("filled"), sem("router_steps")
            h_ready, h_turned, hT_ready, gR_ready = sem("h_ready"), sem("h_turned"), sem("hT_ready"), sem("gR_ready")
            logit_done, shifted, exp_ready = sem("logit_done"), sem("shifted"), sem("exp_ready")
            with nc.Block() as block:
                @block.gpsimd
                def _(pool):
                    pool.memset(score[:, :, :], -1.0).then_inc(filled, 1)

                @block.scalar
                def _(act):
                    act.wait_ge(varied, 1)
                    act.activation(small[:, 0, :], variances(k), ACT.Sqrt, bias=k.eps[:, :]).then_inc(std1, 1)
                    act.wait_ge(varied, 2)
                    act.activation(small[:, 2, :], small[:, 1, :], ACT.Sqrt, bias=k.eps[:, :]).then_inc(std2, 1)
                    for c in range(4):
                        act.wait_ge(h_turned, c + 1)
                        act.activation(hT[:, c * 512:(c + 1) * 512], turned[:, c % 2, :], ACT.Copy).then_inc(hT_ready, 1)
                    act.wait_ge(shifted, 1)
                    act.activation(lg[:, :, :], lg[:, :, :], ACT.Exp).then_inc(exp_ready, 1)

                @block.tensor
                def _(pe):
                    for c in range(4):
                        pe.wait_ge(h_ready, c + 1)
                        if c >= 2:
                            pe.wait_ge(hT_ready, c - 1)
                        for j in range(4):
                            t = 4 * c + j
                            mm = pe.transpose(turned[:, c % 2, j * P:(j + 1) * P], k.res[:, t * P:(t + 1) * P], k.c["ident"])
                        mm.then_inc(h_turned, 1)
                    pe.wait_ge(gR_ready, 1)
                    pe.matmul(bp[:, 0:E0], k.c["rn_b"].to_broadcast([P, P]), k.c["router"], start=True, stop=True)
                    for t in range(NT):
                        if t % 4 == 0:
                            pe.wait_ge(hT_ready, t // 4 + 1)
                        mm = pe.matmul(lp[:, t * E0:(t + 1) * E0], hT[:, t * P:(t + 1) * P], gR[:, :], start=True, stop=True)
                    mm.then_inc(logit_done, 1)

                @block.vector
                def _(dve):
                    order = Order(dve, steps, 21)
                    aggregate(dve, order, k)
                    dve.sem_inc(varied, 1)
                    dve.wait_ge(std1, 1)
                    order(dve.reciprocal(rstd[:, :], small[:, 0, :]))
                    order(dve.tensor_tensor(small[:, 1, :], variances(k), rstd[:, :], ALU.mult))
                    order(dve.tensor_tensor(small[:, 1, :], small[:, 1, :], rstd[:, :], ALU.mult))
                    dve.sem_inc(varied, 1)
                    dve.tensor_scalar(gR[:, :], k.c["router"], k.c["rn_g"], None, ALU.mult).then_inc(gR_ready, 1)
                    for t in range(NT):
                        ins = dve.tensor_scalar(k.res[:, t * P:(t + 1) * P], k.xs[:, t * P:(t + 1) * P], k.mv[:, 2 * t:2 * t + 1],
                                                rstd[:, t:t + 1], ALU.subtract, ALU.mult)
                        if t % 4 == 3:
                            ins.then_inc(h_ready, 1)
                    dve.wait_ge(std2, 1)
                    order(dve.reciprocal(small[:, 3, :], small[:, 2, :]))
                    dve.wait_ge(logit_done, 1)
                    order(dve.tensor_copy(bR[:, :], bp[:, 0:E0]))
                    order(dve.tensor_tensor(lg[:, :, :], lp[:, 0:NT * E0].rearrange("p (t e) -> p t e", e=E0),
                                            small[:, 3, :].unsqueeze(2).to_broadcast([P, NT, E0]), ALU.mult))
                    order(dve.tensor_tensor(lg[:, :, :], lg[:, :, :], bR[:, :].unsqueeze(1).to_broadcast([P, NT, E0]), ALU.add))
                    order(dve.tensor_reduce(red[:, 0, :], lg[:, :, :], AX.X, ALU.max))
                    dve.tensor_tensor(lg[:, :, :], lg[:, :, :], red[:, 0, :].unsqueeze(2).to_broadcast([P, NT, E0]),
                                      ALU.subtract).then_inc(shifted, 1)
                    dve.wait_ge(exp_ready, 1)
                    order(dve.tensor_reduce(red[:, 1, :], lg[:, :, :], AX.X, ALU.add))
                    order(dve.reciprocal(red[:, 1, :], red[:, 1, :]))
                    dve.wait_ge(filled, 1)
                    order(dve.tensor_tensor(score[:, :, 0:E0], lg[:, :, :], red[:, 1, :].unsqueeze(2).to_broadcast([P, NT, E0]), ALU.mult))
                    top_experts(dve, order, filled, score, picked, values, comb[:, :, :], E0, 2, 6)
                    order(dve.tensor_reduce(red[:, 2, :], comb[:, :, :], AX.X, ALU.add))
                    order(dve.tensor_scalar(red[:, 2, :], red[:, 2, :], 1e-8, None, ALU.add))
                    order(dve.reciprocal(red[:, 2, :], red[:, 2, :]))
                    order(dve.tensor_tensor(comb[:, :, :], comb[:, :, :], red[:, 2, :].unsqueeze(2).to_broadcast([P, NT, E0]), ALU.mult))
                    order.end()

        xq, hT, z, aT = sb("h", [P, P]), sb("hT", [P, P]), sb("hidden_n", [P, E0, H0]), sb("hidden_T", [P, N8, P])
        st4, mv4, std4, r4 = sb("st4", [P, E0, 6]), sb("mv4", [P, E0, 2]), sb("std4", [P, E0]), sb("rstd4", [P, E0])
        acc, y, so, mo, stdo, ro = (sb("mixed", [P, P]), sb("mixed_n", [P, P]), sb("sto", [P, 6]), sb("mvo", [P, 2]),
                                    sb("stdo", [P, 1]), sb("rstdo", [P, 1]))
        tp, hp, zp, op = psum("turn_bank", [P, 512]), psum("hidden_p", [P, 2, 512]), psum("z_turned", [P, 2, 512]), psum("out_p", [P, 512])
        x_ready, x_turned, xT_ready, hid_done, var_ready, std_ready = (
            sem(n) for n in ("x_ready", "x_turned", "xT_ready", "hid_done", "var_ready", "std_ready"))
        z_ready, z_turned, a_ready, out_done, steps = (sem(n) for n in ("z_ready", "z_turned", "a_ready", "out_done", "tile_steps"))
        mixed, ovar_ready, ostd_ready, msteps, x_added = (sem(n) for n in ("mixed", "ovar_ready", "ostd_ready", "mix_steps", "x_added"))
        with nc.Block() as block:
            @block.vector
            def _(dve):
                def norm_in(i):
                    dve.wait_ge(x_turned, i)
                    dve.tensor_scalar(xq[:, :], k.xs[:, tile(i)], k.mv[:, bass.ds(2 * i, 1)], rstd[:, bass.ds(i, 1)],
                                      ALU.subtract, ALU.mult).then_inc(x_ready, 1)

                def norm_hidden(i):
                    order = Order(dve, steps, 3, i)
                    dve.wait_ge(hid_done, i + 1)
                    for e in range(E0):
                        ins = dve.bn_stats(st4[:, e, :], hp[:, e // 2, e % 2 * H0:(e % 2 + 1) * H0])
                    order(ins)
                    settle(dve, k)
                    for e in range(E0):
                        ins = dve.bn_aggr(mv4[:, e, :], st4[:, e, :])
                    order(ins)
                    dve.sem_inc(var_ready, 1)
                    dve.wait_ge(std_ready, i + 1)
                    order(dve.reciprocal(r4[:, :], std4[:, :]))
                    order.end()
                    dve.wait_ge(z_turned, i)
                    for e in range(E0):
                        ins = dve.tensor_scalar(z[:, e, :], hp[:, e // 2, e % 2 * H0:(e % 2 + 1) * H0], mv4[:, e, 0:1],
                                                r4[:, e:e + 1], ALU.subtract, ALU.mult)
                    ins.then_inc(z_ready, 1)

                def mix(i):
                    order = Order(dve, msteps, 9, i)
                    dve.wait_ge(out_done, i + 1)
                    order(dve.tensor_scalar(acc[:, :], op[:, 0:P], comb_of(i, 0), None, ALU.mult))
                    for e in range(1, E0):
                        order(dve.scalar_tensor_tensor(acc[:, :], op[:, e * P:(e + 1) * P], comb_of(i, e), acc[:, :], ALU.mult, ALU.add))
                    dve.sem_inc(mixed, 1)
                    order(dve.bn_stats(so[:, :], acc[:, :]))
                    settle(dve, k)
                    order(dve.bn_aggr(mo[:, :], so[:, :]))
                    dve.sem_inc(ovar_ready, 1)
                    dve.wait_ge(ostd_ready, i + 1)
                    order(dve.reciprocal(ro[:, :], stdo[:, :]))
                    order(dve.tensor_scalar(y[:, :], acc[:, :], mo[:, 0:1], ro[:, :], ALU.subtract, ALU.mult))
                    order(dve.tensor_tensor(y[:, :], y[:, :], k.row("on_g"), ALU.mult))
                    order.end()
                    dve.tensor_tensor(y[:, :], y[:, :], k.row("on_b"), ALU.add).then_inc(x_added, 1)
                    dve.wait_ge(x_added, 2 * i + 1)
                    dve.tensor_tensor(k.xs[:, tile(i)], k.xs[:, tile(i)], y[:, :], ALU.add).then_inc(x_added, 1)
                    dve.wait_ge(x_added, 2 * i + 2)
                    dve.bn_stats(k.st[:, bass.ds(6 * i, 6)], k.xs[:, tile(i)])

                def comb_of(i, e):
                    return comb[:, :, :].rearrange("p t e -> p (t e)")[:, bass.ds(E0 * i + e, 1)]

                norm_in(0)
                norm_in(1)
                norm_hidden(0)
                with dve.Fori(1, NT - 1) as i:
                    norm_in(i + 1)
                    norm_hidden(i)
                    mix(i - 1)
                norm_hidden(NT - 1)
                mix(NT - 2)
                mix(NT - 1)

            @block.scalar
            def _(act):
                def front(i):
                    act.wait_ge(x_turned, i + 1)
                    act.wait_ge(hid_done, i)
                    act.activation(hT[:, :], tp[:, 0:P], ACT.Copy).then_inc(xT_ready, 1)

                def std(i):
                    act.wait_ge(var_ready, i + 1)
                    act.activation(std4[:, :], mv4[:, :, 1], ACT.Sqrt, bias=k.eps[:, :]).then_inc(std_ready, 1)

                def gains(i):
                    act.wait_ge(out_done, i)
                    for n in range(N8):
                        if n % 4 == 0:
                            act.wait_ge(z_turned, i + 1)
                        ins = act.activation(aT[:, n, :], zp[:, n // 4, n % 4 * P:(n % 4 + 1) * P], ACT.Relu,
                                             bias=k.c["lnb"][:, n:n + 1], scale=k.c["lng"][:, n:n + 1])
                    ins.then_inc(a_ready, 1)

                def ostd(i):
                    act.wait_ge(ovar_ready, i + 1)
                    act.activation(stdo[:, :], mo[:, 1:2], ACT.Sqrt, bias=k.eps[:, :]).then_inc(ostd_ready, 1)

                front(0)
                front(1)
                std(0)
                with act.Fori(1, NT - 1) as i:
                    gains(i - 1)
                    front(i + 1)
                    std(i)
                    ostd(i - 1)
                gains(NT - 2)
                std(NT - 1)
                gains(NT - 1)
                ostd(NT - 2)
                ostd(NT - 1)

            @block.tensor
            def _(pe):
                def front(i):
                    pe.wait_ge(x_ready, i + 1)
                    pe.wait_ge(xT_ready, i)
                    pe.transpose(tp[:, 0:P], xq[:, :], k.c["ident"]).then_inc(x_turned, 1)

                def hidden(i):
                    pe.wait_ge(xT_ready, i + 1)
                    pe.wait_ge(z_ready, i)
                    for h in range(2):
                        mm = pe.matmul(hp[:, h, :], hT[:, :], k.c["w1"][:, h * 512:(h + 1) * 512], start=True, stop=True)
                    mm.then_inc(hid_done, 1)

                def turn(i):
                    pe.wait_ge(z_ready, i + 1)
                    pe.wait_ge(a_ready, i)
                    zf = z[:, :, :].rearrange("p e h -> p (e h)")
                    for n in range(N8):
                        mm = pe.transpose(zp[:, n // 4, n % 4 * P:(n % 4 + 1) * P], zf[:, n * P:(n + 1) * P], k.c["ident"])
                    mm.then_inc(z_turned, 1)

                def down(i):
                    pe.wait_ge(a_ready, i + 1)
                    pe.wait_ge(mixed, i)
                    for e in range(E0):
                        for j in range(2):
                            n = 2 * e + j
                            mm = pe.matmul(op[:, e * P:(e + 1) * P], aT[:, n, :], k.c["w2"][:, n * P:(n + 1) * P],
                                           start=j == 0, stop=j == 1)
                    mm.then_inc(out_done, 1)

                front(0)
                hidden(0)
                front(1)
                turn(0)
                with pe.Fori(1, NT - 1) as i:
                    hidden(i)
                    front(i + 1)
                    down(i - 1)
                    turn(i)
                hidden(NT - 1)
                down(NT - 2)
                turn(NT - 1)
                down(NT - 1)


def feed_forward(nc, k):
    NB = FF // P
    sem = lambda name: k.sem(f"f_{name}")
    with ExitStack() as ctx:
        def sb(name, shape, dt=F32):
            return ctx.enter_context(nc.sbuf_tensor(f"f_{name}", shape, dt))

        def psum(name, shape):
            return ctx.enter_context(nc.psum_tensor(f"f_{name}", shape, F32))

        std, rstd = sb("std", [P, NT]), sb("rstd", [P, NT])
        xn, xq, xT, gT = sb("normal", [P, P]), sb("y", [P, P]), sb("yT", [P, P]), sb("innerT", [P, NB, P])
        tp, ip, op = psum("turn_bank", [P, 512]), psum("inner_p", [P, 2, 512]), psum("out_p", [P, 2, 512])
        stats, std_made, made, own = sem("stats"), sem("std_made"), sem("rstd_made"), sem("tile_steps")
        x_ready, x_turned, xT_ready, in_done, g_ready, out_done, summed = (
            sem(n) for n in ("x_ready", "x_turned", "xT_ready", "in_done", "g_ready", "out_done", "summed"))
        end_steps, var_ready, end_std = sem("end_steps"), sem("var_ready"), sem("end_std")
        stored, loaded, x_final = sem("stored"), sem("loaded"), sem("x_final")
        with nc.Block() as block:
            @block.vector
            def _(dve):
                aggregate(dve, Order(dve, stats, 1), k)
                dve.wait_ge(std_made, 1)
                dve.reciprocal(rstd[:, :], std[:, :]).then_inc(made, 1)
                dve.wait_ge(made, 1)

                def norm_in(i):
                    dve.wait_ge(x_turned, i)
                    order = Order(dve, own, 2, i)
                    order(dve.tensor_scalar(xn[:, :], k.rs[:, tile(i)], k.mv[:, bass.ds(2 * i, 1)], rstd[:, bass.ds(i, 1)],
                                            ALU.subtract, ALU.mult))
                    order(dve.tensor_tensor(xn[:, :], xn[:, :], k.row("so_g"), ALU.mult))
                    order.end()
                    dve.tensor_tensor(k.res[:, tile(i)], xn[:, :], k.row("so_be"), ALU.add)
                    dve.tensor_tensor(xq[:, :], xn[:, :], k.row("so_be"), ALU.add).then_inc(x_ready, 1)

                def add_out(i, j):
                    dve.wait_ge(out_done, i + 1)
                    dve.tensor_tensor(k.rs[:, tile(i)], op[:, j, 0:P], k.res[:, tile(i)], ALU.add).then_inc(summed, 1)
                    dve.wait_ge(summed, i + 1)
                    dve.bn_stats(k.st[:, bass.ds(6 * i, 6)], k.rs[:, tile(i)])

                norm_in(0)
                norm_in(1)
                with dve.Fori(0, NT // 2 - 1) as m:
                    for j in range(2):
                        add_out(2 * m + j, j)
                        norm_in(2 * m + j + 2)
                for j in range(2):
                    add_out(NT - 2 + j, j)

            @block.scalar
            def _(act):
                act.wait_ge(stats, 1)
                act.activation(std[:, :], variances(k), ACT.Sqrt, bias=k.eps[:, :]).then_inc(std_made, 1)

                def turned(i):
                    act.wait_ge(x_turned, i + 1)
                    act.wait_ge(in_done, i)
                    act.activation(xT[:, :], tp[:, 0:P], ACT.Copy).then_inc(xT_ready, 1)

                def inner(i, j):
                    act.wait_ge(out_done, i)
                    for n in range(NB):
                        if n == 0:
                            act.wait_ge(in_done, i + 1)
                        ins = act.activation(gT[:, n, :], ip[:, j, n * P:(n + 1) * P], ACT.Gelu, bias=k.c["fi_b"][:, n:n + 1])
                    ins.then_inc(g_ready, 1)

                turned(0)
                with act.Fori(0, NT // 2 - 1) as m:
                    for j in range(2):
                        turned(2 * m + j + 1)
                        inner(2 * m + j, j)
                turned(NT - 1)
                inner(NT - 2, 0)
                inner(NT - 1, 1)

            @block.tensor
            def _(pe):
                def front(i, j):
                    pe.wait_ge(x_ready, i + 1)
                    pe.wait_ge(xT_ready, i)
                    pe.transpose(tp[:, 0:P], xq[:, :], k.c["ident"]).then_inc(x_turned, 1)
                    pe.wait_ge(xT_ready, i + 1)
                    for n in range(NB):
                        mm = pe.matmul(ip[:, j, n * P:(n + 1) * P], k.c["fi"][:, n * P:(n + 1) * P], xT[:, :], start=True, stop=True)
                    mm.then_inc(in_done, 1)

                def down(i, j):
                    pe.wait_ge(g_ready, i + 1)
                    pe.matmul(op[:, j, 0:P], k.ones[0:1, :], k.row("fo_b")[0:1, :], start=True, stop=False)
                    for n in range(NB):
                        mm = pe.matmul(op[:, j, 0:P], gT[:, n, :], k.c["fo"][:, n * P:(n + 1) * P], start=False, stop=n == NB - 1)
                    mm.then_inc(out_done, 1)

                front(0, 0)
                front(1, 1)
                with pe.Fori(0, NT // 2 - 1) as m:
                    for j in range(2):
                        i = 2 * m + j
                        pe.wait_ge(summed, i)
                        down(i, j)
                        front(i + 2, j)
                pe.wait_ge(summed, NT - 2)
                down(NT - 2, 0)
                down(NT - 1, 1)

        with nc.Block() as block:
            all3 = lambda ap: ap[:, :].rearrange("p (t d) -> p t d", d=P)
            rows3 = lambda name: k.row(name).unsqueeze(1).to_broadcast([P, NT, P])

            @block.vector
            def _(dve):
                order = Order(dve, end_steps, 4)
                aggregate(dve, order, k)
                dve.sem_inc(var_ready, 1)
                dve.wait_ge(end_std, 1)
                order(dve.reciprocal(rstd[:, :], std[:, :]))
                for t in range(NT):
                    ins = dve.tensor_scalar(k.rs[:, t * P:(t + 1) * P], k.rs[:, t * P:(t + 1) * P], k.mv[:, 2 * t:2 * t + 1],
                                            rstd[:, t:t + 1], ALU.subtract, ALU.mult)
                order(ins)
                order(dve.tensor_tensor(all3(k.rs), all3(k.rs), rows3("fo_g"), ALU.mult))
                order.end()
                dve.tensor_tensor(all3(k.rs), all3(k.rs), rows3("fo_be"), ALU.add).then_inc(x_final, 1)
                dve.wait_ge(x_final, 1)
                dve.tensor_tensor(k.xs[:, :], k.xs[:, :], k.rs[:, :], ALU.add).then_inc(x_final, 1)

            @block.scalar
            def _(act):
                act.wait_ge(var_ready, 1)
                act.activation(std[:, :], variances(k), ACT.Sqrt, bias=k.eps[:, :]).then_inc(end_std, 1)

            @block.sync
            def _(sp):
                sp.wait_ge(x_final, 2)
                sp.dma_start(k.turn_dram.rearrange("(t b) s d -> (b s) t d", b=2), all3(k.xs)).then_inc(stored, 16)
                sp.wait_ge(stored, 16)
                load_turned(sp, k, k.turn_dram, loaded)
                sp.wait_ge(loaded, 64)


def load_turned(sp, k, src, loaded):
    for q in range(4):
        sp.dma_start(k.xe[32 * q:32 * q + 32, :].rearrange("p (g d) -> p g d", d=P),
                     src.rearrange("t (g q) d -> q t g d", q=4)[q]).then_inc(loaded, 16)


def memory_stage(nc, k):
    HD = NHM * DM
    NP2 = NHM // 2
    SCALE = 1.0 / np.sqrt(DM)
    sem = lambda name: k.sem(f"m_{name}")
    with ExitStack() as ctx:
        def sb(name, shape, dt=F32):
            return ctx.enter_context(nc.sbuf_tensor(f"m_{name}", shape, dt))

        std, rstd = sb("std", [P, NT]), sb("rstd", [P, NT])
        xq, hT = sb("h", [P, P]), sb("hT", [P, P])
        ex = sb("exp", [P, 2, 512])
        kq = sb("features", [P, NP2, 2, P])
        bs = sb("beta_sums", [P, 3 * NHM])
        eb, cc, sh = sb("exp_beta", [P, NHM]), sb("sigma_sums", [P, NHM]), sb("sums_kept", [P, 1])
        c = sb("c", [P, 2, NHM])
        clow = sb("c_low", [P, 2, NHM])
        rq = sb("q_scale", [P, 2, NHM])
        R = sb("rhs", [P, 2, NHM, DM])
        gm = sb("products", [P, 2, NHM, 2, P])
        X, Ym, cX, T = (sb(n, [P, NHM, 32]) for n in ("inverse", "masked", "c_inverse", "inverse_T"))
        Tb = sb("inverse_T_blocks", [P, 2, NHM, P])
        U0, V, U, on = (sb(n, [P, NHM, DM]) for n in ("u0", "v", "u", "out_rows"))
        oT = sb("outT", [P, NP2, P])
        F = ctx.enter_context(nc.psum_tensor("m_front", [P, 3, 512], F32))
        C = ctx.enter_context(nc.psum_tensor("m_chain", [P, 5, 512], F32))
        h32 = lambda ap: ap.rearrange("p (h n) -> p h n", n=32)
        h64 = lambda a: C[:, a:a + 2, :].rearrange("p b (h n) -> p (b h) n", n=DM)
        bc = lambda v, n: v.unsqueeze(2).to_broadcast([P, NHM, n])
        lvl = lambda j: k.c[f"lvl{j}"].unsqueeze(1).to_broadcast([P, NHM, 32])
        eye = k.c["eye32"].unsqueeze(1).to_broadcast([P, NHM, 32])
        masks = k.pack["cst"][:, 208:208 + 2 * P].rearrange("p (g t) -> p g t", g=2)
        ind2_on = k.pack["cst"][:, 464:560]
        assert [n for n, _ in PACKS["cst"]][3:6] == ["bd_strict", "bd_upper", "ind2"] and width(PACKS["cst"][:3]) == 208

        stats, std_made, made, cleared = sem("stats"), sem("std_made"), sem("rstd_made"), sem("cleared")
        x_ready, x_turned, hT_ready = sem("x_ready"), sem("x_turned"), sem("hT_ready")
        qk_done, ex_ready, clipped, kq_ready = sem("qk_done"), sem("ex_ready"), sem("clipped"), sem("kq_ready")
        v_done, sum_done, bs_ready, eb_ready, small, rhs_ready = (
            sem(n) for n in ("v_done", "sum_done", "bs_ready", "eb_ready", "small_steps", "rhs_ready"))
        ga_done, gm_ready, c_ready = sem("ga_done"), sem("gm_ready"), sem("c_ready")
        cx_ready, y_done, ysteps, ym_ready, z_done, X_ready, T_ready, Tb_ready = (
            sem(n) for n in ("cx_ready", "y_done", "y_steps", "ym_ready", "z_done", "X_ready", "T_ready", "Tb_ready"))
        u0_done, u0_ready, v1_ready, gy_done, v2_ready, xy_done, u_ready, cu_ready = (
            sem(n) for n in ("u0_done", "u0_ready", "v1_ready", "gy_done", "v2_ready", "xy_done", "u_ready", "cu_ready"))
        o_done, on_ready, oT_done, oT_ready, p_done, summed = (
            sem(n) for n in ("o_done", "on_ready", "oT_done", "oT_ready", "p_done", "summed"))

        FRONT = ["x", "qk0", "qk1", "qk2", "qk3", "v", "sum", "ga0", "ga1", "ga2", "ga3"]
        INVERT = ["y0", "y1", "z1", "y2", "z2", "y3", "z3"]
        APPLY = ["u0", "gy", "xy", "o", "oT", "proj"]
        PERIOD = ["u0", "gy", "x", "y0", "qk0", "qk1", "y1", "xy", "z1", "o", "qk2", "y2", "qk3", "z2", "oT", "v", "sum",
                  "y3", "ga0", "ga1", "z3", "ga2", "proj", "ga3"]
        assert sorted(PERIOD) == sorted(FRONT + INVERT + APPLY)

        schedule = lambda eng, steps: three_deep(eng, steps, PERIOD, APPLY, INVERT)
        block = ctx.enter_context(nc.Block())

        def wide(h, width, most):
            return slice(h, min(h + most, (h * width // 512 + 1) * 512 // width))

        @block.tensor
        def _(pe):
            def x(i, j):
                pe.wait_ge(x_ready, i + 1)
                pe.wait_ge(bs_ready, i)
                pe.transpose(F[:, 2, 0:P], xq[:, :], k.c["ident"]).then_inc(x_turned, 1)

            def qk(g):
                def step(i, j):
                    if g == 0:
                        pe.wait_ge(hT_ready, i + 1)
                        pe.wait_ge(gm_ready, 8 * i)
                    if g >= 2:
                        pe.wait_ge(kq_ready, 4 * i + g - 1)
                    w = k.c["mk"] if g % 2 == 0 else k.c["mq"]
                    for a in range(4):
                        n = 4 * (g // 2) + a
                        mm = pe.matmul(F[:, g % 2, a * P:(a + 1) * P], w[:, n * P:(n + 1) * P], hT[:, :], start=True, stop=True)
                    mm.then_inc(qk_done, 1)
                return step

            def v(i, j):
                pe.wait_ge(kq_ready, 4 * i + 4)
                for h in range(2):
                    pe.matmul(F[:, h, :], hT[:, :], k.c["mv"][:, h * 512:(h + 1) * 512], start=True, stop=True)
                pe.matmul(F[:, 2, P:P + NHM], hT[:, :], k.c["mbeta"], start=True, stop=True).then_inc(v_done, 1)

            def sums(i, j):
                for w in range(2):
                    for a in range(NP2):
                        at = P + NHM * (w + 1) + 2 * a
                        mm = pe.matmul(F[:, 2, at:at + 96], kq[:, a, w, :], ind2_on, start=True, stop=True)
                mm.then_inc(sum_done, 1)

            def ga(r):
                def step(i, j):
                    if r == 0:
                        pe.wait_ge(rhs_ready, i + 1)
                    else:
                        pe.wait_ge(gm_ready, 8 * i + 2 * r)
                    for h in range(2):
                        for a in range(2):
                            rows = slice(DM * h, DM * (h + 1))
                            mm = pe.matmul(F[:, h, a * 2 * P:(a + 1) * 2 * P], kq[rows, 2 * r + a, 0, :],
                                           kq[rows, 2 * r + a, :, :].rearrange("p w t -> p (w t)"), start=True, stop=True)
                        mm.then_inc(ga_done, 1)
                return step

            def y(l):
                def step(i, j):
                    pe.wait_ge(cx_ready, 4 * i + l + 1)
                    if l == 0:
                        pe.wait_ge(gm_ready, 8 * i + 8)
                    for h in range(NHM):
                        w = wide(h, 32, 3)
                        mm = pe.matmul(C[:, 0, 32 * w.start:32 * w.stop], gm[:, j, h, 0, :],
                                       cX[:, w, :].rearrange("p h n -> p (h n)"), start=True, stop=True)
                    mm.then_inc(y_done, 1)
                return step

            def z(l):
                def step(i, j):
                    pe.wait_ge(ym_ready, 3 * i + l)
                    pe.wait_ge(Tb_ready, 4 * i + l)
                    for h in range(NHM):
                        w = wide(h, 32, 3)
                        mm = pe.matmul(C[:, 1, 32 * w.start:32 * w.stop], Tb[:, j, h, :],
                                       Ym[:, w, :].rearrange("p h n -> p (h n)"), start=True, stop=True)
                    mm.then_inc(z_done, 1)
                return step

            def apply(at, left, right, done):
                for h in range(NHM):
                    w = wide(h, DM, 2)
                    mm = pe.matmul(C[:, at + h // 8, h % 8 * DM:(h % 8 + w.stop - h) * DM], left(h),
                                   right[:, w, :].rearrange("p h n -> p (h n)"), start=True, stop=True)
                mm.then_inc(done, 1)

            def u0(i, j):
                pe.wait_ge(Tb_ready, 4 * i + 4)
                pe.wait_ge(oT_ready, i)
                apply(2, lambda h: Tb[:, j, h, :], R[:, j, :, :], u0_done)

            def gy(i, j):
                pe.wait_ge(v1_ready, i + 1)
                apply(2, lambda h: gm[:, j, h, 0, :], V, gy_done)

            def xy(i, j):
                pe.wait_ge(v2_ready, i + 1)
                apply(2, lambda h: Tb[:, j, h, :], V, xy_done)

            def o(i, j):
                pe.wait_ge(cu_ready, i + 1)
                apply(2, lambda h: gm[:, j, h, 1, :], V, o_done)

            def oT_(i, j):
                pe.wait_ge(on_ready, i + 1)
                of = on[:, :, :].rearrange("p h n -> p (h n)")
                for a in range(NP2):
                    mm = pe.transpose(C[:, 2 + a // 4, a % 4 * P:(a % 4 + 1) * P], of[:, a * P:(a + 1) * P], k.c["ident"])
                mm.then_inc(oT_done, 1)

            def proj(i, j):
                pe.wait_ge(oT_ready, i + 1)
                pe.wait_ge(summed, i)
                for a in range(NP2):
                    mm = pe.matmul(C[:, 4, 0:P], oT[:, a, :], k.c["mo"][:, a * P:(a + 1) * P], start=a == 0, stop=a == NP2 - 1)
                mm.then_inc(p_done, 1)

            schedule(pe, {"x": x, "v": v, "sum": sums, "u0": u0, "gy": gy, "xy": xy, "o": o, "oT": oT_, "proj": proj,
                          **{f"qk{g}": qk(g) for g in range(4)}, **{f"ga{r}": ga(r) for r in range(4)},
                          **{f"y{l}": y(l) for l in range(4)}, **{f"z{l}": z(l) for l in range(1, 4)}})

        @block.scalar
        def _(act):
            act.wait_ge(stats, 1)
            act.activation(std[:, :], variances(k), ACT.Sqrt, bias=k.eps[:, :]).then_inc(std_made, 1)
            act.wait_ge(cleared, 1)

            def x(i, j):
                act.wait_ge(x_turned, i + 1)
                act.wait_ge(v_done, i)
                act.activation(hT[:, :], F[:, 2, 0:P], ACT.Copy).then_inc(hT_ready, 1)

            def qk(g):
                def step(i, j):
                    act.wait_ge(qk_done, 4 * i + g + 1)
                    if g >= 2:
                        act.wait_ge(kq_ready, 4 * i + g - 1)
                    else:
                        act.wait_ge(kq_ready, 4 * i)
                    act.activation(ex[:, g % 2, :], F[:, g % 2, :], ACT.Exp).then_inc(ex_ready, 1)
                return step

            def sums(i, j):
                act.wait_ge(bs_ready, i + 1)
                act.wait_ge(c_ready, i)
                act.activation(eb[:, :], bs[:, 0:NHM], ACT.Exp, scale=-1.0).then_inc(eb_ready, 1)

            def spread(n):
                def step(i, j):
                    act.wait_ge(T_ready, 4 * i + n)
                    if n == 1:
                        reused(act, xy_done, i - 1)
                    else:
                        act.wait_ge(z_done, 3 * i + n - 1)
                    for q in range(4):
                        r = slice(32 * q, 32 * q + 32)
                        ins = act.activation(Tb[r, j, :, r], T[r, :, :], ACT.Copy)
                    ins.then_inc(Tb_ready, 1)
                return step

            def gy(i, j):
                act.wait_ge(gy_done, i + 1)
                act.activation(V[:, :, :], h64(2), ACT.Copy, scale=k.c["rowhigh"]).then_inc(v2_ready, 1)

            def oT_(i, j):
                act.wait_ge(oT_done, i + 1)
                act.wait_ge(p_done, i)
                act.activation(oT[:, :, :], C[:, 2:4, :].rearrange("p b (a t) -> p (b a) t", t=P), ACT.Copy).then_inc(oT_ready, 1)

            schedule(act, {"x": x, "sum": sums, "gy": gy, "oT": oT_, "y0": spread(1), "z1": spread(2), "z2": spread(3),
                           "z3": spread(4), **{f"qk{g}": qk(g) for g in range(4)}})

        @block.gpsimd
        def _(pool):
            pool.memset(Tb[:, :, :, :], 0.0).then_inc(cleared, 1)

            def cx(l):
                def step(i, j):
                    if l == 0:
                        pool.wait_ge(c_ready, i + 1)
                    else:
                        pool.wait_ge(X_ready, 4 * i + l)
                    if l == 0:
                        pool.wait_ge(y_done, 4 * i)
                    else:
                        pool.wait_ge(y_done, 4 * i + l)
                    pool.tensor_tensor(cX[:, :, :], eye if l == 0 else X[:, :, :], bc(c[:, j, :], 32), ALU.mult).then_inc(cx_ready, 1)
                return step

            def u0(i, j):
                pool.wait_ge(u0_ready, i + 1)
                pool.wait_ge(o_done, i)
                pool.tensor_tensor(V[:, :, :], U0[:, :, :], bc(clow[:, j, :], DM), ALU.mult).then_inc(v1_ready, 1)

            def xy(i, j):
                pool.wait_ge(u_ready, i + 1)
                pool.tensor_tensor(V[:, :, :], U[:, :, :], bc(c[:, j, :], DM), ALU.mult).then_inc(cu_ready, 1)

            schedule(pool, {"u0": u0, "xy": xy, **{f"y{l}": cx(l) for l in range(4)}})

        @block.vector
        def _(dve):
            row_stats(dve, Order(dve, stats0 := sem("stats0"), 2), k, k.xe)
            dve.sem_inc(stats, 1)
            dve.wait_ge(std_made, 1)
            dve.reciprocal(rstd[:, :], std[:, :]).then_inc(made, 1)
            dve.wait_ge(made, 1)

            def x(i, j):
                dve.wait_ge(x_turned, i)
                for out in (k.rs[:, tile(i)], xq[:, :]):
                    ins = dve.tensor_scalar(out, k.xe[:, tile(i)], k.mv[:, bass.ds(2 * i, 1)], rstd[:, bass.ds(i, 1)],
                                            ALU.subtract, ALU.mult)
                ins.then_inc(x_ready, 1)

            def qk(g):
                def step(i, j):
                    dve.wait_ge(ex_ready, 4 * i + g + 1)
                    dve.tensor_scalar(ex[:, g % 2, :], ex[:, g % 2, :], 1.0, None, ALU.min).then_inc(clipped, 1)
                    dve.wait_ge(clipped, 4 * i + g + 1)
                    dve.wait_ge(ga_done, 8 * i)
                    n = 4 * (g // 2)
                    dve.scalar_tensor_tensor(kq[:, n:n + 4, g % 2, :], F[:, g % 2, :].rearrange("p (a t) -> p a t", t=P), 0.0,
                                             ex[:, g % 2, :].rearrange("p (a t) -> p a t", t=P), ALU.max, ALU.add).then_inc(kq_ready, 1)
                return step

            def sums(i, j):
                dve.wait_ge(sum_done, i + 1)
                dve.wait_ge(eb_ready, i)
                dve.tensor_copy(bs[:, :], F[:, 2, P:P + 3 * NHM]).then_inc(bs_ready, 1)
                dve.wait_ge(bs_ready, i + 1)
                sk, sq = bs[:, NHM:2 * NHM], bs[:, 2 * NHM:]
                dve.tensor_tensor(R[:, j, :, :], F[:, 0:2, :].rearrange("p b (h n) -> p (b h) n", n=DM), bc(sk, DM),
                                  ALU.mult).then_inc(rhs_ready, 1)
                order = Order(dve, small, 6, i)
                order(dve.reciprocal(rq[:, j, :], sq))
                order(dve.tensor_scalar(rq[:, j, :], rq[:, j, :], float(SCALE), None, ALU.mult))
                dve.wait_ge(eb_ready, i + 1)
                order(dve.tensor_scalar(cc[:, :], eb[:, :], 1.0, None, ALU.add))
                order(dve.tensor_tensor(cc[:, :], cc[:, :], sk, ALU.mult))
                order(dve.tensor_tensor(cc[:, :], cc[:, :], sk, ALU.mult))
                order(dve.reciprocal(c[:, j, :], cc[:, :]))
                order.end()
                dve.tensor_scalar(clow[:, j, :], c[:, j, :], k.c["rowlow"], None, ALU.mult).then_inc(c_ready, 1)

            def ga(r):
                def step(i, j):
                    for h in range(2):
                        dve.wait_ge(ga_done, 8 * i + 2 * r + h + 1)
                        out = gm[:, j, 4 * r + h:4 * r + 4:2, :, :]
                        dve.tensor_tensor(out, F[:, h, :].rearrange("p (a g t) -> p a g t", a=2, g=2),
                                          masks.unsqueeze(1).to_broadcast([P, 2, 2, P]), ALU.mult).then_inc(gm_ready, 1)
                return step

            def y(l):
                def step(i, j):
                    dve.wait_ge(y_done, 4 * i + l + 1)
                    if l:
                        dve.wait_ge(z_done, 3 * i + l - 1)
                        dve.tensor_tensor(Ym[:, :, :], h32(C[:, 0, :]), lvl(l), ALU.mult).then_inc(ym_ready, 1)
                    else:
                        dve.tensor_tensor(Ym[:, :, :], h32(C[:, 0, :]), lvl(0), ALU.mult).then_inc(ysteps, 1)
                        dve.wait_ge(ysteps, i + 1)
                        dve.tensor_tensor(X[:, :, :], eye, Ym[:, :, :], ALU.subtract).then_inc(X_ready, 1)
                        turn(1, i)
                return step

            def turn(n, i):
                dve.wait_ge(X_ready, 4 * i + n)
                dve.wait_ge(Tb_ready, 4 * i + n - 1)
                dve.transpose(T[:, :, :], X[:, :, :]).then_inc(T_ready, 1)

            def z(l):
                def step(i, j):
                    dve.wait_ge(z_done, 3 * i + l)
                    dve.wait_ge(cx_ready, 4 * i + l + 1)
                    dve.tensor_tensor(X[:, :, :], X[:, :, :], h32(C[:, 1, :]), ALU.subtract).then_inc(X_ready, 1)
                    turn(l + 1, i)
                return step

            def u0(i, j):
                dve.wait_ge(u0_done, i + 1)
                dve.tensor_copy(U0[:, :, :], h64(2)).then_inc(u0_ready, 1)

            def xy(i, j):
                dve.wait_ge(xy_done, i + 1)
                dve.tensor_tensor(U[:, :, :], U0[:, :, :], h64(2), ALU.subtract).then_inc(u_ready, 1)

            def o(i, j):
                dve.wait_ge(o_done, i + 1)
                dve.tensor_tensor(on[:, :, :], h64(2), bc(rq[:, j, :], DM), ALU.mult).then_inc(on_ready, 1)

            def proj(i, j):
                dve.wait_ge(p_done, i + 1)
                dve.tensor_tensor(k.rs[:, tile(i)], C[:, 4, 0:P], k.rs[:, tile(i)], ALU.add).then_inc(summed, 1)
                dve.wait_ge(summed, i + 1)
                dve.bn_stats(k.st[:, bass.ds(6 * i, 6)], k.rs[:, tile(i)])

            schedule(dve, {"x": x, "sum": sums, "u0": u0, "xy": xy, "o": o, "proj": proj,
                           **{f"qk{g}": qk(g) for g in range(4)}, **{f"ga{r}": ga(r) for r in range(4)},
                           **{f"y{l}": y(l) for l in range(4)}, **{f"z{l}": z(l) for l in range(1, 4)}})

    memory_end(nc, k)


def memory_end(nc, k):
    sem = lambda name: k.sem(f"n_{name}")
    with nc.sbuf_tensor("n_std", [P, NT], F32) as std, nc.sbuf_tensor("n_rstd", [P, NT], F32) as rstd:
        steps, var_ready, std_made = sem("steps"), sem("var_ready"), sem("std_made")
        all3 = lambda ap: ap[:, :].rearrange("p (t d) -> p t d", d=P)
        rows3 = lambda name: k.row(name).unsqueeze(1).to_broadcast([P, NT, P])
        with nc.Block() as block:
            @block.vector
            def _(dve):
                order = Order(dve, steps, 5)
                aggregate(dve, order, k)
                dve.sem_inc(var_ready, 1)
                dve.wait_ge(std_made, 1)
                order(dve.reciprocal(rstd[:, :], std[:, :]))
                for t in range(NT):
                    ins = dve.tensor_scalar(k.rs[:, t * P:(t + 1) * P], k.rs[:, t * P:(t + 1) * P], k.mv[:, 2 * t:2 * t + 1],
                                            rstd[:, t:t + 1], ALU.subtract, ALU.mult)
                order(ins)
                order(dve.tensor_tensor(all3(k.rs), all3(k.rs), rows3("m_g"), ALU.mult))
                order(dve.tensor_tensor(all3(k.rs), all3(k.rs), rows3("m_b"), ALU.add))
                order.end()
                dve.tensor_tensor(k.xe[:, :], k.xe[:, :], k.rs[:, :], ALU.add)

            @block.scalar
            def _(act):
                act.wait_ge(var_ready, 1)
                act.activation(std[:, :], variances(k), ACT.Sqrt, bias=k.eps[:, :]).then_inc(std_made, 1)


def shared_experts_stage(nc, k):
    NA = E1 + 1
    sem = lambda name: k.sem(f"s_{name}")
    with ExitStack() as ctx:
        def sb(name, shape, dt=F32):
            return ctx.enter_context(nc.sbuf_tensor(f"s_{name}", shape, dt))

        xT = sb("xT", [P, B * S])
        comb = sb("weights", [P, NT, NE])
        acc = k.xs
        with ExitStack() as inner:
            def isb(name, shape):
                return inner.enter_context(nc.sbuf_tensor(f"s_{name}", shape, F32))

            lg, score, picked = isb("logits", [P, NT, E1]), isb("scores", [P, NT, E1 + 5]), isb("picked", [P, NT, E1 + 5])
            values, red, b2, combT = isb("values", [P, NT, 8]), isb("reduced", [P, 3, NT]), isb("b2", [NA, P]), isb("weightsT", [NA, NT, P])
            std, rstd = isb("std", [P, NT]), isb("rstd", [P, NT])
            varied, std_made, norm_steps, xn_ready = (sem(n) for n in ("varied", "std_made", "norm_steps", "xn_ready"))
            turned = inner.enter_context(nc.psum_tensor("s_turned_p", [P, 4, 512], F32))
            lp = inner.enter_context(nc.psum_tensor("s_logit_p", [P, 512], F32))
            filled, steps, turned_s, xT_ready, logit_done, shifted, exp_ready, b2_loaded = (
                sem(n) for n in ("filled", "router_steps", "rows_turned", "xT_ready", "logit_done", "shifted", "exp_ready", "b2_loaded"))
            comb_ready, combT_done, combT_ready, bias_done, acc_ready = (
                sem(n) for n in ("comb_ready", "combT_done", "combT_ready", "bias_done", "acc_ready"))
            with nc.Block() as block:
                @block.sync
                def _(sp):
                    sp.dma_start(b2[:, :], k.dram["b2"]).then_inc(b2_loaded, 16)

                @block.gpsimd
                def _(pool):
                    pool.memset(score[:, :, :], -1.0).then_inc(filled, 1)
                    pool.memset(comb[:, :, :], 1.0).then_inc(filled, 1)

                @block.scalar
                def _(act):
                    act.wait_ge(varied, 2)
                    act.activation(std[:, :], variances(k), ACT.Sqrt, bias=k.eps[:, :]).then_inc(std_made, 1)
                    for c in range(4):
                        act.wait_ge(turned_s, c + 1)
                        act.activation(xT[:, c * 512:(c + 1) * 512], turned[:, c, :], ACT.Copy).then_inc(xT_ready, 1)
                    act.wait_ge(shifted, 1)
                    act.activation(lg[:, :, :], lg[:, :, :], ACT.Exp).then_inc(exp_ready, 1)
                    for c in range(4):
                        act.wait_ge(combT_done, c + 1)
                        act.activation(combT[:, 4 * c:4 * c + 4, :], turned[0:NA, c, :].rearrange("p (t n) -> p t n", n=P),
                                       ACT.Copy).then_inc(combT_ready, 1)

                @block.tensor
                def _(pe):
                    for t in range(NT):
                        if t % 4 == 0:
                            pe.wait_ge(xn_ready, t // 4 + 1)
                        mm = pe.transpose(turned[:, t // 4, t % 4 * P:(t % 4 + 1) * P], k.rs[:, t * P:(t + 1) * P], k.c["ident"])
                        if t % 4 == 3:
                            mm.then_inc(turned_s, 1)
                    for t in range(NT):
                        if t % 4 == 0:
                            pe.wait_ge(xT_ready, t // 4 + 1)
                        mm = pe.matmul(lp[:, t * E1:(t + 1) * E1], xT[:, t * P:(t + 1) * P], k.c["gate"], start=True, stop=True)
                    mm.then_inc(logit_done, 1)
                    pe.wait_ge(comb_ready, 1)
                    for t in range(NT):
                        mm = pe.matmul(turned[0:NA, t // 4, t % 4 * P:(t % 4 + 1) * P], comb[:, t, 0:NA], k.c["ident"], start=True, stop=True)
                        if t % 4 == 3:
                            mm.then_inc(combT_done, 1)
                    pe.wait_ge(b2_loaded, 16)
                    for t in range(NT):
                        if t % 4 == 0:
                            pe.wait_ge(combT_ready, t // 4 + 1)
                        mm = pe.matmul(turned[:, t // 4, t % 4 * P:(t % 4 + 1) * P], combT[:, t, :], b2[:, :], start=True, stop=True)
                        if t % 4 == 3:
                            mm.then_inc(bias_done, 1)

                @block.vector
                def _(dve):
                    row_stats(dve, Order(dve, varied, 2), k, k.xe)
                    norm = Order(dve, norm_steps, 1)
                    dve.wait_ge(std_made, 1)
                    norm(dve.reciprocal(rstd[:, :], std[:, :]))
                    for t in range(NT):
                        ins = dve.tensor_scalar(k.rs[:, t * P:(t + 1) * P], k.xe[:, t * P:(t + 1) * P], k.mv[:, 2 * t:2 * t + 1],
                                                rstd[:, t:t + 1], ALU.subtract, ALU.mult)
                        if t % 4 == 3:
                            ins.then_inc(xn_ready, 1)
                    order = Order(dve, steps, 13)
                    dve.wait_ge(logit_done, 1)
                    l3 = lp[:, 0:NT * E1].rearrange("p (t e) -> p t e", e=E1)
                    over = lambda n: red[:, n, :].unsqueeze(2).to_broadcast([P, NT, E1])
                    order(dve.tensor_reduce(red[:, 0, :], l3, AX.X, ALU.max))
                    dve.tensor_tensor(lg[:, :, :], l3, over(0), ALU.subtract).then_inc(shifted, 1)
                    dve.wait_ge(exp_ready, 1)
                    order(dve.tensor_reduce(red[:, 1, :], lg[:, :, :], AX.X, ALU.add))
                    order(dve.reciprocal(red[:, 1, :], red[:, 1, :]))
                    dve.wait_ge(filled, 2)
                    order(dve.tensor_tensor(score[:, :, 0:E1], lg[:, :, :], over(1), ALU.mult))
                    top_experts(dve, order, filled, score, picked, values, lg[:, :, :], E1, 3, 5)
                    order(dve.tensor_reduce(red[:, 2, :], lg[:, :, :], AX.X, ALU.add))
                    order(dve.tensor_scalar(red[:, 2, :], red[:, 2, :], 1e-20, None, ALU.add))
                    order(dve.reciprocal(red[:, 2, :], red[:, 2, :]))
                    dve.tensor_tensor(comb[:, :, 0:E1], lg[:, :, :], over(2), ALU.mult).then_inc(comb_ready, 1)
                    order(dve.memset(k.unused[:, :], 0.0))
                    order.end()
                    for c in range(4):
                        dve.wait_ge(bias_done, c + 1)
                        r = slice(c * 512, (c + 1) * 512)
                        dve.tensor_tensor(acc[:, r], turned[:, c, :], k.xe[:, r], ALU.add).then_inc(acc_ready, 1)

        WX = width(EXW)
        ew, w2 = sb("expert_weights", [P, 2, WX]), sb("down_weights", [P, 2, P])
        gl, a = sb("gates", [P, 2, 512]), sb("gated", [P, 2, 512])
        up = ctx.enter_context(nc.psum_tensor("s_up", [P, 2, 2, 512], F32))
        dn = ctx.enter_context(nc.psum_tensor("s_down", [P, 2, 512], F32))
        e_loaded = [sem(f"expert_loaded{j}") for j in range(2)]
        w2_ready, up_done, g_ready, a_ready, dn_done, mixed, out_stored = (
            sem(n) for n in ("w2_ready", "up_done", "g_ready", "a_ready", "dn_done", "mixed", "out_stored"))
        w = [fields_of(ew[:, j, :], EXW) for j in range(2)]
        flat = comb[:, :, :].rearrange("p t e -> p (t e)")

        def experts(eng, step):
            with eng.Fori(0, NE // 2) as m:
                for j in range(2):
                    step(m, j, False)
            step(NE // 2, 0, True)

        with nc.Block() as block:
            @block.sync
            def _(sp):
                for e in range(2):
                    sp.dma_start(ew[:, e, :], k.dram["experts"][e]).then_inc(e_loaded[e], 16)

                def load(e, j):
                    sp.wait_ge(dn_done, 4 * e + 4)
                    sp.wait_ge(a_ready, 4 * e + 4)
                    sp.dma_start(ew[:, j, :], k.dram["experts"][bass.ds(e + 2, 1), :, :].rearrange("e p w -> p (e w)")).then_inc(e_loaded[j], 16)

                with sp.Fori(0, NE // 2 - 1) as m:
                    for j in range(2):
                        load(2 * m + j, j)
                load(NE - 3, 0)
                sp.wait_ge(mixed, 4 * NE)
                for q in range(4):
                    sp.dma_start(k.out.rearrange("t (g q) d -> q t g d", q=4)[q],
                                 acc[32 * q:32 * q + 32, :].rearrange("p (g d) -> p g d", d=P)).then_inc(out_stored, 16)
                sp.wait_ge(out_stored, 64)

            @block.gpsimd
            def _(pool):
                def step(m, j, used):
                    e = 2 * m + j
                    if used:
                        pool.wait_ge(dn_done, 4 * e - 4)
                    pool.wait_ge(e_loaded[j], 16 * (m + 1))
                    pool.tensor_tensor(w2[:, j, :], w[j]["fc2"], w[j]["mult"].to_broadcast([P, P]), ALU.mult).then_inc(w2_ready, 1)

                for j in range(2):
                    step(0, j, False)
                with pool.Fori(1, NE // 2) as m:
                    for j in range(2):
                        step(m, j, True)
                step(NE // 2, 0, True)

            @block.scalar
            def _(act):
                def step(m, j, last):
                    e = 2 * m + j
                    for c in range(4):
                        act.wait_ge(up_done, 4 * e + c + 1)
                        act.activation(gl[:, c % 2, :], up[:, c % 2, 1, :], ACT.Gelu, bias=w[j]["b1"][:, 1:2]).then_inc(g_ready, 1)

                experts(act, step)

            @block.tensor
            def _(pe):
                def project_up(m, j, c):
                    if c == 0:
                        pe.wait_ge(e_loaded[j], 16 * (m + 1))
                    for h in range(2):
                        mm = pe.matmul(up[:, c % 2, h, :], w[j]["fc1"][:, h * F1:(h + 1) * F1], xT[:, c * 512:(c + 1) * 512],
                                       start=True, stop=True)
                    mm.then_inc(up_done, 1)

                def step(m, j, last):
                    e = 2 * m + j
                    for c in range(4):
                        if not (last and c == 3):
                            pe.wait_ge(a_ready, 4 * e + c)
                            if c < 3:
                                project_up(m, j, c + 1)
                            else:
                                project_up(m + j, 1 - j, 0)
                        pe.wait_ge(a_ready, 4 * e + c + 1)
                        pe.wait_ge(w2_ready, e + 1)
                        pe.wait_ge(mixed, 4 * e + c)
                        for q in range(4):
                            mm = pe.matmul(dn[:, c % 2, q * P:(q + 1) * P], a[:, c % 2, q * P:(q + 1) * P], w2[:, j, :],
                                           start=True, stop=True)
                        mm.then_inc(dn_done, 1)

                project_up(0, 0, 0)
                experts(pe, step)

            @block.vector
            def _(dve):
                def step(m, j, last):
                    e = 2 * m + j
                    for c in range(4):
                        s = 4 * e + c
                        dve.wait_ge(g_ready, s + 1)
                        dve.scalar_tensor_tensor(a[:, c % 2, :], up[:, c % 2, 0, :], w[j]["b1"][:, 0:1], gl[:, c % 2, :],
                                                 ALU.add, ALU.mult).then_inc(a_ready, 1)
                        dve.wait_ge(dn_done, s + 1)
                        for q in range(4):
                            t = 4 * c + q
                            r = slice(t * P, (t + 1) * P)
                            ins = dve.scalar_tensor_tensor(acc[:, r], dn[:, c % 2, q * P:(q + 1) * P], flat[:, bass.ds(t * NE + e, 1)],
                                                           acc[:, r], ALU.mult, ALU.add)
                        ins.then_inc(mixed, 1)

                experts(dve, step)


def build(nc, dram, out):
    with ExitStack() as ctx:
        def sb(name, shape, dt=F32):
            return ctx.enter_context(nc.sbuf_tensor(f"all_{name}", shape, dt))

        k = Shared()
        k.dram, k.out = dram, out
        taken = []

        def sem(name):
            taken.append(nc.alloc_semaphore(name=name))
            return taken[-1]

        def stage(part, *args):
            part(nc, k, *args)
            nc.clear_and_free_semaphores(taken)
            nc.all_engine_barrier()
            taken.clear()

        k.sem = sem
        k.pack = {name: sb(f"pack_{name}", [P, width(f)]) for name, f in PACKS.items()}
        k.c = {}
        for name, f in PACKS.items():
            k.c.update(fields_of(k.pack[name], f))
        k.rows = sb("rows", [P, len(ROWS) * P])
        k.row = lambda name: k.rows[:, ROWS.index(name) * P:(ROWS.index(name) + 1) * P]
        k.xs = sb("x_tiles", [P, NT * P])
        k.res = sb("residual_tiles", [P, NT * P])
        k.rs = sb("sum_tiles", [P, NT * P])
        k.st = sb("six_tuples", [P, 6 * NT])
        k.mv = sb("mean_var", [P, 2 * NT])
        k.ones = sb("ones", [P, P])
        k.eps = sb("eps", [P, 1])
        k.unused = sb("unused", [P, 1])
        k.ones3 = sb("ones3", [P, P], BF16)
        k.identb = sb("identb", [P, P], BF16)
        k.pick3 = sb("pick3", [P, 32], BF16)
        k.hm = sb("head_scale", [P, NH])
        k.mask3_a = sb("mask3_a", [3, B * SC], BF16)
        k.mask3_d = sb("mask3_d", [3, B * SC], BF16)
        k.mask = sb("mask", [B, SC])
        k.mtmp = sb("mask_rest", [B, 2, SC])
        k.split_a = sb("mask_split_a", [B, 3, SC], BF16)
        k.split_d = sb("mask_split_d", [B, 3, SC], BF16)
        k.xe = k.res
        k.turn_dram = nc.dram_tensor("turned_rows", (B, S, P), F32).ap()
        k.early_loaded, k.late_loaded, k.const_made, k.const_ordered, k.mask_moved = (
            ctx.enter_context(nc.semaphore(n)) for n in ("early_loaded", "late_loaded", "const_made", "const_ordered", "mask_moved"))
        c = k.c
        taps = lambda w: [w[:, t * P:(t + 1) * P] for t in range(KS)]
        load_constants(nc, k)
        stage(attention, "a", taps(c["wq"]), taps(c["wk"]), taps(c["wv"]), c["wo"], c["a_bq"], c["a_bk"], "a_bv", "a_bo",
                  k.xs, None, k.mask3_a, False)
        stage(scan_stage)
        experts_stage(nc, k)
        stage(attention, "dc", [c["cq"]], [c["ck"]], [c["cv"]], c["co"], c["cq_b"], c["ck_b"], "cv_b", "co_b",
                  k.xs, None, k.mask3_d, False)
        stage(attention, "ds", [c["sq"]], [c["sk"]], [c["sv"]], c["so"], c["sq_b"], c["sk_b"], "sv_b", "so_b",
                  k.rs, ("co_g", "co_be"), None, True)
        stage(feed_forward)
        stage(memory_stage)
        stage(shared_experts_stage)


def constants():
    r, c = np.arange(P)[:, None], np.arange(P)[None, :]
    c32 = np.arange(32)[None, :]
    same = r // 32 == c // 32
    cst = {
        "ident": r == c,
        "sel64": r % S == np.arange(S)[None, :],
        "headmask": r // DH == np.arange(NH)[None, :],
        "bd_strict": same & (r < c),
        "bd_upper": same & (r <= c),
        "eye32": r % 32 == c32,
        "rowlow": r % 32 < 16,
        "rowhigh": r % 32 >= 16,
        "ind2": r // 64 == np.arange(2)[None, :],
        "pick3": (r % 32 == c32) & (r < 96),
    }
    for j in range(4):
        w = 2 ** j
        cst[f"lvl{j}"] = ((r % 32) // (2 * w) == c32 // (2 * w)) & ((r % 32) // w % 2 == 1) & (c32 // w % 2 == 0)
    return {n: v.astype(np.float32) for n, v in cst.items()}


def lay_out(a):
    cat = lambda *xs: np.concatenate(xs, axis=1)
    taps = lambda w: cat(*w)
    col = lambda v: v.reshape(-1, P).T
    down = lambda w: cat(*w.reshape(-1, P, w.shape[-1]))
    parts = constants()
    parts.update(
        a_bq=col(a["L0_xattn_bq"]), a_bk=col(a["L0_xattn_bk"]), b_delta=col(a["L0_attn_b_delta"]), d_skip=col(a["L0_attn_D_skip"]),
        norm_w=col(a["L0_attn_norm_weight"]), rn_g=col(a["L0_ffn_rn_g"]), rn_b=col(a["L0_ffn_rn_b"]), lng=col(a["L0_ffn_ln_g"]),
        lnb=col(a["L0_ffn_ln_b"]), cq_b=col(a["L1_xattn_cq_b"]), ck_b=col(a["L1_xattn_ck_b"]), sq_b=col(a["L1_xattn_sq_b"]),
        sk_b=col(a["L1_xattn_sk_b"]), fi_b=col(a["L1_xattn_fi_b"]),
        wq=taps(a["L0_xattn_Wq"]), wk=taps(a["L0_xattn_Wk"]), wv=taps(a["L0_xattn_Wv"]), wo=a["L0_xattn_Wo"],
        wdelta=a["L0_attn_W_delta"], wbc=cat(a["L0_attn_W_B"], a["L0_attn_W_C"]), alog=a["L0_attn_A_log"],
        router=a["L0_ffn_router_w"].T, w1=cat(*a["L0_ffn_w1"]), w2=down(a["L0_ffn_w2"].reshape(-1, P)),
        fi=a["L1_xattn_fi_w"], fo=down(a["L1_xattn_fo_w"]), gate=a["L1_ffn_gate_w"].T)
    for n in ("cq", "ck", "cv", "co", "sq", "sk", "sv", "so"):
        parts[n] = a[f"L1_xattn_{n}_w"]
    w = a["L1_attn_W_qkvb"].reshape(P, NHM, 3 * DM + 1)
    parts.update(mq=w[:, :, 0:DM].reshape(P, -1), mk=w[:, :, DM:2 * DM].reshape(P, -1), mv=w[:, :, 2 * DM:3 * DM].reshape(P, -1),
                 mbeta=w[:, :, 3 * DM], mo=down(a["L1_attn_W_o"]))
    arrays = {name: cat(*(parts[n] for n, _ in f)) for name, f in PACKS.items()}
    rows = dict(a_bv="L0_xattn_bv", a_bo="L0_xattn_bo", on_g="L0_ffn_on_g", on_b="L0_ffn_on_b", m_g="L1_attn_ln_g", m_b="L1_attn_ln_b")
    arrays["rows"] = np.concatenate([a[rows.get(n, f"L1_xattn_{n}")] for n in ROWS])
    f1, f2, sf1, sf2 = a["L1_ffn_fc1_w"], a["L1_ffn_fc2_w"], a["L1_ffn_s_fc1_w"], a["L1_ffn_s_fc2_w"]
    up, down2, bias, mult = list(f1), list(f2), list(a["L1_ffn_fc1_b"]), list(a["L1_ffn_geglu_mult"])
    for h in range(FS // F1):
        r = slice(h * F1, (h + 1) * F1)
        g = slice(FS + h * F1, FS + (h + 1) * F1)
        up.append(np.concatenate([sf1[r], sf1[g]]))
        down2.append(sf2[:, r])
        bias.append(np.concatenate([a["L1_ffn_s_fc1_b"][r], a["L1_ffn_s_fc1_b"][g]]))
        mult.append(a["L1_ffn_s_geglu_mult"][r])
    arrays["experts"] = np.stack([cat(u.T, d.T, col(v), col(m)) for u, d, v, m in zip(up, down2, bias, mult)])
    arrays["b2"] = cat(*[v[None] for v in (np.concatenate([a["L1_ffn_fc2_b"], a["L1_ffn_s_fc2_b"][None]]))]).reshape(E1 + 1, P)
    arrays["x"] = a["x"]
    arrays["ctxT"] = a["ctx_1024"].transpose(2, 0, 1).reshape(P, B * SC)
    arrays["mask"] = a["mask_Bx1x1xS2_ff0"].reshape(B, SC)
    return {n: np.ascontiguousarray(v) for n, v in arrays.items()}


def kernel(**inputs):
    import concourse.bacc as _bacc
    from concourse import mybir as _mybir
    from concourse.bass_utils import run_bass_kernel_spmd as _run

    nc = _bacc.Bacc("TRN2", target_bir_lowering=False, num_devices=1)
    laid = lay_out({n: np.asarray(v) for n, v in inputs.items()})
    arrays, dram = {}, {}
    for name, a in laid.items():
        arrays[f"in_{name}_dram"] = a
        dram[name] = nc.dram_tensor(f"in_{name}_dram", a.shape, _mybir.dt.from_np(a.dtype), kind="ExternalInput").ap()
    out = nc.dram_tensor("out_0_dram", (B, S, P), F32, kind="ExternalOutput").ap()
    build(nc, dram, out)
    r = _run(nc, [arrays], core_ids=[0])
    return r.results[0]["out_0_dram"]
```

```python
from contextlib import ExitStack

import concourse.bass as bass
import numpy as np
from concourse import mybir

ALU = mybir.AluOpType
ACT = mybir.ActivationFunctionType
AX = mybir.AxisListType
F32 = mybir.dt.float32
BF16 = mybir.dt.bfloat16

P = 128
B, S, SC = 32, 64, 128
NT = B * S // P
NH, DH = 16, 8
NPAIR = NH // 2
KS = 3
NSTATE = 16
E0, H0 = 4, 256
FF = 512
NHM, DM = 16, 64
E1, F1, FS = 15, 128, 256
NE = E1 + FS // F1
EPS = 1e-5
DT_MIN, DT_MAX, RMS_EPS = 0.0001, 10.0, 1e-6

PACKS = {
    "cst": [("ident", P), ("sel64", S), ("headmask", 16), ("bd_strict", P), ("bd_upper", P), ("ind2", 2), ("lvl0", 32), ("lvl1", 32),
            ("lvl2", 32), ("lvl3", 32), ("lvl0T", 32), ("eye32", 32), ("rowlow", 1), ("rowhigh", 1), ("pick3", 32)],
    "col": [("a_bq", 1), ("a_bk", 1), ("b_delta", 1), ("d_skip", 1), ("norm_w", 1), ("rn_g", 1), ("rn_b", 1),
            ("lng", 8), ("lnb", 8), ("cq_b", 1), ("ck_b", 1), ("sq_b", 1), ("sk_b", 1), ("fi_b", 4)],
    "w_a": [("wq", KS * P), ("wk", KS * P), ("wv", KS * P), ("wo", P)],
    "w_b": [("wdelta", P), ("wbc", 2 * NSTATE), ("alog", NSTATE)],
    "w_c": [("router", E0), ("w1", E0 * H0), ("w2", E0 * H0)],
    "w_d": [("cq", P), ("ck", P), ("cv", P), ("co", P), ("sq", P), ("sk", P), ("sv", P), ("so", P), ("fi", FF), ("fo", FF)],
    "w_e": [("mq", NHM * DM), ("mk", NHM * DM), ("mv", NHM * DM), ("mbeta", NHM), ("mo", NHM * DM)],
    "w_f": [("gate", E1)],
}
ROWS = ["a_bv", "a_bo", "on_g", "on_b", "cv_b", "co_b", "co_g", "co_be", "sv_b", "so_b", "so_g", "so_be",
        "fo_b", "fo_g", "fo_be", "m_g", "m_b"]
EXW = [("fc1", 2 * F1), ("fc2", P), ("b1", 2), ("mult", 1)]


class Shared:
    pass


def width(fields):
    return sum(w for _, w in fields)


def fields_of(ap, fields):
    out, at = {}, 0
    for name, w in fields:
        out[name] = ap[:, at:at + w]
        at += w
    return out


class Order:

    def __init__(self, eng, sem, per, i=0):
        self.eng, self.sem, self.per, self.base, self.n = eng, sem, per, i * per, 0

    def __call__(self, ins):
        ins.then_inc(self.sem, 1)
        self.n += 1
        self.eng.wait_ge(self.sem, self.base + self.n)

    def end(self):
        assert self.n == self.per, (self.n, self.per)


def settle(dve, k):
    dve.memset(k.unused[:, :], 0.0)


def tile(i, w=P):
    return bass.ds(i * w, w)


def pipeline(eng, n, body):
    with eng.Fori(0, n - 1) as i:
        body(i, False)
    body(n - 1, True)


def reused(eng, sem, count):
    if not (isinstance(count, int) and count <= 0):
        eng.wait_ge(sem, count)


def staggered(eng, steps, ahead):
    def run(i, j):
        for name, n in ahead.items():
            if name in steps and not (isinstance(i, int) and not 0 <= i + n < NT):
                steps[name](i + n, (j + n) % 2)

    most = max(ahead.values())
    pairs = (NT - most) // 2
    for i in range(-most, 2):
        run(i, i % 2)
    with eng.Fori(1, pairs) as m:
        run(2 * m, 0)
        run(2 * m + 1, 1)
    for i in range(2 * pairs, NT):
        run(i, i % 2)


def behind(order, middle, front):
    return {name: 1 if name in middle else 2 if name in front else 0 for name in order}


def row_stats(dve, order, k, src):
    for t in range(NT):
        ins = dve.bn_stats(k.st[:, 6 * t:6 * t + 6], src[:, t * P:(t + 1) * P])
    order(ins)
    for t in range(NT):
        ins = dve.bn_aggr(k.mv[:, 2 * t:2 * t + 2], k.st[:, 6 * t:6 * t + 6])
    order(ins)


def aggregate(dve, order, k):
    for t in range(NT):
        ins = dve.bn_aggr(k.mv[:, 2 * t:2 * t + 2], k.st[:, 6 * t:6 * t + 6])
    order(ins)


def variances(k):
    return k.mv[:, :].rearrange("p (t two) -> p t two", two=2)[:, :, 1]


def add_normalised(nc, k, name, gain, shift, into, with_stats, store=None):
    sem = lambda n: k.sem(f"{name}_{n}")
    with nc.sbuf_tensor(f"{name}_factors", [P, 3, NT], F32) as f:
        std, rstd, nm = f[:, 0, :], f[:, 1, :], f[:, 2, :]
        steps, var_ready, std_made, made, scaled, gained, shifted, added = (
            sem(n) for n in ("steps", "var_ready", "std_made", "made", "scaled", "gained", "shifted", "added"))
        four = lambda ap, c: ap[:, c * 512:(c + 1) * 512].rearrange("p (t d) -> p t d", d=P)
        row = lambda n: k.row(n).unsqueeze(1).to_broadcast([P, 4, P])
        with nc.Block() as block:
            @block.vector
            def _(dve):
                order = Order(dve, steps, 2)
                aggregate(dve, order, k)
                dve.sem_inc(var_ready, 1)
                dve.wait_ge(std_made, 1)
                order(dve.reciprocal(rstd, std))
                mean = k.mv[:, :].rearrange("p (t two) -> p t two", two=2)[:, :, 0]
                dve.scalar_tensor_tensor(nm, mean, -1.0, rstd, ALU.mult, ALU.mult).then_inc(made, 1)
                order.end()
                for c in range(4):
                    dve.wait_ge(scaled, c + 1)
                    dve.tensor_tensor(four(k.rs, c), four(k.rs, c), row(gain), ALU.mult).then_inc(gained, 1)
                    dve.wait_ge(gained, c + 1)
                    dve.tensor_tensor(four(k.rs, c), four(k.rs, c), row(shift), ALU.add).then_inc(shifted, 1)
                if with_stats:
                    for t in range(NT):
                        if t % 4 == 0:
                            dve.wait_ge(added, t // 4 + 1)
                        dve.bn_stats(k.st[:, 6 * t:6 * t + 6], into[:, t * P:(t + 1) * P])

            @block.scalar
            def _(act):
                act.preload_act_table_set("sqrt_and_others")
                act.wait_ge(var_ready, 1)
                act.activation(std, variances(k), ACT.Sqrt, bias=k.eps[:, :]).then_inc(std_made, 1)
                act.wait_ge(made, 1)
                for t in range(NT):
                    r = slice(t * P, (t + 1) * P)
                    ins = act.activation(k.rs[:, r], k.rs[:, r], ACT.Identity, bias=nm[:, t:t + 1], scale=rstd[:, t:t + 1])
                    if t % 4 == 3:
                        ins.then_inc(scaled, 1)

            if store:
                @block.sync
                def _(sp):
                    store(sp, added)

            @block.gpsimd
            def _(pool):
                for c in range(4):
                    pool.wait_ge(shifted, c + 1)
                    r = slice(c * 512, (c + 1) * 512)
                    pool.tensor_tensor(into[:, r], into[:, r], k.rs[:, r], ALU.add).then_inc(added, 1)


def load_constants(nc, k):
    with nc.Block() as block:
        @block.sync
        def _(sp):
            sp.dma_start(k.xs[:, :].rearrange("p (t d) -> p t d", d=P),
                         k.dram["x"].rearrange("(t b) s d -> (b s) t d", b=2)).then_inc(k.early_loaded, 16)
            for name in ("cst", "col"):
                sp.dma_start(k.pack[name][:, :], k.dram[name]).then_inc(k.early_loaded, 16)
            sp.dma_start(k.pack["w_a"][:, :], k.dram["w_a"]).then_inc(k.weights_loaded, 16)
            sp.dma_start(k.rows[:, :], k.dram["rows"].partition_broadcast(P)).then_inc(k.weights_loaded, 16)
            for name in ("w_b", "w_c", "w_d", "w_e", "w_f"):
                sp.dma_start(k.pack[name][:, :], k.dram[name]).then_inc(k.late_loaded, 16)

        @block.gpsimd
        def _(pool):
            pool.memset(k.ones[:, :], 1.0).then_inc(k.const_made, 1)
            pool.memset(k.ones3[:, :], 1.0).then_inc(k.const_made, 1)
            pool.memset(k.eps[:, :], EPS).then_inc(k.const_made, 1)

        @block.vector
        def _(dve):
            dve.wait_ge(k.early_loaded, 16 * 3)
            order = Order(dve, k.const_ordered, 4)
            order(dve.tensor_scalar(k.hm[:, :], k.c["headmask"], float(DH) ** -0.5, None, ALU.mult))
            order(dve.tensor_copy(k.pick3[:, :], k.c["pick3"]))
            row_stats(dve, order, k, k.xs)
            order.end()


def attention(nc, k, st, wq, wk, wv, wo, bq, bk, bv_row, bo_row, src, affine, mask_scale, own_keys):
    taps = len(wq)
    NK = S if own_keys else SC
    PB = SC // NK
    NB = NPAIR // PB
    HB = NB // 2
    first = affine is None and taps == KS
    sem = lambda name: k.sem(f"{st}_{name}")
    with ExitStack() as ctx:
        def sb(name, shape, dt=F32):
            return ctx.enter_context(nc.sbuf_tensor(f"{st}_{name}", shape, dt))

        cx = sb("context", [P, 2, 2, SC + 2])
        mk = sb("mask_rows", [P, 2, 2, SC])
        xq = sb("query_in", [P, P])
        xs_n = sb("scaled_in", [P, P])
        xT = sb("query_inT", [P, 2, S + 2])
        qT = sb("qT", [P, 2, S])
        qbd = sb("q_heads", [P, 2, NH, S])
        v_in = sb("v_plain", [P, 2, P])
        kT = sb("kT", [P, 2, NK])
        va = sb("v_ones", [P, 2, 2, NB, PB, 17])
        pr = sb("probs", [P, 2, 2, NPAIR, NK])
        prT = sb("probsT", [P, 2, NB, P])
        mx = sb("row_max", [P, 2, NPAIR])
        rd = sb("row_recip", [P, 2, NPAIR])
        on = sb("attended", [P, 2, NPAIR, 2, DH])
        oT = sb("attendedT", [P, P])
        std = sb("std", [P, NT])
        rstd = sb("rstd", [P, NT])
        sc = ctx.enter_context(nc.psum_tensor(f"{st}_scores", [P, 2, 2, 512], F32))
        pt = ctx.enter_context(nc.psum_tensor(f"{st}_turned", [P, 2, 512], F32))
        pa = ctx.enter_context(nc.psum_tensor(f"{st}_even_bank", [P, 512], F32))
        pb = ctx.enter_context(nc.psum_tensor(f"{st}_odd_bank", [P, 512], F32))
        oT_p, out_p = pa[:, 384:512], pb[:, 384:512]
        q_p, k_p, v_p, xT_p = pt[:, 0, 0:P], pt[:, 0, P:P + 2 * NK], pt[:, 1, 0:2 * P], pt[:, 0, 384:512]

        def att_p(b):
            return (pa, pb)[b][:, 0:NPAIR * 17].rearrange("p (a c) -> p a c", c=17)

        FRONT = ["n", "x", "qkv"]
        SCORE = ["S0", "E0", "S1", "E1"]
        APPLY = ["T0", "T1", "O0", "D0", "O1", "D1", "P1", "P2"]
        if first:
            PERIOD = ["T0", "n", "S0", "T1", "O0", "x", "E0", "D0", "O1", "D1", "S1", "P1", "qkv", "P2", "E1"]
        else:
            PERIOD = ["T0", "n", "S0", "T1", "O0", "D0", "O1", "x", "D1", "S1", "qkv", "P1", "E0", "E1", "P2"]
        if own_keys:
            PERIOD = ["T0", "n", "S0", "T1", "S1", "E0", "O0", "x", "D0", "O1", "D1", "qkv", "E1", "P1", "P2"]
        assert sorted(PERIOD) == sorted(FRONT + SCORE + APPLY)
        AHEAD = behind(PERIOD, SCORE, FRONT)

        zeroed, stats, std_made, rstd_made = sem("zeroed"), sem("stats"), sem("std_made"), sem("rstd_made")
        ctx_ready, xq_ready = [sem("ctx_ready0"), sem("ctx_ready1")], sem("xq_ready")
        xT_turned, xT_ready = sem("xT_turned"), sem("xT_ready")
        k_done, v_done = sem("k_done"), sem("v_done")
        q_copied, k_ready, v_copied = sem("q_copied"), sem("k_ready"), sem("v_copied")
        q_ready, v_ready = sem("q_ready"), sem("v_ready")
        s_done, max_ready, p_ready, e_ready = sem("s_done"), sem("max_ready"), sem("p_ready"), sem("e_ready")
        t_done, t_ready, o_done, recip_ready, o_ready = sem("t_done"), sem("t_ready"), sem("o_done"), sem("recip_ready"), sem("o_ready")
        oT_done, oT_ready, out_done, sum_ready = sem("oT_done"), sem("oT_ready"), sem("out_done"), sem("sum_ready")
        sc_left = p_ready if mask_scale is None else sem("sc_left")
        own, va_cleared, va_filled = sem("tile_steps"), sem("va_cleared"), sem("va_filled")
        block = ctx.enter_context(nc.Block())

        @block.sync
        def _(sp):
            if own_keys:
                return
            sp.wait_ge(zeroed, 3)

            def load(i, j):
                reused(sp, sc_left, 2 * i - 2)
                sp.dma_start(cx[:, j, :, 1:SC + 1], k.dram["ctxT"][:, tile(i, 2 * SC)].rearrange("p (b n) -> p b n", b=2))\
                    .then_inc(ctx_ready[j], 16)
                sp.dma_start(mk[:, j, :, :], k.dram["mask"][bass.ds(2 * i, 2), :].partition_broadcast(P)).then_inc(ctx_ready[j], 16)

            load(0, 0)
            load(1, 1)
            with sp.Fori(1, NT // 2) as m:
                load(2 * m, 0)
                load(2 * m + 1, 1)

        @block.gpsimd
        def _(pool):
            pool.memset(cx[:, :, :, :], 0.0).then_inc(zeroed, 1)
            pool.memset(xT[:, :, :], 0.0).then_inc(zeroed, 1)
            pool.memset(on[:, :, :, :, :], 0.0).then_inc(zeroed, 1)
            pool.memset(va[:, :, :, :, :, :], 0.0).then_inc(va_cleared, 1)
            for n in range(PB):
                pool.wait_ge(va_cleared, n + 1)
                pool.memset(va[n * NK:(n + 1) * NK, :, :, :, n, 16], 1.0).then_inc(va_cleared, 1)
            pool.wait_ge(va_cleared, PB + 1)
            if first:
                pool.wait_ge(k.weights_loaded, 16 * 2)
            pool.sem_inc(zeroed, 1)

            def qkv(i, j):
                pool.wait_ge(q_copied, i + 1)
                reused(pool, s_done, 2 * i)
                for b in range(2):
                    pool.tensor_tensor(qbd[:, b, :, :], qT[:, b, :].unsqueeze(1).to_broadcast([P, NH, S]),
                                       k.hm[:, :].unsqueeze(2).to_broadcast([P, NH, S]), ALU.mult).then_inc(q_ready, 1)
                pool.wait_ge(v_copied, i + 1)
                reused(pool, o_done, 2 * i - 2)
                for n in range(PB):
                    r = slice(n * NK, (n + 1) * NK)
                    blocks = lambda ap: ap.rearrange("p (a n c) -> p a n c", n=PB, c=16)[:, :, n, :]
                    for b in range(2):
                        ins = pool.tensor_tensor(va[r, j, b, :, n, 0:16], blocks(v_in[r, b, :]), blocks(k.row(bv_row)[r, :]), ALU.add)
                    if n < PB - 1:
                        ins.then_inc(va_filled, 1)
                        pool.wait_ge(va_filled, i + 1)
                ins.then_inc(v_ready, 1)
                if PB > 1:
                    pool.wait_ge(v_ready, i + 1)

            staggered(pool, {"qkv": qkv}, AHEAD)

        @block.scalar
        def _(act):
            act.preload_act_table_set("sqrt_and_others")
            act.wait_ge(stats, 1)
            act.activation(std[:, :], variances(k), ACT.Sqrt, bias=k.eps[:, :]).then_inc(std_made, 1)
            act.wait_ge(zeroed, 4)

            def x(i, j):
                act.wait_ge(xT_turned, i + 1)
                reused(act, v_done, i)
                act.activation(xT[:, :, 1:S + 1], xT_p.rearrange("p (b s) -> p b s", b=2), ACT.Copy).then_inc(xT_ready, 1)

            def qkv(i, j):
                act.wait_ge(k_done, i + 1)
                reused(act, q_ready, 2 * i)
                act.activation(qT[:, :, :], q_p.rearrange("p (b s) -> p b s", b=2), ACT.Identity, bias=bq).then_inc(q_copied, 1)
                reused(act, s_done, 2 * i)
                act.activation(kT[:, :, :], k_p.rearrange("p (b n) -> p b n", b=2), ACT.Identity, bias=bk).then_inc(k_ready, 1)
                act.wait_ge(v_done, i + 1)
                reused(act, v_ready, i)
                act.activation(v_in[:, :, :], v_p.rearrange("p (b c) -> p b c", b=2), ACT.Copy).then_inc(v_copied, 1)

            def exp(b):
                def step(i, j):
                    act.wait_ge(p_ready, 2 * i + b + 1)
                    act.activation(pr[:, j, b, :, :], pr[:, j, b, :, :], ACT.Exp).then_inc(e_ready, 1)
                return step

            def turn(b):
                def step(i, j):
                    for half in range(2):
                        act.wait_ge(t_done, 4 * i + 2 * b + half + 1)
                        reused(act, o_done, 2 * i + b - 1)
                        act.activation(prT[:, b, HB * half:HB * half + HB, :],
                                       pt[:, half, 0:HB * P].rearrange("p (a c) -> p a c", a=HB), ACT.Copy).then_inc(t_ready, 1)
                return step

            def out_turn(i, j):
                act.wait_ge(oT_done, i + 1)
                reused(act, out_done, i)
                act.activation(oT[:, :], oT_p, ACT.Copy).then_inc(oT_ready, 1)

            act.preload_act_table_set("exp_and_others")
            staggered(act, {"x": x, "qkv": qkv, "E0": exp(0), "E1": exp(1), "T0": turn(0), "T1": turn(1), "P1": out_turn},
                       AHEAD)

        @block.vector
        def _(dve):
            order = Order(dve, stats, 1)
            aggregate(dve, order, k)
            dve.wait_ge(std_made, 1)
            dve.reciprocal(rstd[:, :], std[:, :]).then_inc(rstd_made, 1)
            dve.wait_ge(rstd_made, 1)
            dve.wait_ge(zeroed, 4)

            def norm_in(i, j):
                reused(dve, xT_turned, i)
                outs = [xq[:, :]] if first else [k.res[:, tile(i)], xq[:, :]]
                plain = [xs_n[:, :]] if affine else outs
                for o in plain:
                    ins = dve.tensor_scalar(o, src[:, tile(i)], k.mv[:, bass.ds(2 * i, 1)], rstd[:, bass.ds(i, 1)],
                                            ALU.subtract, ALU.mult)
                if affine:
                    order = Order(dve, own, 2, i)
                    order(ins)
                    order(dve.tensor_tensor(xs_n[:, :], xs_n[:, :], k.row(affine[0]), ALU.mult))
                    order.end()
                    for o in outs:
                        ins = dve.tensor_tensor(o, xs_n[:, :], k.row(affine[1]), ALU.add)
                ins.then_inc(xq_ready, 1)

            def soft(b):
                def step(i, j):
                    dve.wait_ge(s_done, 2 * i + b + 1)
                    s4 = sc[:, b, :, 0:4 * NK].rearrange("p h (a n) -> p h a n", a=4)
                    p4 = pr[:, j, b, :, :].rearrange("p (h a) n -> p h a n", h=2)
                    reused(dve, t_done, 4 * i + 2 * b - 6)
                    if mask_scale is not None:
                        dve.wait_ge(ctx_ready[j], 16 * i - 16 * j + 32)
                        dve.scalar_tensor_tensor(pr[:, j, b, :, :], mk[:, j, b, :].unsqueeze(1).to_broadcast([P, NPAIR, NK]), mask_scale,
                                                 sc[:, b, :, :].rearrange("p h (a n) -> p (h a) n", n=NK), ALU.mult, ALU.add)\
                            .then_inc(sc_left, 1)
                        dve.wait_ge(sc_left, 2 * i + b + 1)
                        s4 = p4
                    dve.tensor_reduce(mx[:, b, :].rearrange("p (h a) -> p h a", h=2), s4, AX.X, ALU.max).then_inc(max_ready, 1)
                    dve.wait_ge(max_ready, 2 * i + b + 1)
                    dve.tensor_tensor(p4, s4,
                                      mx[:, b, :].rearrange("p (h a) -> p h a", h=2).unsqueeze(3).to_broadcast([P, 2, 4, NK]),
                                      ALU.subtract).then_inc(p_ready, 1)
                return step

            def divide(b):
                def step(i, j):
                    dve.wait_ge(o_done, 2 * i + b + 1)
                    o = att_p(b)
                    dve.reciprocal(rd[:, b, :], o[:, :, 16]).then_inc(recip_ready, 1)
                    dve.wait_ge(recip_ready, 2 * i + b + 1)
                    reused(dve, oT_done, i)
                    for h in range(2):
                        r = slice(h * S, (h + 1) * S)
                        ins = dve.tensor_tensor(on[r, b, :, h, :], o[r, :, h * DH:(h + 1) * DH],
                                                rd[r, b, :].unsqueeze(2).to_broadcast([S, NPAIR, DH]), ALU.mult)
                    ins.then_inc(o_ready, 1)
                return step

            def add_out(i, j):
                dve.wait_ge(out_done, i + 1)
                into, old = (k.xs, k.xs) if first else (k.rs, k.res)
                dve.tensor_tensor(into[:, tile(i)], out_p, old[:, tile(i)], ALU.add).then_inc(sum_ready, 1)
                dve.wait_ge(sum_ready, i + 1)
                dve.bn_stats(k.st[:, bass.ds(6 * i, 6)], into[:, tile(i)])

            staggered(dve, {"n": norm_in, "S0": soft(0), "S1": soft(1), "D0": divide(0), "D1": divide(1), "P2": add_out},
                       AHEAD)

        @block.tensor
        def _(pe):
            if first:
                pe.wait_ge(k.weights_loaded, 16 * 2)

            def x(i, j):
                pe.wait_ge(xq_ready, i + 1)
                reused(pe, t_ready, 4 * i - 4)
                pe.transpose(xT_p, xq[:, :], k.c["ident"]).then_inc(xT_turned, 1)

            def qkv(i, j):
                pe.wait_ge(xT_ready, i + 1)
                kv = xT if own_keys else cx[:, j, :, :]
                if not own_keys:
                    pe.wait_ge(ctx_ready[j], 16 * i - 16 * j + 32)
                for t in range(taps):
                    a = 1 + t - taps // 2
                    pe.matmul(q_p.rearrange("p (b s) -> p b s", b=2), wq[t], xT[:, :, a:a + S], start=t == 0, stop=t == taps - 1)
                for t in range(taps):
                    a = 1 + t - taps // 2
                    mm = pe.matmul(k_p.rearrange("p (b n) -> p b n", b=2), wk[t], kv[:, :, a:a + NK],
                                   start=t == 0, stop=t == taps - 1)
                mm.then_inc(k_done, 1)
                for b in range(2):
                    for n in range(PB):
                        for t in range(taps):
                            a = 1 + t - taps // 2
                            mm = pe.matmul(v_p[n * NK:(n + 1) * NK, b * P:(b + 1) * P], kv[:, b, a:a + NK], wv[t],
                                           start=t == 0, stop=t == taps - 1)
                mm.then_inc(v_done, 1)

            def scores(b):
                def step(i, j):
                    pe.wait_ge(q_ready, 2 * i + b + 1)
                    if b == 0:
                        pe.wait_ge(k_ready, i + 1)
                    reused(pe, sc_left, 2 * i + b - 1)
                    for h in range(2):
                        out = sc[:, b, h, 0:4 * NK].rearrange("p (a n) -> p a n", a=4)
                        if own_keys:
                            for a in ((0, 1, 2, 3), (3, 2, 1, 0))[b]:
                                n = 8 * h + 2 * a
                                at, keys = (a * NK, kT[:, :, :]) if b == 0 else (a * NK - NK, kT[:, :, :]) if a else (0, kT[:, 1:2, :])
                                width = keys.shape[1] * NK
                                mm = pe.matmul(sc[:, b, h, at:at + width], qbd[:, b, n:n + 2, :].rearrange("p a s -> p (a s)"),
                                               keys.rearrange("p b n -> p (b n)"), start=True, stop=True)
                            continue
                        for a in range(4):
                            n = 8 * h + 2 * a
                            mm = pe.matmul(out[:, a, :], qbd[:, b, n:n + 2, :].rearrange("p a s -> p (a s)"), kT[:, b, :],
                                           start=True, stop=True)
                    mm.then_inc(s_done, 1)
                return step

            def turn(b):
                def step(i, j):
                    if b == 0 and not (isinstance(i, int) and i == NT - 1):
                        pe.wait_ge(k_ready, i + 2)
                        pe.wait_ge(v_copied, i + 2)
                    pe.wait_ge(e_ready, 2 * i + b + 1)
                    for half in range(2):
                        if b:
                            pe.wait_ge(t_ready, 4 * i + half + 1)
                        for n in range(HB):
                            a = (HB * half + n) * PB
                            mm = pe.transpose(pt[:, half, n * P:(n + 1) * P],
                                              pr[:, j, b, a:a + PB, :].rearrange("p a n -> p (a n)"), k.c["ident"])
                        mm.then_inc(t_done, 1)
                return step

            def attend(b):
                def step(i, j):
                    pe.wait_ge(t_ready, 4 * i + 2 * b + 2)
                    pe.wait_ge(v_ready, i + 1)
                    reused(pe, (oT_ready, sum_ready)[b], i)
                    for n in range(NB):
                        last = min(n + 6 // PB, NB)
                        mm = pe.matmul((pa, pb)[b][:, n * 17 * PB:last * 17 * PB], prT[:, b, n, :],
                                       va[:, j, b, n:last, :, :].rearrange("p n a c -> p (n a c)"), start=True, stop=True)
                    mm.then_inc(o_done, 1)
                return step

            def out_turn(i, j):
                pe.wait_ge(o_ready, 2 * i + 2)
                for b in range(2):
                    mm = pe.matmul(oT_p[:, b * S:(b + 1) * S], on[:, b, :, :, :].rearrange("p a h d -> p (a h d)"), k.c["sel64"],
                                   start=True, stop=True)
                mm.then_inc(oT_done, 1)

            def project(i, j):
                pe.wait_ge(oT_ready, i + 1)
                pe.matmul(out_p, k.ones[0:1, :], k.row(bo_row)[0:1, :], start=True, stop=False)
                pe.matmul(out_p, oT[:, :], wo, start=False, stop=True).then_inc(out_done, 1)

            staggered(pe, {"x": x, "qkv": qkv, "S0": scores(0), "S1": scores(1), "T0": turn(0), "T1": turn(1), "O0": attend(0),
                            "O1": attend(1), "P1": out_turn, "P2": project}, AHEAD)


def scan_stage(nc, k):
    CH = 512
    NC = B * S // CH
    G = 4
    centre, half = (DT_MAX + DT_MIN) / 2.0, (DT_MAX - DT_MIN) / 2.0
    sem = lambda name: k.sem(f"b_{name}")
    with ExitStack() as ctx:
        def sb(name, shape, dt=F32):
            return ctx.enter_context(nc.sbuf_tensor(f"b_{name}", shape, dt))

        xnT = sb("xnT", [P, B * S])
        delta = sb("delta", [P, B * S])
        u = sb("sqrt_delta_x", [P, B * S])
        bc3 = sb("bc_terms", [96, B * S], BF16)
        sa = sb("half_a", [P, NSTATE])
        zeros = sb("zeros", [1, CH], BF16)
        dskip = sb("skip_diagonal", [P, P])
        small = sb("row_factors", [P, 6, NT])
        neg1 = sb("minus_one", [P, 1])
        tbias = sb("tanh_bias", [P, 1])
        rbias = sb("rms_eps", [P, 1])
        with ExitStack() as inner:
            t1 = inner.enter_context(nc.sbuf_tensor("b_t1", [P, B * S], F32))
            t2 = inner.enter_context(nc.sbuf_tensor("b_t2", [P, B * S], F32))
            rest = inner.enter_context(nc.sbuf_tensor("b_rest", [32, 2, CH], F32))
            low = inner.enter_context(nc.sbuf_tensor("b_low", [32, 2, B * S], BF16))
            turned = inner.enter_context(nc.psum_tensor("b_turned", [P, 2, 512], F32))
            dp = inner.enter_context(nc.psum_tensor("b_delta_p", [P, 2, 512], F32))
            bp = inner.enter_context(nc.psum_tensor("b_bc_p", [32, 2, 512], F32))
            made, varied, std1, std2 = sem("constants"), sem("varied"), sem("std1"), sem("std2")
            xn_ready, xn_turned, xnT_ready = sem("xn_ready"), sem("xn_turned"), sem("xnT_ready")
            d_done, d_left, bc_done, bc_left = sem("d_done"), sem("d_left"), sem("bc_done"), sem("bc_left")
            act_steps, dve_steps, low_ready = sem("act_steps"), sem("dve_steps"), sem("low_ready")
            soft_ready, sum_ready, tanh_ready, delta_ready, root_ready = (
                sem("soft_ready"), sem("sum_ready"), sem("tanh_ready"), sem("delta_ready"), sem("root_ready"))
            HALF = B * S // 2
            halves = [slice(0, HALF), slice(HALF, 2 * HALF)]
            a_ready, moved = sem("a_ready"), sem("moved")
            with nc.Block() as block:
                @block.gpsimd
                def _(pool):
                    pool.memset(zeros[:, :], 0.0)
                    pool.memset(neg1[:, :], -1.0).then_inc(made, 1)
                    pool.memset(tbias[:, :], -centre / half).then_inc(made, 1)
                    pool.memset(rbias[:, :], RMS_EPS).then_inc(made, 1)
                    pool.tensor_scalar(dskip[:, :], k.c["ident"], k.c["d_skip"], None, ALU.mult)

                @block.sync
                def _(sp):
                    sp.wait_ge(low_ready, NC)
                    for j in range(2):
                        sp.dma_start(bc3[32 * (j + 1):32 * (j + 2), :], low[:, j, :]).then_inc(moved, 16)
                    sp.wait_ge(moved, 32)

                @block.vector
                def _(dve):
                    order = Order(dve, dve_steps, 6 + 5 * NC)
                    aggregate(dve, order, k)
                    dve.sem_inc(varied, 1)
                    dve.wait_ge(std1, 1)
                    rstd, msq, r2, rs = small[:, 1, :], small[:, 2, :], small[:, 4, :], small[:, 5, :]
                    order(dve.reciprocal(rstd, small[:, 0, :]))
                    order(dve.tensor_tensor(msq, variances(k), rstd, ALU.mult))
                    order(dve.tensor_tensor(msq, msq, rstd, ALU.mult))
                    dve.sem_inc(varied, 1)
                    dve.wait_ge(std2, 1)
                    order(dve.reciprocal(r2, small[:, 3, :]))
                    order(dve.tensor_tensor(rs, rstd, r2, ALU.mult))
                    for t in range(NT):
                        ins = dve.tensor_scalar(k.res[:, t * P:(t + 1) * P], k.xs[:, t * P:(t + 1) * P], k.mv[:, 2 * t:2 * t + 1],
                                                rs[:, t:t + 1], ALU.subtract, ALU.mult)
                        if t % 4 == 3:
                            ins.then_inc(xn_ready, 1)
                    for c in range(NC):
                        r = slice(c * CH, (c + 1) * CH)
                        dve.wait_ge(bc_done, c + 1)
                        b = bp[:, c % 2, :]
                        order(dve.tensor_copy(bc3[0:32, r], b))
                        order(dve.tensor_tensor(rest[:, 0, :], b, bc3[0:32, r], ALU.subtract))
                        dve.sem_inc(bc_left, 1)
                        order(dve.tensor_copy(low[:, 0, r], rest[:, 0, :]))
                        order(dve.tensor_tensor(rest[:, 1, :], rest[:, 0, :], low[:, 0, r], ALU.subtract))
                        order(dve.tensor_copy(low[:, 1, r], rest[:, 1, :]))
                        dve.sem_inc(low_ready, 1)
                    for h in halves:
                        dve.wait_ge(soft_ready, h.start // HALF + 1)
                        dve.tensor_tensor(t1[:, h], t1[:, h], t2[:, h], ALU.add).then_inc(sum_ready, 1)
                    for h in halves:
                        dve.wait_ge(tanh_ready, h.start // HALF + 1)
                        dve.tensor_scalar(delta[:, h], t1[:, h], half, centre, ALU.mult, ALU.add).then_inc(delta_ready, 1)
                    for h in halves:
                        dve.wait_ge(root_ready, h.start // HALF + 1)
                        dve.tensor_tensor(u[:, h], t2[:, h], xnT[:, h], ALU.mult)
                    dve.wait_ge(a_ready, 1)
                    dve.tensor_scalar(sa[:, :], sa[:, :], 0.5, None, ALU.mult)
                    order.end()

                @block.scalar
                def _(act):
                    act.preload_act_table_set("sqrt_and_others")
                    act.wait_ge(k.late_loaded, 16 * 5)
                    act.wait_ge(varied, 1)
                    act.activation(small[:, 0, :], variances(k), ACT.Sqrt, bias=k.eps[:, :]).then_inc(std1, 1)
                    act.wait_ge(varied, 2)
                    act.wait_ge(made, 3)
                    act.activation(small[:, 3, :], small[:, 2, :], ACT.Sqrt, bias=rbias[:, :]).then_inc(std2, 1)
                    for c in range(NC):
                        act.wait_ge(xn_turned, c + 1)
                        act.activation(xnT[:, c * CH:(c + 1) * CH], turned[:, c % 2, :], ACT.Copy, scale=k.c["norm_w"]).then_inc(xnT_ready, 1)
                    for c in range(NC):
                        r = slice(c * CH, (c + 1) * CH)
                        act.wait_ge(d_done, c + 1)
                        act.activation(t1[:, r], dp[:, c % 2, :], ACT.Abs, bias=k.c["b_delta"])
                        act.activation(t2[:, r], dp[:, c % 2, :], ACT.Relu, bias=k.c["b_delta"]).then_inc(d_left, 1)
                    act.wait_ge(d_left, NC)
                    act.preload_act_table_set("natural_log_exp_and_others")
                    act.activation(sa[:, :], k.c["alog"], ACT.Exp).then_inc(a_ready, 1)
                    for h in halves:
                        act.activation(t1[:, h], t1[:, h], ACT.Exp, scale=-1.0).then_inc(act_steps, 1)
                    for h in halves:
                        act.wait_ge(act_steps, h.start // HALF + 1)
                        act.activation(t1[:, h], t1[:, h], ACT.Ln, bias=k.ones[:, 0:1]).then_inc(soft_ready, 1)
                    for h in halves:
                        act.wait_ge(sum_ready, h.start // HALF + 1)
                        act.activation(t1[:, h], t1[:, h], ACT.Tanh, bias=tbias[:, :], scale=1.0 / half).then_inc(tanh_ready, 1)
                    act.preload_act_table_set("natural_log_exp_and_others")
                    for h in halves:
                        act.wait_ge(delta_ready, h.start // HALF + 1)
                        act.activation(t2[:, h], delta[:, h], ACT.Ln).then_inc(act_steps, 1)
                    for h in halves:
                        act.wait_ge(act_steps, h.start // HALF + 3)
                        act.activation(t2[:, h], t2[:, h], ACT.Exp, scale=0.5).then_inc(root_ready, 1)

                @block.tensor
                def _(pe):
                    pe.wait_ge(k.late_loaded, 16 * 5)
                    for c in range(NC):
                        pe.wait_ge(xn_ready, c + 1)
                        if c >= 2:
                            pe.wait_ge(xnT_ready, c - 1)
                        for j in range(4):
                            t = 4 * c + j
                            mm = pe.transpose(turned[:, c % 2, j * P:(j + 1) * P], k.res[:, t * P:(t + 1) * P], k.c["ident"])
                        mm.then_inc(xn_turned, 1)
                    for c in range(NC):
                        r = slice(c * CH, (c + 1) * CH)
                        pe.wait_ge(xnT_ready, c + 1)
                        if c >= 2:
                            pe.wait_ge(d_left, c - 1)
                            pe.wait_ge(bc_left, c - 1)
                        pe.matmul(dp[:, c % 2, :], k.c["wdelta"], xnT[:, r], start=True, stop=True).then_inc(d_done, 1)
                        pe.matmul(bp[:, c % 2, :], k.c["wbc"], xnT[:, r], start=True, stop=True).then_inc(bc_done, 1)

        with ExitStack() as inner:
            def buf(name, n):
                return inner.enter_context(nc.sbuf_tensor(f"b_{name}", [P, n, CH], F32))

            inv, ab, w, bx, h, hc = buf("inverse", G), buf("a_bar", G), buf("inverse_u", G), buf("b_x", 2), buf("states", 2), buf("states_c", 2)
            bb = inner.enter_context(nc.psum_tensor("b_b_bank", [P, G, 512], F32))
            cb = inner.enter_context(nc.psum_tensor("b_c_bank", [P, 2, 512], F32))
            yp = inner.enter_context(nc.psum_tensor("b_y_bank", [P, 2, 512], F32))
            cleared, ln_ready, inv_ready, ab_ready, w_ready = (sem(n) for n in ("cleared", "ln_ready", "inv_ready", "ab_ready", "w_ready"))
            bb_done, cb_done, bx_ready, h_ready, hc_ready, y_done, added = (
                sem(n) for n in ("bb_done", "cb_done", "bx_ready", "h_ready", "hc_ready", "y_done", "added"))

            def groups(eng, body, chunk_end=None):
                for c in range(NC):
                    body(c, 0, NSTATE * c, c == 0)
                    with eng.Fori(1, NSTATE // G - 1) as g:
                        body(c, G * g, NSTATE * c + G * g, False)
                    body(c, NSTATE - G, NSTATE * (c + 1) - G, False)
                    if chunk_end:
                        chunk_end(c)

            with nc.Block() as block:
                @block.scalar
                def _(act):
                    act.wait_ge(cleared, 1)
                    act.preload_act_table_set("natural_log_exp_and_others")

                    def body(c, n, s, first):
                        for p in (0, 2):
                            if not first:
                                act.wait_ge(w_ready, s + p - 2)
                            for j in (p, p + 1):
                                ins = act.activation(inv[:, j, :], delta[:, c * CH:(c + 1) * CH], ACT.Ln, bias=k.ones[:, 0:1],
                                                     scale=sa[:, bass.ds(n + j, 1)])
                            ins.then_inc(ln_ready, 2)
                            act.wait_ge(ln_ready, s + p + 2)
                            act.activation(inv[:, p:p + 2, :], inv[:, p:p + 2, :], ACT.Exp, scale=-1.0).then_inc(inv_ready, 2)
                            act.wait_ge(inv_ready, s + p + 2)
                            if not first:
                                act.wait_ge(h_ready, s + p - 2)
                            act.activation(ab[:, p:p + 2, :].rearrange("p j (b s) -> p (j b) s", s=S)[:, :, 1:S],
                                           inv[:, p:p + 2, :].rearrange("p j (b s) -> p (j b) s", s=S)[:, :, 1:S],
                                           ACT.Identity, bias=neg1[:, :], scale=2.0).then_inc(ab_ready, 2)

                    groups(act, body)

                @block.gpsimd
                def _(pool):
                    pool.memset(ab[:, :, :], 0.0).then_inc(cleared, 1)

                    def body(c, n, s, first):
                        for j in range(G):
                            pool.wait_ge(inv_ready, s + j - j % 2 + 2)
                            if not first:
                                pool.wait_ge(bx_ready, s + j - 3)
                            pool.tensor_tensor(w[:, j, :], inv[:, j, :], u[:, c * CH:(c + 1) * CH], ALU.mult).then_inc(w_ready, 1)

                    groups(pool, body)

                @block.vector
                def _(dve):
                    dve.wait_ge(cleared, 1)

                    def weigh(s, j):
                        dve.wait_ge(w_ready, s + j + 1)
                        dve.wait_ge(bb_done, s + j + 1)
                        dve.tensor_tensor(bx[:, j % 2, :], w[:, j % G, :], bb[:, j % G, :], ALU.mult).then_inc(bx_ready, 1)

                    def body(c, n, s, first):
                        for j in range(G):
                            dve.wait_ge(bx_ready, s + j + 1)
                            dve.wait_ge(ab_ready, s + j - j % 2 + 2)
                            dve.tensor_tensor_scan(h[:, j % 2, :], ab[:, j, :], bx[:, j % 2, :], 0.0, ALU.mult, ALU.add).then_inc(h_ready, 1)
                            if not (isinstance(s, int) and s + j == NC * NSTATE - 1):
                                weigh(s, j + 1)
                            dve.wait_ge(h_ready, s + j + 1)
                            dve.wait_ge(cb_done, s + j + 1)
                            if not (first and j < 2):
                                dve.wait_ge(y_done, s + j - 1)
                            dve.tensor_tensor(hc[:, j % 2, :], h[:, j % 2, :], cb[:, j % 2, :], ALU.mult).then_inc(hc_ready, 1)

                    def chunk_end(c):
                        r = slice(c * CH, (c + 1) * CH)
                        dve.wait_ge(y_done, NSTATE * (c + 1))
                        dve.tensor_tensor(k.xs[:, r], k.xs[:, r], yp[:, c % 2, :], ALU.add).then_inc(added, 1)
                        dve.wait_ge(added, c + 1)
                        for t in range(4 * c, 4 * c + 4):
                            dve.bn_stats(k.st[:, 6 * t:6 * t + 6], k.xs[:, t * P:(t + 1) * P])

                    weigh(0, 0)
                    groups(dve, body, chunk_end)

                @block.tensor
                def _(pe):
                    def add(c, j, last=False):
                        for q in range(4):
                            mm = pe.matmul(yp[:, c % 2, q * P:(q + 1) * P], hc[:, j % 2, q * P:(q + 1) * P], k.c["ident"],
                                           start=False, stop=last and q == 3)
                        mm.then_inc(y_done, 1)

                    def spread(bank, row, c):
                        return pe.matmul(bank, k.pick3[0:96, bass.ds(row, 1)].to_broadcast([96, P]), bc3[:, c * CH:(c + 1) * CH],
                                         start=True, stop=True)

                    def body(c, n, s, first):
                        for j in range(G):
                            if not (first and j < 2):
                                pe.wait_ge(hc_ready, s + j - 1)
                            spread(cb[:, j % 2, :], n + j + NSTATE, c).then_inc(cb_done, 1)
                            if not (first and j < 3):
                                pe.wait_ge(bx_ready, s + j - 2)
                            if not (isinstance(n, int) and n + j == NSTATE - 1):
                                spread(bb[:, (j + 1) % G, :], n + j + 1, c).then_inc(bb_done, 1)
                            elif c < NC - 1:
                                spread(bb[:, 0, :], 0, c + 1).then_inc(bb_done, 1)
                            if isinstance(n, int) and n + j == 0:
                                if c:
                                    pe.wait_ge(hc_ready, s)
                                    add(c - 1, G - 1, True)
                                if c >= 2:
                                    pe.wait_ge(added, c - 1)
                                pe.matmul(yp[:, c % 2, :], k.ones3[0:1, :], zeros[:, :], start=True, stop=False)
                                for q in range(4):
                                    pe.matmul(yp[:, c % 2, q * P:(q + 1) * P], xnT[:, c * CH + q * P:c * CH + (q + 1) * P],
                                              dskip[:, :], start=False, stop=False)
                            else:
                                pe.wait_ge(hc_ready, s + j)
                                add(c, j - 1)

                    spread(bb[:, 0, :], 0, 0).then_inc(bb_done, 1)
                    groups(pe, body)
                    pe.wait_ge(hc_ready, NSTATE * NC)
                    add(NC - 1, G - 1, True)


def top_experts(dve, order, pool_filled, score, picked, values, kept, n, top, pad):
    for t in range(NT):
        ins = dve.max(values[:, t, :], score[:, t, :])
    order(ins)
    order(dve.memset(values[:, :, top:8], -1.0))
    for t in range(NT):
        ins = dve.match_replace(picked[:, t, :], values[:, t, :], score[:, t, :], -2.0)
    order(ins)
    order(dve.tensor_scalar(picked[:, :, 0:n], picked[:, :, 0:n], -2.0, None, ALU.is_equal))
    order(dve.tensor_tensor(kept, picked[:, :, 0:n], score[:, :, 0:n], ALU.mult))


def experts_stage(nc, k):
    N8 = E0 * H0 // P
    sem = lambda name: k.sem(f"c_{name}")
    with ExitStack() as ctx:
        def sb(name, shape, dt=F32):
            return ctx.enter_context(nc.sbuf_tensor(f"c_{name}", shape, dt))

        def psum(name, shape):
            return ctx.enter_context(nc.psum_tensor(f"c_{name}", shape, F32))

        comb = sb("weights", [P, NT, E0])
        rstd = sb("rstd", [P, NT])
        hT = sb("hT", [P, B * S])
        with ExitStack() as inner:
            small = inner.enter_context(nc.sbuf_tensor("c_row_factors", [P, 4, NT], F32))
            gR = inner.enter_context(nc.sbuf_tensor("c_scaled_router", [P, E0], F32))
            bR = inner.enter_context(nc.sbuf_tensor("c_router_bias", [P, E0], F32))
            lg = inner.enter_context(nc.sbuf_tensor("c_logits", [P, NT, E0], F32))
            score = inner.enter_context(nc.sbuf_tensor("c_scores", [P, NT, E0 + 6], F32))
            picked = inner.enter_context(nc.sbuf_tensor("c_picked", [P, NT, E0 + 6], F32))
            values = inner.enter_context(nc.sbuf_tensor("c_values", [P, NT, 8], F32))
            red = inner.enter_context(nc.sbuf_tensor("c_reduced", [P, 4, NT], F32))
            turned = inner.enter_context(nc.psum_tensor("c_turned_p", [P, 2, 512], F32))
            lp = inner.enter_context(nc.psum_tensor("c_logit_p", [P, 512], F32))
            bp = inner.enter_context(nc.psum_tensor("c_bias_p", [P, 512], F32))
            varied, std1, std2, filled, steps = sem("varied"), sem("std1"), sem("std2"), sem("filled"), sem("router_steps")
            h_ready, h_turned, hT_ready, gR_ready = sem("h_ready"), sem("h_turned"), sem("hT_ready"), sem("gR_ready")
            logit_done, shifted, exp_ready = sem("logit_done"), sem("shifted"), sem("exp_ready")
            with nc.Block() as block:
                @block.gpsimd
                def _(pool):
                    pool.memset(score[:, :, :], -1.0).then_inc(filled, 1)

                @block.scalar
                def _(act):
                    act.preload_act_table_set("sqrt_and_others")
                    act.wait_ge(varied, 1)
                    act.activation(small[:, 0, :], variances(k), ACT.Sqrt, bias=k.eps[:, :]).then_inc(std1, 1)
                    act.wait_ge(varied, 2)
                    act.activation(small[:, 2, :], small[:, 1, :], ACT.Sqrt, bias=k.eps[:, :]).then_inc(std2, 1)
                    for c in range(4):
                        act.wait_ge(h_turned, c + 1)
                        act.activation(hT[:, c * 512:(c + 1) * 512], turned[:, c % 2, :], ACT.Copy).then_inc(hT_ready, 1)
                    act.wait_ge(shifted, 1)
                    act.activation(lg[:, :, :], lg[:, :, :], ACT.Exp).then_inc(exp_ready, 1)

                @block.tensor
                def _(pe):
                    for c in range(4):
                        pe.wait_ge(h_ready, c + 1)
                        if c >= 2:
                            pe.wait_ge(hT_ready, c - 1)
                        for j in range(4):
                            t = 4 * c + j
                            mm = pe.transpose(turned[:, c % 2, j * P:(j + 1) * P], k.res[:, t * P:(t + 1) * P], k.c["ident"])
                        mm.then_inc(h_turned, 1)
                    pe.wait_ge(gR_ready, 1)
                    pe.matmul(bp[:, 0:E0], k.c["rn_b"].to_broadcast([P, P]), k.c["router"], start=True, stop=True)
                    for t in range(NT):
                        if t % 4 == 0:
                            pe.wait_ge(hT_ready, t // 4 + 1)
                        mm = pe.matmul(lp[:, t * E0:(t + 1) * E0], hT[:, t * P:(t + 1) * P], gR[:, :], start=True, stop=True)
                    mm.then_inc(logit_done, 1)

                @block.vector
                def _(dve):
                    order = Order(dve, steps, 21)
                    aggregate(dve, order, k)
                    dve.sem_inc(varied, 1)
                    dve.wait_ge(std1, 1)
                    order(dve.reciprocal(rstd[:, :], small[:, 0, :]))
                    order(dve.tensor_tensor(small[:, 1, :], variances(k), rstd[:, :], ALU.mult))
                    order(dve.tensor_tensor(small[:, 1, :], small[:, 1, :], rstd[:, :], ALU.mult))
                    dve.sem_inc(varied, 1)
                    dve.tensor_scalar(gR[:, :], k.c["router"], k.c["rn_g"], None, ALU.mult).then_inc(gR_ready, 1)
                    for t in range(NT):
                        ins = dve.tensor_scalar(k.res[:, t * P:(t + 1) * P], k.xs[:, t * P:(t + 1) * P], k.mv[:, 2 * t:2 * t + 1],
                                                rstd[:, t:t + 1], ALU.subtract, ALU.mult)
                        if t % 4 == 3:
                            ins.then_inc(h_ready, 1)
                    dve.wait_ge(std2, 1)
                    order(dve.reciprocal(small[:, 3, :], small[:, 2, :]))
                    dve.wait_ge(logit_done, 1)
                    order(dve.tensor_copy(bR[:, :], bp[:, 0:E0]))
                    order(dve.tensor_tensor(lg[:, :, :], lp[:, 0:NT * E0].rearrange("p (t e) -> p t e", e=E0),
                                            small[:, 3, :].unsqueeze(2).to_broadcast([P, NT, E0]), ALU.mult))
                    order(dve.tensor_tensor(lg[:, :, :], lg[:, :, :], bR[:, :].unsqueeze(1).to_broadcast([P, NT, E0]), ALU.add))
                    order(dve.tensor_reduce(red[:, 0, :], lg[:, :, :], AX.X, ALU.max))
                    dve.tensor_tensor(lg[:, :, :], lg[:, :, :], red[:, 0, :].unsqueeze(2).to_broadcast([P, NT, E0]),
                                      ALU.subtract).then_inc(shifted, 1)
                    dve.wait_ge(exp_ready, 1)
                    order(dve.tensor_reduce(red[:, 1, :], lg[:, :, :], AX.X, ALU.add))
                    order(dve.reciprocal(red[:, 1, :], red[:, 1, :]))
                    dve.wait_ge(filled, 1)
                    order(dve.tensor_tensor(score[:, :, 0:E0], lg[:, :, :], red[:, 1, :].unsqueeze(2).to_broadcast([P, NT, E0]), ALU.mult))
                    top_experts(dve, order, filled, score, picked, values, comb[:, :, :], E0, 2, 6)
                    order(dve.tensor_reduce(red[:, 2, :], comb[:, :, :], AX.X, ALU.add))
                    order(dve.tensor_scalar(red[:, 2, :], red[:, 2, :], 1e-8, None, ALU.add))
                    order(dve.reciprocal(red[:, 2, :], red[:, 2, :]))
                    order(dve.tensor_tensor(comb[:, :, :], comb[:, :, :], red[:, 2, :].unsqueeze(2).to_broadcast([P, NT, E0]), ALU.mult))
                    order.end()

        z, aT, acc, hi = sb("hidden_n", [P, E0, H0]), sb("hidden_T", [P, 2, N8, P]), sb("mixed", [P, P]), sb("tile_hT", [P, 2, P])
        st4, mv4, std4, r4 = sb("st4", [P, E0, 6]), sb("mv4", [P, E0, 2]), sb("std4", [P, E0]), sb("rstd4", [P, E0])
        hp, zp, op = psum("hidden_p", [P, 2, 2, 512]), psum("z_turned", [P, 2, 512]), psum("out_p", [P, 2, 512])
        h_taken, hid_done, var_ready, std_ready = (sem(n) for n in ("h_taken", "hid_done", "var_ready", "std_ready"))
        z_ready, z_turned, a_ready, out_done, steps, mixed = (
            sem(n) for n in ("z_ready", "z_turned", "a_ready", "out_done", "tile_steps", "mixed"))
        with nc.Block() as block:
            AHEAD = {"h": 3, "z": 1, "a": 0, "hid": 2, "out": 0}

            @block.vector
            def _(dve):
                def hidden_of(j, e):
                    return hp[:, j, e // 2, e % 2 * H0:(e % 2 + 1) * H0]

                def normalise(i, j):
                    out = not (isinstance(i, int) and i < 2)
                    order = Order(dve, steps, 3, i)
                    dve.wait_ge(hid_done, i + 1)
                    for e in range(E0):
                        ins = dve.bn_stats(st4[:, e, :], hidden_of(j, e))
                    order(ins)
                    settle(dve, k)
                    for e in range(E0):
                        ins = dve.bn_aggr(mv4[:, e, :], st4[:, e, :])
                    order(ins)
                    dve.sem_inc(var_ready, 1)
                    if out:
                        mix(i - 2, j, range(0, 2))
                    dve.wait_ge(std_ready, i + 1)
                    order(dve.reciprocal(r4[:, :], std4[:, :]))
                    order.end()
                    reused(dve, z_turned, i)
                    for e in range(E0):
                        ins = dve.tensor_scalar(z[:, e, :], hidden_of(j, e), mv4[:, e, 0:1], r4[:, e:e + 1], ALU.subtract, ALU.mult)
                    ins.then_inc(z_ready, 1)
                    if out:
                        mix(i - 2, j, range(2, E0))
                        finish(i - 2)

                def mix(i, j, experts):
                    for e in experts:
                        weight = comb[:, :, :].rearrange("p t e -> p (t e)")[:, bass.ds(E0 * i + e, 1)]
                        if e == 0:
                            dve.wait_ge(out_done, i + 1)
                            dve.tensor_scalar(acc[:, :], op[:, j, 0:P], weight, None, ALU.mult).then_inc(mixed, 1)
                        else:
                            dve.wait_ge(mixed, E0 * i + e)
                            into = acc[:, :] if e < E0 - 1 else k.rs[:, tile(i)]
                            dve.scalar_tensor_tensor(into, op[:, j, e * P:(e + 1) * P], weight, acc[:, :],
                                                     ALU.mult, ALU.add).then_inc(mixed, 1)

                def finish(i):
                    dve.wait_ge(mixed, E0 * (i + 1))
                    dve.bn_stats(k.st[:, bass.ds(6 * i, 6)], k.rs[:, tile(i)])

                def last(i, j):
                    if isinstance(i, int) and i >= NT - 2:
                        mix(i, j, range(E0))
                        finish(i)

                staggered(dve, {"z": normalise, "out": last}, AHEAD)

            @block.scalar
            def _(act):
                def take(i, j):
                    reused(act, hid_done, i - 1)
                    act.activation(hi[:, j, :], hT[:, tile(i)], ACT.Copy).then_inc(h_taken, 1)

                def std(i, j):
                    act.wait_ge(var_ready, i + 1)
                    act.activation(std4[:, :], mv4[:, :, 1], ACT.Sqrt, bias=k.eps[:, :]).then_inc(std_ready, 1)

                def gains(i, j):
                    reused(act, out_done, i - 1)
                    act.wait_ge(z_turned, i + 1)
                    for n in range(N8):
                        ins = act.activation(aT[:, j, n, :], zp[:, n // 4, n % 4 * P:(n % 4 + 1) * P], ACT.Relu,
                                             bias=k.c["lnb"][:, n:n + 1], scale=k.c["lng"][:, n:n + 1])
                    ins.then_inc(a_ready, 1)

                staggered(act, {"h": take, "z": std, "a": gains}, AHEAD)

            @block.tensor
            def _(pe):
                def hidden(i, j):
                    pe.wait_ge(h_taken, i + 1)
                    reused(pe, z_ready, i - 1)
                    for h in range(2):
                        mm = pe.matmul(hp[:, j, h, :], hi[:, j, :], k.c["w1"][:, h * 512:(h + 1) * 512], start=True, stop=True)
                    mm.then_inc(hid_done, 1)

                def turn(i, j):
                    pe.wait_ge(z_ready, i + 1)
                    reused(pe, a_ready, i)
                    zf = z[:, :, :].rearrange("p e h -> p (e h)")
                    for n in range(N8):
                        mm = pe.transpose(zp[:, n // 4, n % 4 * P:(n % 4 + 1) * P], zf[:, n * P:(n + 1) * P], k.c["ident"])
                    mm.then_inc(z_turned, 1)

                def down(i, j):
                    pe.wait_ge(a_ready, i + 1)
                    reused(pe, mixed, E0 * (i - 1))
                    for e in range(E0):
                        for h in range(2):
                            n = 2 * e + h
                            mm = pe.matmul(op[:, j, e * P:(e + 1) * P], aT[:, j, n, :], k.c["w2"][:, n * P:(n + 1) * P],
                                           start=h == 0, stop=h == 1)
                    mm.then_inc(out_done, 1)

                staggered(pe, {"hid": hidden, "out": down, "a": turn}, AHEAD)

    add_normalised(nc, k, "c_end", "on_g", "on_b", k.xs, True)


def feed_forward(nc, k):
    NB = FF // P
    sem = lambda name: k.sem(f"f_{name}")
    with ExitStack() as ctx:
        def sb(name, shape, dt=F32):
            return ctx.enter_context(nc.sbuf_tensor(f"f_{name}", shape, dt))

        def psum(name, shape):
            return ctx.enter_context(nc.psum_tensor(f"f_{name}", shape, F32))

        std, rstd = sb("std", [P, NT]), sb("rstd", [P, NT])
        xn, xq, xT, gT = sb("normal", [P, 2, P]), sb("y", [P, 2, P]), sb("yT", [P, P]), sb("innerT", [P, 2, NB, P])
        tp, ip, op = psum("turn_bank", [P, 512]), psum("inner_p", [P, 2, 512]), psum("out_p", [P, 2, 512])
        stats, std_made, made, own = sem("stats"), sem("std_made"), sem("rstd_made"), sem("tile_steps")
        x_ready, x_turned, xT_ready, in_done, g_ready, out_done, summed = (
            sem(n) for n in ("x_ready", "x_turned", "xT_ready", "in_done", "g_ready", "out_done", "summed"))
        AHEAD = {"in": 1, "out": 0, "x": 2, "n": 3}
        with nc.Block() as block:
            @block.vector
            def _(dve):
                aggregate(dve, Order(dve, stats, 1), k)
                dve.wait_ge(std_made, 1)
                dve.reciprocal(rstd[:, :], std[:, :]).then_inc(made, 1)
                dve.wait_ge(made, 1)

                def norm_in(i, j):
                    reused(dve, x_turned, i - 1)
                    order = Order(dve, own, 2, i)
                    order(dve.tensor_scalar(xn[:, j, :], k.rs[:, tile(i)], k.mv[:, bass.ds(2 * i, 1)], rstd[:, bass.ds(i, 1)],
                                            ALU.subtract, ALU.mult))
                    order(dve.tensor_tensor(xn[:, j, :], xn[:, j, :], k.row("so_g"), ALU.mult))
                    order.end()
                    dve.tensor_tensor(k.res[:, tile(i)], xn[:, j, :], k.row("so_be"), ALU.add)
                    dve.tensor_tensor(xq[:, j, :], xn[:, j, :], k.row("so_be"), ALU.add).then_inc(x_ready, 1)

                def add_out(i, j):
                    dve.wait_ge(out_done, i + 1)
                    dve.tensor_tensor(k.rs[:, tile(i)], op[:, j, 0:P], k.res[:, tile(i)], ALU.add).then_inc(summed, 1)
                    dve.wait_ge(summed, i + 1)
                    dve.bn_stats(k.st[:, bass.ds(6 * i, 6)], k.rs[:, tile(i)])

                staggered(dve, {"n": norm_in, "out": add_out}, AHEAD)

            @block.scalar
            def _(act):
                act.preload_act_table_set("sqrt_and_others")
                act.wait_ge(stats, 1)
                act.activation(std[:, :], variances(k), ACT.Sqrt, bias=k.eps[:, :]).then_inc(std_made, 1)

                def turned(i, j):
                    act.wait_ge(x_turned, i + 1)
                    reused(act, in_done, i)
                    act.activation(xT[:, :], tp[:, 0:P], ACT.Copy).then_inc(xT_ready, 1)

                def inner(i, j):
                    reused(act, out_done, i - 1)
                    act.wait_ge(in_done, i + 1)
                    for n in range(NB):
                        ins = act.activation(gT[:, j, n, :], ip[:, j, n * P:(n + 1) * P], ACT.Gelu, bias=k.c["fi_b"][:, n:n + 1])
                    ins.then_inc(g_ready, 1)

                act.preload_act_table_set("gelu_and_others")
                staggered(act, {"x": turned, "in": inner}, AHEAD)

            @block.tensor
            def _(pe):
                def turn(i, j):
                    pe.wait_ge(x_ready, i + 1)
                    reused(pe, xT_ready, i)
                    pe.transpose(tp[:, 0:P], xq[:, j, :], k.c["ident"]).then_inc(x_turned, 1)

                def project(i, j):
                    pe.wait_ge(xT_ready, i + 1)
                    reused(pe, g_ready, i - 1)
                    for n in range(NB):
                        mm = pe.matmul(ip[:, j, n * P:(n + 1) * P], k.c["fi"][:, n * P:(n + 1) * P], xT[:, :], start=True, stop=True)
                    mm.then_inc(in_done, 1)

                def down(i, j):
                    pe.wait_ge(g_ready, i + 1)
                    reused(pe, summed, i - 1)
                    pe.matmul(op[:, j, 0:P], k.ones[0:1, :], k.row("fo_b")[0:1, :], start=True, stop=False)
                    for n in range(NB):
                        mm = pe.matmul(op[:, j, 0:P], gT[:, j, n, :], k.c["fo"][:, n * P:(n + 1) * P], start=False, stop=n == NB - 1)
                    mm.then_inc(out_done, 1)

                staggered(pe, {"x": turn, "in": project, "out": down}, AHEAD)

    stored, loaded = sem("stored"), sem("loaded")

    def turn(sp, added):
        for c in range(4):
            sp.wait_ge(added, c + 1)
            sp.dma_start(k.turn_dram[8 * c:8 * c + 8].rearrange("(t b) s d -> (b s) t d", b=2),
                         k.xs[:, c * 512:(c + 1) * 512].rearrange("p (t d) -> p t d", d=P)).then_inc(stored, 16)
        sp.wait_ge(stored, 64)
        load_turned(sp, k, k.turn_dram, loaded)
        sp.wait_ge(loaded, 64)

    add_normalised(nc, k, "f_end", "fo_g", "fo_be", k.xs, False, turn)


def load_turned(sp, k, src, loaded):
    for q in range(4):
        sp.dma_start(k.xe[32 * q:32 * q + 32, :].rearrange("p (g d) -> p g d", d=P),
                     src.rearrange("t (g q) d -> q t g d", q=4)[q]).then_inc(loaded, 16)


def memory_stage(nc, k):
    NP2 = NHM // 2
    SCALE = 1.0 / np.sqrt(DM)
    sem = lambda name: k.sem(f"m_{name}")
    with ExitStack() as ctx:
        def sb(name, shape, dt=F32):
            return ctx.enter_context(nc.sbuf_tensor(f"m_{name}", shape, dt))

        std, rstd = sb("std", [P, NT]), sb("rstd", [P, NT])
        xq, hT = sb("h", [P, P]), sb("hT", [P, P])
        ex = sb("exp", [P, 2, 512])
        kq = sb("features", [P, NP2, 2, P])
        bs = sb("beta_sums", [P, 3 * NHM])
        eb, cc = sb("exp_beta", [P, NHM]), sb("sigma_sums", [P, NHM])
        c = sb("c", [P, 2, NHM])
        clow = sb("c_low", [P, 2, NHM])
        rq = sb("q_scale", [P, 2, NHM])
        R = sb("rhs", [P, 2, NHM, DM])
        gm = sb("products", [P, 2, NHM, 2, P])
        X, Ym, cX, T, Gc, cl = (sb(n, [P, NHM, 32]) for n in ("inverse", "masked", "c_inverse", "inverse_T", "compact", "c_level0"))
        Tb = sb("inverse_T_blocks", [P, 2, NHM, P])
        U0, V, U, on = (sb(n, [P, NHM, DM]) for n in ("u0", "v", "u", "out_rows"))
        oT = sb("outT", [P, NP2, P])
        F = ctx.enter_context(nc.psum_tensor("m_front", [P, 3, 512], F32))
        C = ctx.enter_context(nc.psum_tensor("m_chain", [P, 5, 512], F32))
        h32 = lambda ap: ap.rearrange("p (h n) -> p h n", n=32)
        h64 = lambda a: C[:, a:a + 2, :].rearrange("p b (h n) -> p (b h) n", n=DM)
        bc = lambda v, n: v.unsqueeze(2).to_broadcast([P, NHM, n])
        lvl = lambda j: k.c[f"lvl{j}"].unsqueeze(1).to_broadcast([P, NHM, 32])
        lvl0T = k.c["lvl0T"].unsqueeze(1).to_broadcast([P, NHM, 32])
        eye = k.c["eye32"].unsqueeze(1).to_broadcast([P, NHM, 32])
        masks = k.pack["cst"][:, 208:208 + 2 * P].rearrange("p (g t) -> p g t", g=2)
        ind2_on = k.pack["cst"][:, 464:560]
        assert [n for n, _ in PACKS["cst"]][3:6] == ["bd_strict", "bd_upper", "ind2"] and width(PACKS["cst"][:3]) == 208

        stats, std_made, made, cleared = sem("stats"), sem("std_made"), sem("rstd_made"), sem("cleared")
        x_ready, x_turned, hT_ready = sem("x_ready"), sem("x_turned"), sem("hT_ready")
        qk_done, ex_ready, clipped, kq_ready = sem("qk_done"), sem("ex_ready"), sem("clipped"), sem("kq_ready")
        v_done, sum_done, bs_ready, eb_ready, small, rhs_ready = (
            sem(n) for n in ("v_done", "sum_done", "bs_ready", "eb_ready", "small_steps", "rhs_ready"))
        ga_done, gm_ready, c_ready, gc_ready = sem("ga_done"), sem("gm_ready"), sem("c_ready"), sem("gc_ready")
        cx_ready, y_done, ysteps, ym_ready, z_done, X_ready, T_ready, Tb_ready = (
            sem(n) for n in ("cx_ready", "y_done", "y_steps", "ym_ready", "z_done", "X_ready", "T_ready", "Tb_ready"))
        u0_done, u0_ready, v1_ready, gy_done, v2_ready, xy_done, u_ready, cu_ready = (
            sem(n) for n in ("u0_done", "u0_ready", "v1_ready", "gy_done", "v2_ready", "xy_done", "u_ready", "cu_ready"))
        o_done, on_ready, oT_done, oT_ready, p_done, summed = (
            sem(n) for n in ("o_done", "on_ready", "oT_done", "oT_ready", "p_done", "summed"))

        FRONT = ["x", "qk0", "qk1", "qk2", "qk3", "v", "sum", "ga0", "ga1", "ga2", "ga3"]
        INVERT = ["g0", "y0", "y1", "z1", "y2", "z2", "y3", "z3"]
        APPLY = ["u0", "gy", "xy", "o", "oT", "proj"]
        PERIOD = ["g0", "u0", "x", "y0", "qk0", "gy", "y1", "qk1", "xy", "z1", "o", "y2", "qk2", "qk3", "z2", "v", "sum",
                  "y3", "ga0", "oT", "ga1", "z3", "ga2", "proj", "ga3"]
        assert sorted(PERIOD) == sorted(FRONT + INVERT + APPLY)

        AHEAD = behind(PERIOD, INVERT, FRONT)
        block = ctx.enter_context(nc.Block())

        def wide(h, width, most):
            return slice(h, min(h + most, (h * width // 512 + 1) * 512 // width))

        @block.tensor
        def _(pe):
            def x(i, j):
                pe.wait_ge(x_ready, i + 1)
                pe.wait_ge(bs_ready, i)
                pe.transpose(F[:, 2, 0:P], xq[:, :], k.c["ident"]).then_inc(x_turned, 1)

            def qk(g):
                def step(i, j):
                    if g == 0:
                        pe.wait_ge(hT_ready, i + 1)
                        pe.wait_ge(gm_ready, 8 * i)
                    if g >= 2:
                        pe.wait_ge(kq_ready, 4 * i + g - 1)
                    w = k.c["mk"] if g % 2 == 0 else k.c["mq"]
                    for a in range(4):
                        n = 4 * (g // 2) + a
                        mm = pe.matmul(F[:, g % 2, a * P:(a + 1) * P], w[:, n * P:(n + 1) * P], hT[:, :], start=True, stop=True)
                    mm.then_inc(qk_done, 1)
                return step

            def v(i, j):
                pe.wait_ge(kq_ready, 4 * i + 4)
                for h in range(2):
                    pe.matmul(F[:, h, :], hT[:, :], k.c["mv"][:, h * 512:(h + 1) * 512], start=True, stop=True)
                pe.matmul(F[:, 2, P:P + NHM], hT[:, :], k.c["mbeta"], start=True, stop=True).then_inc(v_done, 1)

            def sums(i, j):
                for w in range(2):
                    for a in range(NP2):
                        at = P + NHM * (w + 1) + 2 * a
                        mm = pe.matmul(F[:, 2, at:at + 96], kq[:, a, w, :], ind2_on, start=True, stop=True)
                mm.then_inc(sum_done, 1)

            def ga(r):
                def step(i, j):
                    if r == 0:
                        pe.wait_ge(rhs_ready, i + 1)
                    else:
                        pe.wait_ge(gm_ready, 8 * i + 2 * r)
                    for h in range(2):
                        for a in range(2):
                            rows = slice(DM * h, DM * (h + 1))
                            mm = pe.matmul(F[:, h, a * 2 * P:(a + 1) * 2 * P], kq[rows, 2 * r + a, 0, :],
                                           kq[rows, 2 * r + a, :, :].rearrange("p w t -> p (w t)"), start=True, stop=True)
                        mm.then_inc(ga_done, 1)
                return step

            def y(l):
                def step(i, j):
                    pe.wait_ge(cx_ready, 4 * i + l + 1)
                    if l == 1:
                        pe.wait_ge(gm_ready, 8 * i + 8)
                    for h in range(NHM):
                        w = wide(h, 32, 3)
                        mm = pe.matmul(C[:, 0, 32 * w.start:32 * w.stop], gm[:, j, h, 0, :],
                                       cX[:, w, :].rearrange("p h n -> p (h n)"), start=True, stop=True)
                    mm.then_inc(y_done, 1)
                return step

            def z(l):
                def step(i, j):
                    pe.wait_ge(ym_ready, 3 * i + l)
                    pe.wait_ge(Tb_ready, 4 * i + l)
                    for h in range(NHM):
                        w = wide(h, 32, 3)
                        mm = pe.matmul(C[:, 1, 32 * w.start:32 * w.stop], Tb[:, j, h, :],
                                       Ym[:, w, :].rearrange("p h n -> p (h n)"), start=True, stop=True)
                    mm.then_inc(z_done, 1)
                return step

            def apply(at, left, right, done):
                for h in range(NHM):
                    w = wide(h, DM, 2)
                    mm = pe.matmul(C[:, at + h // 8, h % 8 * DM:(h % 8 + w.stop - h) * DM], left(h),
                                   right[:, w, :].rearrange("p h n -> p (h n)"), start=True, stop=True)
                mm.then_inc(done, 1)

            def u0(i, j):
                pe.wait_ge(Tb_ready, 4 * i + 4)
                pe.wait_ge(oT_ready, i)
                apply(2, lambda h: Tb[:, j, h, :], R[:, j, :, :], u0_done)

            def gy(i, j):
                pe.wait_ge(v1_ready, i + 1)
                apply(2, lambda h: gm[:, j, h, 0, :], V, gy_done)

            def xy(i, j):
                pe.wait_ge(v2_ready, i + 1)
                apply(2, lambda h: Tb[:, j, h, :], V, xy_done)

            def o(i, j):
                pe.wait_ge(cu_ready, i + 1)
                apply(2, lambda h: gm[:, j, h, 1, :], V, o_done)

            def oT_(i, j):
                pe.wait_ge(on_ready, i + 1)
                of = on[:, :, :].rearrange("p h n -> p (h n)")
                for a in range(NP2):
                    mm = pe.transpose(C[:, 2 + a // 4, a % 4 * P:(a % 4 + 1) * P], of[:, a * P:(a + 1) * P], k.c["ident"])
                mm.then_inc(oT_done, 1)

            def proj(i, j):
                pe.wait_ge(oT_ready, i + 1)
                pe.wait_ge(summed, i)
                for a in range(NP2):
                    mm = pe.matmul(C[:, 4, 0:P], oT[:, a, :], k.c["mo"][:, a * P:(a + 1) * P], start=a == 0, stop=a == NP2 - 1)
                mm.then_inc(p_done, 1)

            staggered(pe, {"x": x, "v": v, "sum": sums, "u0": u0, "gy": gy, "xy": xy, "o": o, "oT": oT_, "proj": proj,
                          **{f"qk{g}": qk(g) for g in range(4)}, **{f"ga{r}": ga(r) for r in range(4)},
                          **{f"y{l}": y(l) for l in range(1, 4)}, **{f"z{l}": z(l) for l in range(1, 4)}}, AHEAD)

        @block.scalar
        def _(act):
            act.preload_act_table_set("sqrt_and_others")
            act.wait_ge(stats, 2)
            act.activation(std[:, :], variances(k), ACT.Sqrt, bias=k.eps[:, :]).then_inc(std_made, 1)
            act.wait_ge(cleared, 1)
            act.preload_act_table_set("exp_and_others")

            def x(i, j):
                act.wait_ge(x_turned, i + 1)
                act.wait_ge(v_done, i)
                act.activation(hT[:, :], F[:, 2, 0:P], ACT.Copy).then_inc(hT_ready, 1)

            def qk(g):
                def step(i, j):
                    act.wait_ge(qk_done, 4 * i + g + 1)
                    if g >= 2:
                        act.wait_ge(kq_ready, 4 * i + g - 1)
                    else:
                        act.wait_ge(kq_ready, 4 * i)
                    act.activation(ex[:, g % 2, :], F[:, g % 2, :], ACT.Exp).then_inc(ex_ready, 1)
                return step

            def sums(i, j):
                act.wait_ge(bs_ready, i + 1)
                act.wait_ge(c_ready, i)
                act.activation(eb[:, :], bs[:, 0:NHM], ACT.Exp, scale=-1.0).then_inc(eb_ready, 1)

            def gather(i, j):
                act.wait_ge(gm_ready, 8 * i + 8)
                reused(act, X_ready, 4 * i - 3)
                for q in range(4):
                    r = slice(32 * q, 32 * q + 32)
                    ins = act.activation(Gc[r, :, :], gm[r, j, :, 0, r], ACT.Copy)
                ins.then_inc(gc_ready, 1)

            def spread(n):
                def step(i, j):
                    act.wait_ge(T_ready, 4 * i + n)
                    if n == 1:
                        reused(act, xy_done, i - 1)
                    else:
                        act.wait_ge(z_done, 3 * i + n - 1)
                    for q in range(4):
                        r = slice(32 * q, 32 * q + 32)
                        ins = act.activation(Tb[r, j, :, r], T[r, :, :], ACT.Copy)
                    ins.then_inc(Tb_ready, 1)
                return step

            def gy(i, j):
                act.wait_ge(gy_done, i + 1)
                act.activation(V[:, :, :], h64(2), ACT.Copy, scale=k.c["rowhigh"]).then_inc(v2_ready, 1)

            def oT_(i, j):
                act.wait_ge(oT_done, i + 1)
                act.wait_ge(p_done, i)
                act.activation(oT[:, :, :], C[:, 2:4, :].rearrange("p b (a t) -> p (b a) t", t=P), ACT.Copy).then_inc(oT_ready, 1)

            staggered(act, {"x": x, "g0": gather, "sum": sums, "gy": gy, "oT": oT_, "y0": spread(1), "z1": spread(2), "z2": spread(3),
                           "z3": spread(4), **{f"qk{g}": qk(g) for g in range(4)}}, AHEAD)

        @block.gpsimd
        def _(pool):
            pool.memset(Tb[:, :, :, :], 0.0).then_inc(cleared, 1)

            def cx(l):
                def step(i, j):
                    if l == 0:
                        pool.wait_ge(c_ready, i + 1)
                        reused(pool, X_ready, 4 * i - 3)
                        pool.tensor_tensor(cl[:, :, :], lvl0T, bc(c[:, j, :], 32), ALU.mult).then_inc(cx_ready, 1)
                    else:
                        pool.wait_ge(X_ready, 4 * i + l)
                        reused(pool, y_done, 3 * i + l - 1)
                        pool.tensor_tensor(cX[:, :, :], X[:, :, :], bc(c[:, j, :], 32), ALU.mult).then_inc(cx_ready, 1)
                return step

            def u0(i, j):
                pool.wait_ge(u0_ready, i + 1)
                pool.wait_ge(o_done, i)
                pool.tensor_tensor(V[:, :, :], U0[:, :, :], bc(clow[:, j, :], DM), ALU.mult).then_inc(v1_ready, 1)

            def xy(i, j):
                pool.wait_ge(u_ready, i + 1)
                pool.tensor_tensor(V[:, :, :], U[:, :, :], bc(c[:, j, :], DM), ALU.mult).then_inc(cu_ready, 1)

            staggered(pool, {"u0": u0, "xy": xy, **{f"y{l}": cx(l) for l in range(4)}}, AHEAD)

        @block.vector
        def _(dve):
            row_stats(dve, Order(dve, stats, 2), k, k.xe)
            dve.wait_ge(std_made, 1)
            dve.reciprocal(rstd[:, :], std[:, :]).then_inc(made, 1)
            dve.wait_ge(made, 1)

            def x(i, j):
                dve.wait_ge(x_turned, i)
                for out in (k.rs[:, tile(i)], xq[:, :]):
                    ins = dve.tensor_scalar(out, k.xe[:, tile(i)], k.mv[:, bass.ds(2 * i, 1)], rstd[:, bass.ds(i, 1)],
                                            ALU.subtract, ALU.mult)
                ins.then_inc(x_ready, 1)

            def qk(g):
                def step(i, j):
                    dve.wait_ge(ex_ready, 4 * i + g + 1)
                    dve.tensor_scalar(ex[:, g % 2, :], ex[:, g % 2, :], 1.0, None, ALU.min).then_inc(clipped, 1)
                    dve.wait_ge(clipped, 4 * i + g + 1)
                    dve.wait_ge(ga_done, 8 * i)
                    n = 4 * (g // 2)
                    dve.scalar_tensor_tensor(kq[:, n:n + 4, g % 2, :], F[:, g % 2, :].rearrange("p (a t) -> p a t", t=P), 0.0,
                                             ex[:, g % 2, :].rearrange("p (a t) -> p a t", t=P), ALU.max, ALU.add).then_inc(kq_ready, 1)
                return step

            def sums(i, j):
                dve.wait_ge(sum_done, i + 1)
                dve.wait_ge(eb_ready, i)
                dve.tensor_copy(bs[:, :], F[:, 2, P:P + 3 * NHM]).then_inc(bs_ready, 1)
                dve.wait_ge(bs_ready, i + 1)
                sk, sq = bs[:, NHM:2 * NHM], bs[:, 2 * NHM:]
                dve.tensor_tensor(R[:, j, :, :], F[:, 0:2, :].rearrange("p b (h n) -> p (b h) n", n=DM), bc(sk, DM),
                                  ALU.mult).then_inc(rhs_ready, 1)
                order = Order(dve, small, 6, i)
                order(dve.reciprocal(rq[:, j, :], sq))
                order(dve.tensor_scalar(rq[:, j, :], rq[:, j, :], float(SCALE), None, ALU.mult))
                dve.wait_ge(eb_ready, i + 1)
                order(dve.tensor_scalar(cc[:, :], eb[:, :], 1.0, None, ALU.add))
                order(dve.tensor_tensor(cc[:, :], cc[:, :], sk, ALU.mult))
                order(dve.tensor_tensor(cc[:, :], cc[:, :], sk, ALU.mult))
                order(dve.reciprocal(c[:, j, :], cc[:, :]))
                order.end()
                dve.tensor_scalar(clow[:, j, :], c[:, j, :], k.c["rowlow"], None, ALU.mult).then_inc(c_ready, 1)

            def ga(r):
                def step(i, j):
                    for h in range(2):
                        dve.wait_ge(ga_done, 8 * i + 2 * r + h + 1)
                        out = gm[:, j, 4 * r + h:4 * r + 4:2, :, :]
                        dve.tensor_tensor(out, F[:, h, :].rearrange("p (a g t) -> p a g t", a=2, g=2),
                                          masks.unsqueeze(1).to_broadcast([P, 2, 2, P]), ALU.mult).then_inc(gm_ready, 1)
                return step

            def y(l):
                def step(i, j):
                    dve.wait_ge(y_done, 3 * i + l)
                    reused(dve, z_done, 3 * i + l - 1)
                    dve.tensor_tensor(Ym[:, :, :], h32(C[:, 0, :]), lvl(l), ALU.mult).then_inc(ym_ready, 1)
                return step

            def y0(i, j):
                dve.wait_ge(cx_ready, 4 * i + 1)
                dve.wait_ge(gc_ready, i + 1)
                reused(dve, Tb_ready, 4 * i)
                dve.tensor_tensor(T[:, :, :], Gc[:, :, :], cl[:, :, :], ALU.mult).then_inc(ysteps, 1)
                dve.wait_ge(ysteps, i + 1)
                dve.tensor_tensor(T[:, :, :], eye, T[:, :, :], ALU.subtract).then_inc(T_ready, 1)
                dve.wait_ge(T_ready, 4 * i + 1)
                dve.transpose(X[:, :, :], T[:, :, :]).then_inc(X_ready, 1)

            def turn(n, i):
                dve.wait_ge(X_ready, 4 * i + n)
                dve.wait_ge(Tb_ready, 4 * i + n - 1)
                dve.transpose(T[:, :, :], X[:, :, :]).then_inc(T_ready, 1)

            def z(l):
                def step(i, j):
                    dve.wait_ge(z_done, 3 * i + l)
                    dve.wait_ge(cx_ready, 4 * i + l + 1)
                    dve.tensor_tensor(X[:, :, :], X[:, :, :], h32(C[:, 1, :]), ALU.subtract).then_inc(X_ready, 1)
                    turn(l + 1, i)
                return step

            def u0(i, j):
                dve.wait_ge(u0_done, i + 1)
                dve.tensor_copy(U0[:, :, :], h64(2)).then_inc(u0_ready, 1)

            def xy(i, j):
                dve.wait_ge(xy_done, i + 1)
                dve.tensor_tensor(U[:, :, :], U0[:, :, :], h64(2), ALU.subtract).then_inc(u_ready, 1)

            def o(i, j):
                dve.wait_ge(o_done, i + 1)
                dve.tensor_tensor(on[:, :, :], h64(2), bc(rq[:, j, :], DM), ALU.mult).then_inc(on_ready, 1)

            def proj(i, j):
                dve.wait_ge(p_done, i + 1)
                dve.tensor_tensor(k.rs[:, tile(i)], C[:, 4, 0:P], k.rs[:, tile(i)], ALU.add).then_inc(summed, 1)
                dve.wait_ge(summed, i + 1)
                dve.bn_stats(k.st[:, bass.ds(6 * i, 6)], k.rs[:, tile(i)])

            staggered(dve, {"x": x, "y0": y0, "sum": sums, "u0": u0, "xy": xy, "o": o, "proj": proj,
                           **{f"qk{g}": qk(g) for g in range(4)}, **{f"ga{r}": ga(r) for r in range(4)},
                           **{f"y{l}": y(l) for l in range(1, 4)}, **{f"z{l}": z(l) for l in range(1, 4)}}, AHEAD)

    add_normalised(nc, k, "m_end", "m_g", "m_b", k.xe, True)


def shared_experts_stage(nc, k):
    NA = E1 + 1
    sem = lambda name: k.sem(f"s_{name}")
    with ExitStack() as ctx:
        def sb(name, shape, dt=F32):
            return ctx.enter_context(nc.sbuf_tensor(f"s_{name}", shape, dt))

        xT = sb("xT", [P, B * S])
        comb = sb("weights", [P, NT, NE])
        acc = k.xs
        with ExitStack() as inner:
            def isb(name, shape):
                return inner.enter_context(nc.sbuf_tensor(f"s_{name}", shape, F32))

            lg, score, picked = isb("logits", [P, NT, E1]), isb("scores", [P, NT, E1 + 5]), isb("picked", [P, NT, E1 + 5])
            values, red, b2, combT = isb("values", [P, NT, 8]), isb("reduced", [P, 3, NT]), isb("b2", [NA, P]), isb("weightsT", [NA, NT, P])
            std, rstd = isb("std", [P, NT]), isb("rstd", [P, NT])
            varied, std_made, norm_steps, xn_ready = (sem(n) for n in ("varied", "std_made", "norm_steps", "xn_ready"))
            turned = inner.enter_context(nc.psum_tensor("s_turned_p", [P, 4, 512], F32))
            lp = inner.enter_context(nc.psum_tensor("s_logit_p", [P, 512], F32))
            filled, steps, turned_s, xT_ready, logit_done, shifted, exp_ready, b2_loaded = (
                sem(n) for n in ("filled", "router_steps", "rows_turned", "xT_ready", "logit_done", "shifted", "exp_ready", "b2_loaded"))
            comb_ready, combT_done, combT_ready, bias_done, acc_ready = (
                sem(n) for n in ("comb_ready", "combT_done", "combT_ready", "bias_done", "acc_ready"))
            with nc.Block() as block:
                @block.sync
                def _(sp):
                    sp.dma_start(b2[:, :], k.dram["b2"]).then_inc(b2_loaded, 16)

                @block.gpsimd
                def _(pool):
                    pool.memset(score[:, :, :], -1.0).then_inc(filled, 1)
                    pool.memset(comb[:, :, :], 1.0).then_inc(filled, 1)

                @block.scalar
                def _(act):
                    act.preload_act_table_set("sqrt_and_others")
                    act.wait_ge(varied, 1)
                    act.activation(std[:, :], variances(k), ACT.Sqrt, bias=k.eps[:, :]).then_inc(std_made, 1)
                    for c in range(4):
                        act.wait_ge(turned_s, c + 1)
                        act.activation(xT[:, c * 512:(c + 1) * 512], turned[:, c, :], ACT.Copy).then_inc(xT_ready, 1)
                    act.wait_ge(shifted, 1)
                    act.activation(lg[:, :, :], lg[:, :, :], ACT.Exp).then_inc(exp_ready, 1)
                    for c in range(4):
                        act.wait_ge(combT_done, c + 1)
                        act.activation(combT[:, 4 * c:4 * c + 4, :], turned[0:NA, c, :].rearrange("p (t n) -> p t n", n=P),
                                       ACT.Copy).then_inc(combT_ready, 1)

                @block.tensor
                def _(pe):
                    for t in range(NT):
                        if t % 4 == 0:
                            pe.wait_ge(xn_ready, t // 4 + 1)
                        mm = pe.transpose(turned[:, t // 4, t % 4 * P:(t % 4 + 1) * P], k.rs[:, t * P:(t + 1) * P], k.c["ident"])
                        if t % 4 == 3:
                            mm.then_inc(turned_s, 1)
                    for t in range(NT):
                        if t % 4 == 0:
                            pe.wait_ge(xT_ready, t // 4 + 1)
                        mm = pe.matmul(lp[:, t * E1:(t + 1) * E1], xT[:, t * P:(t + 1) * P], k.c["gate"], start=True, stop=True)
                    mm.then_inc(logit_done, 1)
                    pe.wait_ge(comb_ready, 1)
                    for t in range(NT):
                        mm = pe.matmul(turned[0:NA, t // 4, t % 4 * P:(t % 4 + 1) * P], comb[:, t, 0:NA], k.c["ident"], start=True, stop=True)
                        if t % 4 == 3:
                            mm.then_inc(combT_done, 1)
                    pe.wait_ge(b2_loaded, 16)
                    for t in range(NT):
                        if t % 4 == 0:
                            pe.wait_ge(combT_ready, t // 4 + 1)
                        mm = pe.matmul(turned[:, t // 4, t % 4 * P:(t % 4 + 1) * P], combT[:, t, :], b2[:, :], start=True, stop=True)
                        if t % 4 == 3:
                            mm.then_inc(bias_done, 1)

                @block.vector
                def _(dve):
                    aggregate(dve, Order(dve, varied, 1), k)
                    norm = Order(dve, norm_steps, 1)
                    dve.wait_ge(std_made, 1)
                    norm(dve.reciprocal(rstd[:, :], std[:, :]))
                    for t in range(NT):
                        ins = dve.tensor_scalar(k.rs[:, t * P:(t + 1) * P], k.xe[:, t * P:(t + 1) * P], k.mv[:, 2 * t:2 * t + 1],
                                                rstd[:, t:t + 1], ALU.subtract, ALU.mult)
                        if t % 4 == 3:
                            ins.then_inc(xn_ready, 1)
                    order = Order(dve, steps, 13)
                    dve.wait_ge(logit_done, 1)
                    l3 = lp[:, 0:NT * E1].rearrange("p (t e) -> p t e", e=E1)
                    over = lambda n: red[:, n, :].unsqueeze(2).to_broadcast([P, NT, E1])
                    order(dve.tensor_reduce(red[:, 0, :], l3, AX.X, ALU.max))
                    dve.tensor_tensor(lg[:, :, :], l3, over(0), ALU.subtract).then_inc(shifted, 1)
                    dve.wait_ge(exp_ready, 1)
                    order(dve.tensor_reduce(red[:, 1, :], lg[:, :, :], AX.X, ALU.add))
                    order(dve.reciprocal(red[:, 1, :], red[:, 1, :]))
                    dve.wait_ge(filled, 2)
                    order(dve.tensor_tensor(score[:, :, 0:E1], lg[:, :, :], over(1), ALU.mult))
                    top_experts(dve, order, filled, score, picked, values, lg[:, :, :], E1, 3, 5)
                    order(dve.tensor_reduce(red[:, 2, :], lg[:, :, :], AX.X, ALU.add))
                    order(dve.tensor_scalar(red[:, 2, :], red[:, 2, :], 1e-20, None, ALU.add))
                    order(dve.reciprocal(red[:, 2, :], red[:, 2, :]))
                    dve.tensor_tensor(comb[:, :, 0:E1], lg[:, :, :], over(2), ALU.mult).then_inc(comb_ready, 1)
                    order(dve.memset(k.unused[:, :], 0.0))
                    order.end()
                    for c in range(4):
                        dve.wait_ge(bias_done, c + 1)
                        r = slice(c * 512, (c + 1) * 512)
                        dve.tensor_tensor(acc[:, r], turned[:, c, :], k.xe[:, r], ALU.add).then_inc(acc_ready, 1)

        WX = width(EXW)
        ew, w2 = sb("expert_weights", [P, 2, WX]), sb("down_weights", [P, 2, P])
        gl, a = sb("gates", [P, 2, 512]), sb("gated", [P, 2, 512])
        up = ctx.enter_context(nc.psum_tensor("s_up", [P, 2, 2, 512], F32))
        dn = ctx.enter_context(nc.psum_tensor("s_down", [P, 2, 512], F32))
        e_loaded = [sem(f"expert_loaded{j}") for j in range(2)]
        w2_ready, up_done, g_ready, a_ready, dn_done, mixed, out_stored = (
            sem(n) for n in ("w2_ready", "up_done", "g_ready", "a_ready", "dn_done", "mixed", "out_stored"))
        w = [fields_of(ew[:, j, :], EXW) for j in range(2)]
        flat = comb[:, :, :].rearrange("p t e -> p (t e)")

        def experts(eng, step):
            step(0, 0, False)
            with eng.Fori(1, NE // 2) as m:
                step(2 * m - 1, 1, False)
                step(2 * m, 0, False)
            step(NE - 2, 1, False)
            step(NE - 1, 0, True)

        with nc.Block() as block:
            @block.sync
            def _(sp):
                for e in range(2):
                    sp.dma_start(ew[:, e, :], k.dram["experts"][e]).then_inc(e_loaded[e], 16)

                def load(e, j):
                    sp.wait_ge(dn_done, 4 * e + 4)
                    sp.wait_ge(a_ready, 4 * e + 4)
                    sp.dma_start(ew[:, j, :], k.dram["experts"][bass.ds(e + 2, 1), :, :].rearrange("e p w -> p (e w)")).then_inc(e_loaded[j], 16)

                with sp.Fori(0, NE // 2 - 1) as m:
                    for j in range(2):
                        load(2 * m + j, j)
                load(NE - 3, 0)
                sp.wait_ge(mixed, 4 * NE)
                for q in range(4):
                    sp.dma_start(k.out.rearrange("t (g q) d -> q t g d", q=4)[q],
                                 acc[32 * q:32 * q + 32, :].rearrange("p (g d) -> p g d", d=P)).then_inc(out_stored, 16)
                sp.wait_ge(out_stored, 64)

            @block.gpsimd
            def _(pool):
                def step(m, j, used):
                    e = 2 * m + j
                    if used:
                        pool.wait_ge(dn_done, 4 * e - 4)
                    pool.wait_ge(e_loaded[j], 16 * (m + 1))
                    pool.tensor_tensor(w2[:, j, :], w[j]["fc2"], w[j]["mult"].to_broadcast([P, P]), ALU.mult).then_inc(w2_ready, 1)

                for j in range(2):
                    step(0, j, False)
                with pool.Fori(1, NE // 2) as m:
                    for j in range(2):
                        step(m, j, True)
                step(NE // 2, 0, True)

            @block.scalar
            def _(act):
                def step(e, j, last):
                    for c in range(4):
                        act.wait_ge(up_done, 4 * e + c + 1)
                        reused(act, a_ready, 4 * e + c - 1)
                        act.activation(gl[:, c % 2, :], up[:, c % 2, 1, :], ACT.Gelu, bias=w[j]["b1"][:, 1:2]).then_inc(g_ready, 1)

                act.preload_act_table_set("gelu_and_others")
                experts(act, step)

            @block.tensor
            def _(pe):
                def project_up(e, j, c):
                    if c == 0:
                        pe.wait_ge(e_loaded[j], 8 * (e - j) + 16)
                    for h in range(2):
                        mm = pe.matmul(up[:, c % 2, h, :], w[j]["fc1"][:, h * F1:(h + 1) * F1], xT[:, c * 512:(c + 1) * 512],
                                       start=True, stop=True)
                    mm.then_inc(up_done, 1)

                def step(e, j, last):
                    for c in range(4):
                        if not (last and c == 3):
                            reused(pe, a_ready, 4 * e + c)
                            project_up(e + (c == 3), (j + (c == 3)) % 2, (c + 1) % 4)
                        pe.wait_ge(a_ready, 4 * e + c + 1)
                        pe.wait_ge(w2_ready, e + 1)
                        reused(pe, mixed, 4 * e + c - 1)
                        for q in range(4):
                            mm = pe.matmul(dn[:, c % 2, q * P:(q + 1) * P], a[:, c % 2, q * P:(q + 1) * P], w2[:, j, :],
                                           start=True, stop=True)
                        mm.then_inc(dn_done, 1)

                project_up(0, 0, 0)
                experts(pe, step)

            @block.vector
            def _(dve):
                def gate(e, j, c):
                    dve.wait_ge(g_ready, 4 * e + c + 1)
                    reused(dve, dn_done, 4 * e + c - 1)
                    dve.scalar_tensor_tensor(a[:, c % 2, :], up[:, c % 2, 0, :], w[j]["b1"][:, 0:1], gl[:, c % 2, :],
                                             ALU.add, ALU.mult).then_inc(a_ready, 1)

                def step(e, j, last):
                    for c in range(4):
                        if not (last and c == 3):
                            gate(e + (c == 3), (j + (c == 3)) % 2, (c + 1) % 4)
                        dve.wait_ge(dn_done, 4 * e + c + 1)
                        for q in range(4):
                            t = 4 * c + q
                            r = slice(t * P, (t + 1) * P)
                            ins = dve.scalar_tensor_tensor(acc[:, r], dn[:, c % 2, q * P:(q + 1) * P], flat[:, bass.ds(t * NE + e, 1)],
                                                           acc[:, r], ALU.mult, ALU.add)
                        ins.then_inc(mixed, 1)

                gate(0, 0, 0)
                experts(dve, step)


def build(nc, dram, out):
    with ExitStack() as ctx:
        def sb(name, shape, dt=F32):
            return ctx.enter_context(nc.sbuf_tensor(f"all_{name}", shape, dt))

        k = Shared()
        k.dram, k.out = dram, out
        taken = []

        def sem(name):
            taken.append(nc.alloc_semaphore(name=name))
            return taken[-1]

        def stage(part, *args):
            part(nc, k, *args)
            nc.clear_and_free_semaphores(taken)
            nc.all_engine_barrier()
            taken.clear()

        k.sem = sem
        k.pack = {name: sb(f"pack_{name}", [P, width(f)]) for name, f in PACKS.items()}
        k.c = {}
        for name, f in PACKS.items():
            k.c.update(fields_of(k.pack[name], f))
        k.rows = sb("rows", [P, len(ROWS) * P])
        k.row = lambda name: k.rows[:, ROWS.index(name) * P:(ROWS.index(name) + 1) * P]
        k.xs = sb("x_tiles", [P, NT * P])
        k.res = sb("residual_tiles", [P, NT * P])
        k.rs = sb("sum_tiles", [P, NT * P])
        k.st = sb("six_tuples", [P, 6 * NT])
        k.mv = sb("mean_var", [P, 2 * NT])
        k.ones = sb("ones", [P, P])
        k.eps = sb("eps", [P, 1])
        k.unused = sb("unused", [P, 1])
        k.ones3 = sb("ones3", [P, P], BF16)
        k.pick3 = sb("pick3", [P, 32], BF16)
        k.hm = sb("head_scale", [P, NH])
        k.xe = k.res
        k.turn_dram = nc.dram_tensor("turned_rows", (B, S, P), F32).ap()
        k.early_loaded, k.weights_loaded, k.late_loaded, k.const_made, k.const_ordered = (
            ctx.enter_context(nc.semaphore(n)) for n in ("early_loaded", "weights_loaded", "late_loaded", "const_made", "const_ordered"))
        c = k.c
        taps = lambda w: [w[:, t * P:(t + 1) * P] for t in range(KS)]
        load_constants(nc, k)
        stage(attention, "a", taps(c["wq"]), taps(c["wk"]), taps(c["wv"]), c["wo"], c["a_bq"], c["a_bk"], "a_bv", "a_bo",
                  k.xs, None, -1e9, False)
        stage(scan_stage)
        experts_stage(nc, k)
        stage(attention, "dc", [c["cq"]], [c["ck"]], [c["cv"]], c["co"], c["cq_b"], c["ck_b"], "cv_b", "co_b",
                  k.xs, None, 1.0, False)
        stage(attention, "ds", [c["sq"]], [c["sk"]], [c["sv"]], c["so"], c["sq_b"], c["sk_b"], "sv_b", "so_b",
                  k.rs, ("co_g", "co_be"), None, True)
        stage(feed_forward)
        stage(memory_stage)
        stage(shared_experts_stage)


def constants():
    r, c = np.arange(P)[:, None], np.arange(P)[None, :]
    c32 = np.arange(32)[None, :]
    same = r // 32 == c // 32
    cst = {
        "ident": r == c,
        "sel64": r % S == np.arange(S)[None, :],
        "headmask": r // DH == np.arange(NH)[None, :],
        "bd_strict": same & (r < c),
        "bd_upper": same & (r <= c),
        "eye32": r % 32 == c32,
        "rowlow": r % 32 < 16,
        "rowhigh": r % 32 >= 16,
        "ind2": r // 64 == np.arange(2)[None, :],
        "pick3": (r % 32 == c32) & (r < 96),
    }
    for j in range(4):
        w = 2 ** j
        cst[f"lvl{j}"] = ((r % 32) // (2 * w) == c32 // (2 * w)) & ((r % 32) // w % 2 == 1) & (c32 // w % 2 == 0)
    cst["lvl0T"] = cst["lvl0"].reshape(4, 32, 32).transpose(0, 2, 1).reshape(P, 32)
    return {n: v.astype(np.float32) for n, v in cst.items()}


def lay_out(a):
    cat = lambda *xs: np.concatenate(xs, axis=1)
    taps = lambda w: cat(*w)
    col = lambda v: v.reshape(-1, P).T
    down = lambda w: cat(*w.reshape(-1, P, w.shape[-1]))
    parts = constants()
    parts.update(
        a_bq=col(a["L0_xattn_bq"]), a_bk=col(a["L0_xattn_bk"]), b_delta=col(a["L0_attn_b_delta"]), d_skip=col(a["L0_attn_D_skip"]),
        norm_w=col(a["L0_attn_norm_weight"]), rn_g=col(a["L0_ffn_rn_g"]), rn_b=col(a["L0_ffn_rn_b"]), lng=col(a["L0_ffn_ln_g"]),
        lnb=col(a["L0_ffn_ln_b"]), cq_b=col(a["L1_xattn_cq_b"]), ck_b=col(a["L1_xattn_ck_b"]), sq_b=col(a["L1_xattn_sq_b"]),
        sk_b=col(a["L1_xattn_sk_b"]), fi_b=col(a["L1_xattn_fi_b"]),
        wq=taps(a["L0_xattn_Wq"]), wk=taps(a["L0_xattn_Wk"]), wv=taps(a["L0_xattn_Wv"]), wo=a["L0_xattn_Wo"],
        wdelta=a["L0_attn_W_delta"], wbc=cat(a["L0_attn_W_B"], a["L0_attn_W_C"]), alog=a["L0_attn_A_log"],
        router=a["L0_ffn_router_w"].T, w1=cat(*a["L0_ffn_w1"]), w2=down(a["L0_ffn_w2"].reshape(-1, P)),
        fi=a["L1_xattn_fi_w"], fo=down(a["L1_xattn_fo_w"]), gate=a["L1_ffn_gate_w"].T)
    for n in ("cq", "ck", "cv", "co", "sq", "sk", "sv", "so"):
        parts[n] = a[f"L1_xattn_{n}_w"]
    w = a["L1_attn_W_qkvb"].reshape(P, NHM, 3 * DM + 1)
    parts.update(mq=w[:, :, 0:DM].reshape(P, -1), mk=w[:, :, DM:2 * DM].reshape(P, -1), mv=w[:, :, 2 * DM:3 * DM].reshape(P, -1),
                 mbeta=w[:, :, 3 * DM], mo=down(a["L1_attn_W_o"]))
    arrays = {name: cat(*(parts[n] for n, _ in f)) for name, f in PACKS.items()}
    rows = dict(a_bv="L0_xattn_bv", a_bo="L0_xattn_bo", on_g="L0_ffn_on_g", on_b="L0_ffn_on_b", m_g="L1_attn_ln_g", m_b="L1_attn_ln_b")
    arrays["rows"] = np.concatenate([a[rows.get(n, f"L1_xattn_{n}")] for n in ROWS])
    f1, f2, sf1, sf2 = a["L1_ffn_fc1_w"], a["L1_ffn_fc2_w"], a["L1_ffn_s_fc1_w"], a["L1_ffn_s_fc2_w"]
    up, down2, bias, mult = list(f1), list(f2), list(a["L1_ffn_fc1_b"]), list(a["L1_ffn_geglu_mult"])
    for h in range(FS // F1):
        r = slice(h * F1, (h + 1) * F1)
        g = slice(FS + h * F1, FS + (h + 1) * F1)
        up.append(np.concatenate([sf1[r], sf1[g]]))
        down2.append(sf2[:, r])
        bias.append(np.concatenate([a["L1_ffn_s_fc1_b"][r], a["L1_ffn_s_fc1_b"][g]]))
        mult.append(a["L1_ffn_s_geglu_mult"][r])
    arrays["experts"] = np.stack([cat(u.T, d.T, col(v), col(m)) for u, d, v, m in zip(up, down2, bias, mult)])
    arrays["b2"] = cat(*[v[None] for v in (np.concatenate([a["L1_ffn_fc2_b"], a["L1_ffn_s_fc2_b"][None]]))]).reshape(E1 + 1, P)
    arrays["x"] = a["x"]
    arrays["ctxT"] = a["ctx_1024"].transpose(2, 0, 1).reshape(P, B * SC)
    arrays["mask"] = a["mask_Bx1x1xS2_ff0"].reshape(B, SC)
    return {n: np.ascontiguousarray(v) for n, v in arrays.items()}


def kernel(**inputs):
    import concourse.bacc as _bacc
    from concourse import mybir as _mybir
    from concourse.bass_utils import run_bass_kernel_spmd as _run

    nc = _bacc.Bacc("TRN2", target_bir_lowering=False, num_devices=1)
    laid = lay_out({n: np.asarray(v) for n, v in inputs.items()})
    arrays, dram = {}, {}
    for name, a in laid.items():
        arrays[f"in_{name}_dram"] = a
        dram[name] = nc.dram_tensor(f"in_{name}_dram", a.shape, _mybir.dt.from_np(a.dtype), kind="ExternalInput").ap()
    out = nc.dram_tensor("out_0_dram", (B, S, P), F32, kind="ExternalOutput").ap()
    build(nc, dram, out)
    r = _run(nc, [arrays], core_ids=[0])
    return r.results[0]["out_0_dram"]
```
